# Optimizing a Trainium2 kernel written in Bass

```python
import numpy as np
import jax
import jax.numpy as jnp

def _softmax(x, axis=-1):
    return jax.nn.softmax(x, axis=axis)

def _gelu(x):
    return jax.nn.gelu(x, approximate=True)

def _silu(x):
    return jax.nn.silu(x)

def _sigmoid(x):
    return jax.nn.sigmoid(x)

def _layernorm(x, axis=-1, eps=1e-05):
    m = jnp.mean(x, axis=axis, keepdims=True)
    v = jnp.var(x, axis=axis, keepdims=True)
    return (x - m) / jnp.sqrt(v + eps)

def _scatter_add(tgt, idx, src, axis=0):
    return tgt.at[idx].add(src)

def _segment_sum(src, seg, n):
    return jax.ops.segment_sum(src, seg, n)
kernel_name = 'mk_adaln_d2_jaxref_r8_079e14'

def setup_inputs(seed: int=0):
    np.random.seed(seed)
    _w = jnp.asarray

    def _L0_attn_setup():
        import jax, jax.numpy as jnp
        import numpy as np
        LN_EPS = 1e-05
        key = jax.random.key(seed)
        ks = jax.random.split(key, 7)
        B, L, D, N = (8, 256, 128, 16)
        x = jax.random.normal(ks[0], (B, L, D), jnp.float32)
        A = jax.random.normal(ks[1], (D, N, N), jnp.float32) * (0.2 / np.sqrt(N))
        Bp = jax.random.normal(ks[2], (D, N), jnp.float32)
        Cp = jax.random.normal(ks[3], (D, N), jnp.float32)
        Dp = jax.random.normal(ks[4], (D,), jnp.float32)
        Wg = jax.random.normal(ks[5], (D, D), jnp.float32) / np.sqrt(D)
        bg = jnp.zeros((D,), jnp.float32)
        gamma = jnp.ones((D,), jnp.float32)
        beta = jnp.zeros((D,), jnp.float32)
        return dict(x=x, A=A, Bp=Bp, Cp=Cp, Dp=Dp, Wg=Wg, bg=bg, gamma=gamma, beta=beta)
    _L0_attn_in = _L0_attn_setup()

    def _L0_ffn_setup():
        import jax, jax.numpy as jnp
        import numpy as np
        NUM_EXPERTS = 8
        D_MODEL = 128
        D_OUT = 128
        key = jax.random.key(seed)
        ks = jax.random.split(key, 5)
        B, S = (2, 256)
        x = jax.random.normal(ks[0], (B, S, D_MODEL), dtype=jnp.float32)
        gate_w = jax.random.normal(ks[1], (D_MODEL, NUM_EXPERTS), dtype=jnp.float32) * 0.02
        gate_b = jnp.zeros((NUM_EXPERTS,), dtype=jnp.float32)
        expert_w = jax.random.normal(ks[2], (NUM_EXPERTS, D_MODEL, D_OUT), dtype=jnp.float32) * 0.02
        expert_b = jnp.zeros((NUM_EXPERTS, D_OUT), dtype=jnp.float32)
        return {'x': x, 'gate_w': gate_w, 'gate_b': gate_b, 'expert_w': expert_w, 'expert_b': expert_b}
    _L0_ffn_in = _L0_ffn_setup()
    _L0_c = _w((lambda *s: np.random.randn(*s).astype(np.float32) * 0.05)(16, 128))
    _L0_wmod = _w((lambda *s: np.random.randn(*s).astype(np.float32) * 0.05)(128, 6 * 128) * 128 ** (-0.5))

    def _L1_attn_setup():
        import jax, jax.numpy as jnp
        import numpy as np
        D_MODEL = 128
        N_HEADS = 16
        D_HEAD = D_MODEL // N_HEADS
        key = jax.random.key(seed)
        ks = jax.random.split(key, 5)
        B, S = (1, 256)
        x = jax.random.normal(ks[0], (B, S, D_MODEL), dtype=jnp.float32)
        lim = float(np.sqrt(6.0 / (2 * D_MODEL)))

        def w(k):
            return jax.random.uniform(k, (D_MODEL, D_MODEL), jnp.float32, -lim, lim)
        return {'x': x, 'Wq': w(ks[1]), 'bq': jnp.zeros((D_MODEL,), jnp.float32), 'Wk': w(ks[2]), 'bk': jnp.zeros((D_MODEL,), jnp.float32), 'Wv': w(ks[3]), 'bv': jnp.zeros((D_MODEL,), jnp.float32), 'Wo': w(ks[4]), 'bo': jnp.zeros((D_MODEL,), jnp.float32)}
    _L1_attn_in = _L1_attn_setup()

    def _L1_ffn_setup():
        import jax, jax.numpy as jnp
        import numpy as np
        B, S, D = (1, 256, 128)
        I = 256
        E = 8
        K = 2
        LIMIT = 7.0
        ALPHA = 1.702
        EPS = 1e-05

        def _swiglu(h):
            x_glu = jnp.minimum(h[..., ::2], LIMIT)
            x_lin = jnp.clip(h[..., 1::2], -LIMIT, LIMIT)
            return x_glu * jax.nn.sigmoid(ALPHA * x_glu) * (x_lin + 1.0)

        def _moe(t, gate_w, gate_b, mlp1_w, mlp1_b, mlp2_w, mlp2_b):
            T = t.shape[0]
            logits = t @ gate_w + gate_b
            top_v, top_i = jax.lax.top_k(logits, K)
            probs = jax.nn.softmax(top_v, axis=-1)
            w = jnp.zeros((T, E), t.dtype).at[jnp.arange(T)[:, None], top_i].set(probs)

            def body(acc, ew):
                w1, b1, w2, b2, we = ew
                h = _swiglu(t @ w1 + b1)
                y = h @ w2 + b2
                return (acc + we[:, None] * y, None)
            acc0 = jnp.zeros((T, t.shape[1]), t.dtype)
            acc, _ = jax.lax.scan(body, acc0, (mlp1_w, mlp1_b, mlp2_w, mlp2_b, w.T))
            return acc
        key = jax.random.key(seed)
        ks = jax.random.split(key, 4)
        s = 0.02
        return {'x': jax.random.normal(ks[0], (B, S, D), jnp.float32), 'norm_scale': jnp.ones((D,), jnp.float32), 'gate_w': jax.random.normal(ks[1], (D, E), jnp.float32) * s, 'gate_b': jnp.zeros((E,), jnp.float32), 'mlp1_w': jax.random.normal(ks[2], (E, D, 2 * I), jnp.float32) * s, 'mlp1_b': jnp.zeros((E, 2 * I), jnp.float32), 'mlp2_w': jax.random.normal(ks[3], (E, I, D), jnp.float32) * s, 'mlp2_b': jnp.zeros((E, D), jnp.float32)}
    _L1_ffn_in = _L1_ffn_setup()
    _L1_c = _w((lambda *s: np.random.randn(*s).astype(np.float32) * 0.05)(16, 128))
    _L1_wmod = _w((lambda *s: np.random.randn(*s).astype(np.float32) * 0.05)(128, 6 * 128) * 128 ** (-0.5))
    _d = {'L0_attn_x': _L0_attn_in['x'], 'L0_attn_A': _L0_attn_in['A'], 'L0_attn_Bp': _L0_attn_in['Bp'], 'L0_attn_Cp': _L0_attn_in['Cp'], 'L0_attn_Dp': _L0_attn_in['Dp'], 'L0_attn_Wg': _L0_attn_in['Wg'], 'L0_attn_bg': _L0_attn_in['bg'], 'L0_attn_gamma': _L0_attn_in['gamma'], 'L0_attn_beta': _L0_attn_in['beta'], 'L0_ffn_gate_w': _L0_ffn_in['gate_w'], 'L0_ffn_gate_b': _L0_ffn_in['gate_b'], 'L0_ffn_expert_w': _L0_ffn_in['expert_w'], 'L0_ffn_expert_b': _L0_ffn_in['expert_b'], 'L0_c': _L0_c, 'L0_wmod': _L0_wmod, 'L1_attn_Wq': _L1_attn_in['Wq'], 'L1_attn_bq': _L1_attn_in['bq'], 'L1_attn_Wk': _L1_attn_in['Wk'], 'L1_attn_bk': _L1_attn_in['bk'], 'L1_attn_Wv': _L1_attn_in['Wv'], 'L1_attn_bv': _L1_attn_in['bv'], 'L1_attn_Wo': _L1_attn_in['Wo'], 'L1_attn_bo': _L1_attn_in['bo'], 'L1_ffn_norm_scale': _L1_ffn_in['norm_scale'], 'L1_ffn_gate_w': _L1_ffn_in['gate_w'], 'L1_ffn_gate_b': _L1_ffn_in['gate_b'], 'L1_ffn_mlp1_w': _L1_ffn_in['mlp1_w'], 'L1_ffn_mlp1_b': _L1_ffn_in['mlp1_b'], 'L1_ffn_mlp2_w': _L1_ffn_in['mlp2_w'], 'L1_ffn_mlp2_b': _L1_ffn_in['mlp2_b'], 'L1_c': _L1_c, 'L1_wmod': _L1_wmod}
    _x0 = _d['L0_attn_x']
    _d['L0_attn_x'] = jax.random.normal(jax.random.fold_in(jax.random.key(seed), 1), (16, 512, 128), dtype=_x0.dtype)
    del _x0
    return _d

def reference(L0_attn_x, L0_attn_A, L0_attn_Bp, L0_attn_Cp, L0_attn_Dp, L0_attn_Wg, L0_attn_bg, L0_attn_gamma, L0_attn_beta, L0_ffn_gate_w, L0_ffn_gate_b, L0_ffn_expert_w, L0_ffn_expert_b, L0_c, L0_wmod, L1_attn_Wq, L1_attn_bq, L1_attn_Wk, L1_attn_bk, L1_attn_Wv, L1_attn_bv, L1_attn_Wo, L1_attn_bo, L1_ffn_norm_scale, L1_ffn_gate_w, L1_ffn_gate_b, L1_ffn_mlp1_w, L1_ffn_mlp1_b, L1_ffn_mlp2_w, L1_ffn_mlp2_b, L1_c, L1_wmod):

    def _L0_attn_ref(x, A, Bp, Cp, Dp, Wg, bg, gamma, beta):
        import jax, jax.numpy as jnp
        import numpy as np
        LN_EPS = 1e-05
        gate = jax.nn.sigmoid(jnp.einsum('bld,ed->ble', x, Wg) + bg)
        xg = x * gate
        Bsz, L, D = xg.shape
        N = A.shape[-1]

        def step(s, xt):
            s = jnp.einsum('bdn,dnm->bdm', s, A) + xt[..., None] * Bp
            y = jnp.einsum('bdn,dn->bd', s, Cp) + Dp * xt
            return (s, y)
        s0 = jnp.zeros((Bsz, D, N), xg.dtype)
        _, ys = jax.lax.scan(step, s0, jnp.moveaxis(xg, 1, 0))
        y = jnp.moveaxis(ys, 0, 1) + xg
        mu = jnp.mean(y, axis=-1, keepdims=True)
        var = jnp.var(y, axis=-1, keepdims=True)
        return (y - mu) * jax.lax.rsqrt(var + LN_EPS) * gamma + beta

    def _L0_ffn_ref(x, gate_w, gate_b, expert_w, expert_b):
        import jax, jax.numpy as jnp
        import numpy as np
        NUM_EXPERTS = 8
        D_MODEL = 128
        D_OUT = 128
        orig_shape = x.shape
        xt = x.reshape(-1, D_MODEL)
        logits = xt @ gate_w + gate_b
        gates = jax.nn.softmax(logits, axis=-1)
        sel = jnp.argmax(gates, axis=-1)
        onehot = jax.nn.one_hot(sel, NUM_EXPERTS, dtype=xt.dtype)
        y_all = jnp.einsum('td,edh->eth', xt, expert_w) + expert_b[:, None, :]
        out = jnp.einsum('te,eth->th', onehot, y_all)
        return out.reshape(*orig_shape[:-1], D_OUT)

    def _L1_attn_ref(x, Wq, bq, Wk, bk, Wv, bv, Wo, bo):
        import jax, jax.numpy as jnp
        import numpy as np
        D_MODEL = 128
        N_HEADS = 16
        D_HEAD = D_MODEL // N_HEADS
        B, S, _ = x.shape
        H, d = (N_HEADS, D_HEAD)
        q = x @ Wq.T + bq
        k = x @ Wk.T + bk
        v = x @ Wv.T + bv

        def to_z(t):
            return t.reshape(B, S, H, d).transpose(0, 2, 1, 3).reshape(B * H, S, d)
        q = jax.nn.softplus(to_z(q))
        k = jax.nn.softplus(to_z(k))
        v = to_z(v)
        kv = jnp.cumsum(k[:, :, :, None] * v[:, :, None, :], axis=1)
        k1 = jnp.cumsum(k, axis=1)
        num = jnp.einsum('zsD,zsDe->zse', q, kv)
        den = jnp.sum(q * k1, axis=-1, keepdims=True)
        out = num / den
        out = out.reshape(B, H, S, d).transpose(0, 2, 1, 3).reshape(B, S, H * d)
        return out @ Wo.T + bo

    def _L1_ffn_ref(x, norm_scale, gate_w, gate_b, mlp1_w, mlp1_b, mlp2_w, mlp2_b):
        import jax, jax.numpy as jnp
        import numpy as np
        B, S, D = (1, 256, 128)
        I = 256
        E = 8
        K = 2
        LIMIT = 7.0
        ALPHA = 1.702
        EPS = 1e-05

        def _swiglu(h):
            x_glu = jnp.minimum(h[..., ::2], LIMIT)
            x_lin = jnp.clip(h[..., 1::2], -LIMIT, LIMIT)
            return x_glu * jax.nn.sigmoid(ALPHA * x_glu) * (x_lin + 1.0)

        def _moe(t, gate_w, gate_b, mlp1_w, mlp1_b, mlp2_w, mlp2_b):
            T = t.shape[0]
            logits = t @ gate_w + gate_b
            top_v, top_i = jax.lax.top_k(logits, K)
            probs = jax.nn.softmax(top_v, axis=-1)
            w = jnp.zeros((T, E), t.dtype).at[jnp.arange(T)[:, None], top_i].set(probs)

            def body(acc, ew):
                w1, b1, w2, b2, we = ew
                h = _swiglu(t @ w1 + b1)
                y = h @ w2 + b2
                return (acc + we[:, None] * y, None)
            acc0 = jnp.zeros((T, t.shape[1]), t.dtype)
            acc, _ = jax.lax.scan(body, acc0, (mlp1_w, mlp1_b, mlp2_w, mlp2_b, w.T))
            return acc
        Bx, Sx, Dx = x.shape
        ms = jnp.mean(x * x, axis=-1, keepdims=True)
        t = (x * jax.lax.rsqrt(ms + EPS) * norm_scale).reshape(Bx * Sx, Dx)
        y = _moe(t, gate_w, gate_b, mlp1_w, mlp1_b, mlp2_w, mlp2_b)
        return x + y.reshape(Bx, Sx, Dx)
    x = L0_attn_x
    mod = (_silu(L0_c) @ L0_wmod).reshape(L0_c.shape[0], 6, 1, -1)
    sa, ca, ga, sb, cb, gb = (mod[:, 0], mod[:, 1], mod[:, 2], mod[:, 3], mod[:, 4], mod[:, 5])
    ga = (2 * (ga >= 0) - 1) * jnp.maximum(jnp.abs(ga), 0.25)
    gb = (2 * (gb >= 0) - 1) * jnp.maximum(jnp.abs(gb), 0.25)
    h = _layernorm(x, axis=-1) * (1 + ca) + sa
    x = x + ga * _L0_attn_ref(h, L0_attn_A, L0_attn_Bp, L0_attn_Cp, L0_attn_Dp, L0_attn_Wg, L0_attn_bg, L0_attn_gamma, L0_attn_beta)
    h = _layernorm(x, axis=-1) * (1 + cb) + sb
    x = x + gb * _L0_ffn_ref(h, L0_ffn_gate_w, L0_ffn_gate_b, L0_ffn_expert_w, L0_ffn_expert_b)
    mod = (_silu(L1_c) @ L1_wmod).reshape(L1_c.shape[0], 6, 1, -1)
    sa, ca, ga, sb, cb, gb = (mod[:, 0], mod[:, 1], mod[:, 2], mod[:, 3], mod[:, 4], mod[:, 5])
    ga = (2 * (ga >= 0) - 1) * jnp.maximum(jnp.abs(ga), 0.25)
    gb = (2 * (gb >= 0) - 1) * jnp.maximum(jnp.abs(gb), 0.25)
    h = _layernorm(x, axis=-1) * (1 + ca) + sa
    x = x + ga * _L1_attn_ref(h, L1_attn_Wq, L1_attn_bq, L1_attn_Wk, L1_attn_bk, L1_attn_Wv, L1_attn_bv, L1_attn_Wo, L1_attn_bo)
    h = _layernorm(x, axis=-1) * (1 + cb) + sb
    x = x + gb * _L1_ffn_ref(h, L1_ffn_norm_scale, L1_ffn_gate_w, L1_ffn_gate_b, L1_ffn_mlp1_w, L1_ffn_mlp1_b, L1_ffn_mlp2_w, L1_ffn_mlp2_b)
    return x

_drawn_inputs = setup_inputs


def setup_inputs(seed=0):
    import zlib

    import numpy as np

    out = dict(_drawn_inputs(seed))
    spreads = {'L0_attn_bg': (0.0, 0.762),
     'L0_attn_gamma': (1.0, 0.2),
     'L0_attn_beta': (0.0, 0.334),
     'L0_ffn_gate_b': (0.0, 0.1),
     'L0_ffn_expert_b': (0.0, 0.34),
     'L1_attn_bq': (0.0, 2.0),
     'L1_attn_bk': (0.0, 2.0),
     'L1_attn_bv': (0.0, 0.317),
     'L1_attn_bo': (0.0, 0.356),
     'L1_ffn_norm_scale': (1.0, 0.6),
     'L1_ffn_gate_b': (0.0, 0.8),
     'L1_ffn_mlp1_b': (0.0, 0.8),
     'L1_ffn_mlp2_b': (0.0, 0.515)}
    factors = {'L1_attn_Wq': 8.0,
     'L1_attn_Wk': 6.232,
     'L1_ffn_gate_w': 3.849,
     'L1_ffn_mlp1_w': 8.0,
     'L1_ffn_mlp2_w': 7.757}
    for name, (base, spread) in spreads.items():
        noise = np.random.default_rng([zlib.crc32(name.encode()), seed]).standard_normal(out[name].shape)
        drawn = base * np.exp(spread * noise) if base else spread * noise
        out[name] = jnp.asarray(drawn.astype(out[name].dtype))
    for name, factor in factors.items():
        out[name] = (out[name] * factor).astype(out[name].dtype)
    return out
```

```python
from contextlib import ExitStack

import concourse.bass as bass
from concourse import mybir
from concourse.alu_op_type import AluOpType as ALU

F32 = mybir.dt.float32
BF16 = mybir.dt.bfloat16
I32 = mybir.dt.int32
U32 = mybir.dt.uint32
ACT = mybir.ActivationFunctionType
AX = mybir.AxisListType

P = 128
D = 128
C = 4
N = 16
R = 8
G = D // R
H = 16
HD = D // H
E = 8
I2 = 512
U = 4
EPS = 1e-5
LEVELS = 7
NOWHERE = 1e6
CON = {}
for _name, _width in (("ident", P), ("upto", P), ("before", P), ("ones", P), ("group_of", R), ("head_of", H), ("iota", E), ("token", 16), ("restart", 128), ("minus_half", 16)):
    CON[_name] = (sum(w for _, w in CON.values()), _width)
CON_W = sum(w for _, w in CON.values())
ROWS = ("ga_gamma", "ga_beta", "cb1", "sb1", "gb1")


def build(nc, a, out):
    B = a["x"].shape[0]
    NI = B // U
    TILES = B * C
    rows_dram = nc.dram_tensor("rows_dram", [B, len(ROWS) * D], F32).ap()
    taps_dram = nc.dram_tensor("taps_dram", [D, 2 * P], F32)

    ctx = ExitStack()
    names_used = []
    with ctx:
        def sb(name, shape, dt=F32, scope=ctx):
            names_used.append(name)
            return scope.enter_context(nc.sbuf_tensor(f"{name}_{len(names_used)}", shape, dt))

        phase_sems = []
        passed = nc.alloc_semaphore(name="passed")

        def sem(name):
            phase_sems.append(nc.alloc_semaphore(name=name))
            return phase_sems[-1]

        def hold(eng, semaphore, value, i=None):
            eng.wait_ge(semaphore, value)
            eng.sem_inc(passed, 1)

        def end_phase():
            nc.all_engine_barrier()
            nc.clear_and_free_semaphores(phase_sems)
            nc.all_engine_barrier()
            phase_sems.clear()

        ps = ctx.enter_context(nc.psum_tensor("ps", [P, 8, 512], F32))
        con = sb("con", [P, CON_W])

        def k(name, parts=P):
            at, width = CON[name]
            return con[0:parts, at:at + width]

        ident = k("ident")

        def ps3(j):
            return ps[:, 3 * j:3 * j + 3, :].rearrange("p k n -> p (k n)")
        x_tok = sb("x_tok", [P, TILES, D])
        xg = sb("xg", [P, D, TILES])
        mod_t = sb("mod_t", [P, 9, B])
        SA0, CA0, SB0, CB0, GB0, SA1, CA1, GA1, GA_BO = range(9)

        ssm = ExitStack()
        states_of = sb("states_of", [P, G, 3, P], scope=ssm)
        TO_STATE, TO_OUT, CARRY = range(3)
        wg = sb("wg", [P, D], scope=ssm)
        bg = sb("bg", [P, 1], scope=ssm)
        with ExitStack() as sc:
            pw = [sb(f"pw{j}", [P, G, P], scope=sc) for j in range(2)]
            pwt = [sb(f"pwt{j}", [P, G, P], scope=sc) for j in range(2)]
            a1t = sb("a1t", [P, G, P], scope=sc)
            vin = sb("vin", [P, G, P], scope=sc)
            wout = sb("wout", [P, G, P], scope=sc)
            bcol = sb("bcol", [P, G], scope=sc)
            ccol = sb("ccol", [P, G], scope=sc)
            dcol = sb("dcol", [R, G], scope=sc)
            cbd = sb("cbd", [P, G, R], scope=sc)
            taps = sb("taps", [R, G, 2 * P], scope=sc)
            c_t = sb("c_t", [P, 2, B], scope=sc)
            sg_t = sb("sg_t", [P, 2, B], scope=sc)
            wmod = sb("wmod", [P, 2, 6 * D], scope=sc)
            vecs = sb("vecs", [B, 2, D], scope=sc)
            bo = sb("bo", [P, 1], scope=sc)
            ga0 = sb("ga0", [B, D], scope=sc)
            rowv = sb("rowv", [B, len(ROWS), D], scope=sc)
            sign = sb("sign", [P, 2 * D + 2 * B], scope=sc)
            s_x = [sem(f"s_x{j}") for j in range(2)]
            s_con = sem("s_con")
            s_zero = sem("s_zero")
            s_a = sem("s_a")
            s_c = sem("s_c")
            s_par = sem("s_par")
            s_sig = sem("s_sig")
            s_silu = sem("s_silu")
            s_mod = sem("s_mod")
            s_modT = sem("s_modT")
            s_modv = sem("s_modv")
            s_rows = sem("s_rows")
            s_rout = sem("s_rout")
            s_seed = sem("s_seed")
            s_vw = sem("s_vw")
            s_vwc = sem("s_vwc")
            s_sq = sem("s_sq")
            s_sqc = sem("s_sqc")
            s_tr = sem("s_tr")
            s_trc = sem("s_trc")
            s_fin = sem("s_fin")
            s_fint = sem("s_fint")
            s_tap = sem("s_tap")
            s_dv = sem("s_dv")
            s_tout = sem("s_tout")
            with nc.Block() as block:
                @block.sync
                def _(sp):
                    sp.dma_start(con[:, :], a["con"]).then_inc(s_con, 16)
                    sp.dma_start(c_t[:, :, :], a["c_t"]).then_inc(s_c, 16)
                    sp.dma_start(wmod[:, :, :], a["wmod"]).then_inc(s_c, 16)
                    sp.wait_ge(s_zero, 4)
                    with nc.allow_non_contiguous_dma(reason="small state matrices"):
                        for r in range(R):
                            d0 = slice(16 * r, 16 * r + 16)
                            for dst, src in ((pw[0], a["A"]), (pwt[0], a["A_t"]), (a1t, a["A_t"])):
                                sp.dma_start(dst[d0, :, d0], src[r]).then_inc(s_a, 16)
                    sp.dma_start(bcol[:, :], a["B_col"]).then_inc(s_par, 16)
                    sp.dma_start(ccol[:, :], a["C_col"]).then_inc(s_par, 16)
                    sp.dma_start(dcol[:, :], a["D_col"]).then_inc(s_par, 16)
                    sp.dma_start(wg[:, :], a["Wg_t"]).then_inc(s_par, 16)
                    sp.dma_start(bg[:, :], a["bg"]).then_inc(s_par, 16)
                    sp.dma_start(bo[:, :], a["bo"]).then_inc(s_par, 16)
                    for j, name in enumerate(("gamma", "beta")):
                        sp.dma_start(vecs[:, j, :], a[name].partition_broadcast(B)).then_inc(s_par, 16)
                    for j in range(2):
                        h0 = slice(j * B // 2, (j + 1) * B // 2)
                        sp.dma_start(x_tok[:, j * TILES // 2:(j + 1) * TILES // 2, :],
                                     a["x"][h0].rearrange("b (c p) d -> p (b c) d", p=P)).then_inc(s_x[j], 16)
                    sp.wait_ge(s_rows, 1)
                    sp.dma_start(rows_dram, rowv[:, :, :].rearrange("b j d -> b (j d)")).then_inc(s_rout, 16)
                    sp.wait_ge(s_tap, 2)
                    sp.dma_start(taps_dram.ap().rearrange("(g r) t -> r g t", r=R), taps[:, :, :]).then_inc(s_tout, 16)
                    sp.wait_ge(s_par, 8 * 16)
                    sp.wait_ge(s_x[0], 16)
                    sp.wait_ge(s_x[1], 16)
                    sp.wait_ge(s_rout, 16)
                    sp.wait_ge(s_tout, 16)

                @block.gpsimd
                def _(pool):
                    nc.gpsimd.memset(pwt[0][:, :, :], 0.0).then_inc(s_zero, 1)
                    nc.gpsimd.memset(a1t[:, :, :], 0.0).then_inc(s_zero, 1)
                    nc.gpsimd.memset(taps[:, :, :], 0.0).then_inc(s_zero, 1)

                @block.vector
                def _(dve):
                    nc.vector.memset(pw[0][:, :, :], 0.0).then_inc(s_zero, 1)
                    dve.wait_ge(s_sig, 1)
                    nc.vector.tensor_tensor(sg_t[:, :, :], c_t[:, :, :], sg_t[:, :, :], ALU.mult).then_inc(s_silu, 1)
                    n = [0]

                    def link(ins):
                        n[0] += 1
                        ins.then_inc(s_dv, 1)
                        dve.wait_ge(s_dv, n[0])
                    dve.wait_ge(s_modv, 2)
                    dve.wait_ge(s_par, 8 * 16)
                    gates = [(ga0[:, :], sign[0:B, 0:D]), (rowv[:, 4, :], sign[0:B, D:2 * D]),
                             (mod_t[:, GB0, :], sign[:, 2 * D:2 * D + B]), (mod_t[:, GA1, :], sign[:, 2 * D + B:2 * D + 2 * B])]
                    for g, sg in gates:
                        last = nc.vector.tensor_scalar(sg, g, 0.0, 2.0, ALU.is_ge, ALU.mult)
                    link(last)
                    for g, sg in gates:
                        nc.vector.tensor_scalar(sg, sg, -1.0, None, ALU.add)
                        last = nc.vector.scalar_tensor_tensor(g, g, -1.0, g, ALU.mult, ALU.max)
                    link(last)
                    for g, sg in gates:
                        last = nc.vector.tensor_scalar(g, g, 0.25, None, ALU.max)
                    link(last)
                    for g, sg in gates:
                        last = nc.vector.tensor_tensor(g, g, sg, ALU.mult)
                    link(last)
                    nc.vector.tensor_scalar(mod_t[:, GA_BO, :], mod_t[:, GA1, :], bo[:, :], None, ALU.mult)
                    nc.vector.tensor_tensor(rowv[:, 0, :], ga0[:, :], vecs[:, 0, :], ALU.mult)
                    nc.vector.tensor_tensor(rowv[:, 1, :], ga0[:, :], vecs[:, 1, :], ALU.mult).then_inc(s_rows, 1)
                    nc.vector.tensor_tensor(cbd[:, :, :], ccol[:, :].unsqueeze(2).to_broadcast([P, G, R]),
                                            k("group_of").unsqueeze(1).to_broadcast([P, G, R]), ALU.mult)
                    nc.vector.tensor_copy(vin[:, :, 0:1], bcol[:, :].unsqueeze(2))
                    nc.vector.tensor_copy(wout[:, :, 0:1], ccol[:, :].unsqueeze(2)).then_inc(s_seed, 1)
                    for lv in range(LEVELS):
                        m = 1 << lv
                        dve.wait_ge(s_vw, 2 * lv + 1)
                        nc.vector.tensor_copy(vin[:, :, m:2 * m].rearrange("p (k g) m -> p k g m", k=2),
                                              ps[:, 4:6, 0:8 * m].rearrange("p k (g m) -> p k g m", m=m)).then_inc(s_vwc, 1)
                        dve.wait_ge(s_vw, 2 * lv + 2)
                        nc.vector.tensor_copy(wout[:, :, m:2 * m].rearrange("p (k g) m -> p k g m", k=2),
                                              ps[:, 6:8, 0:8 * m].rearrange("p k (g m) -> p k g m", m=m)).then_inc(s_vwc, 1)
                        if lv < LEVELS - 1:
                            for q in range(4):
                                dve.wait_ge(s_tr, 4 * lv + q + 1)
                                nc.vector.tensor_copy(pwt[(lv + 1) % 2][:, 4 * q:4 * q + 4, :],
                                                      ps[:, 4 + q, :].rearrange("p (g m) -> p g m", m=P)).then_inc(s_trc, 1)
                    for q in range(4):
                        dve.wait_ge(s_fin, q + 1)
                        nc.vector.tensor_copy(states_of[:, 4 * q:4 * q + 4, TO_OUT, :],
                                              ps[:, q, :].rearrange("p (g m) -> p g m", m=P)).then_inc(s_fint, 1)
                    dve.wait_ge(s_fin, 12)
                    link(nc.vector.tensor_copy(taps[:, :, P:2 * P].rearrange("r (k g) m -> r k g m", k=4),
                                               ps[0:R, 4:8, :].rearrange("r k (g m) -> r k g m", m=P)))
                    nc.vector.tensor_tensor(taps[:, :, P:P + 1], taps[:, :, P:P + 1], dcol[:, :].unsqueeze(2), ALU.add).then_inc(s_tap, 1)
                    dve.wait_ge(s_tap, 1)
                    nc.vector.tensor_scalar(taps[:, :, P:P + 1], taps[:, :, P:P + 1], 1.0, None, ALU.add).then_inc(s_tap, 1)

                @block.scalar
                def _(act):
                    act.wait_ge(s_c, 32)
                    nc.scalar.activation(sg_t[:, :, :], c_t[:, :, :], ACT.Sigmoid).then_inc(s_sig, 1)
                    act.wait_ge(s_modT, 1)
                    for j in range(8):
                        last = nc.scalar.activation(mod_t[:, j, :], ps[:, 4, 16 * j:16 * j + B], ACT.Copy,
                                                    bias=float(j in (CA0, CB0, CA1)))
                    last.then_inc(s_modv, 1)
                    act.wait_ge(s_mod, 2)
                    nc.scalar.activation(ga0[:, :], ps[0:B, 0, 0:D], ACT.Copy)
                    nc.scalar.activation(rowv[:, 3, :], ps[0:B, 1, 0:D], ACT.Copy)
                    nc.scalar.activation(rowv[:, 2, :], ps[0:B, 1, D:2 * D], ACT.Copy, bias=1.0)
                    nc.scalar.activation(rowv[:, 4, :], ps[0:B, 1, 2 * D:3 * D], ACT.Copy).then_inc(s_modv, 1)
                    for lv in range(LEVELS):
                        for q in range(4):
                            act.wait_ge(s_sq, 4 * lv + q + 1)
                            dst = pw[(lv + 1) % 2][:, 4 * q:4 * q + 4, :]
                            if lv == LEVELS - 1:
                                dst = states_of[:, 4 * q:4 * q + 4, CARRY, :]
                            nc.scalar.activation(dst, ps[:, q, :].rearrange("p (g m) -> p g m", m=P), ACT.Copy).then_inc(s_sqc, 1)
                    for q in range(4):
                        act.wait_ge(s_fin, 5 + q)
                        nc.scalar.activation(states_of[:, 4 * q:4 * q + 4, TO_STATE, :],
                                             ps[:, 4 + q, :].rearrange("p (g m) -> p g m", m=P), ACT.Copy).then_inc(s_sqc, 1)

                @block.tensor
                def _(pe):
                    pe.wait_ge(s_silu, 1)
                    for j, (l, part) in enumerate(((0, 0), (0, 1), (0, 3), (0, 4), (0, 5), (1, 0), (1, 1), (1, 2))):
                        last = nc.tensor.matmul(ps[:, 4, 16 * j:16 * j + B], wmod[:, l, part * D:(part + 1) * D],
                                                sg_t[:, l, :], start=True, stop=True)
                    last.then_inc(s_modT, 1)
                    nc.tensor.matmul(ps[0:B, 0, 0:D], sg_t[:, 0, :], wmod[:, 0, 2 * D:3 * D], start=True, stop=True).then_inc(s_mod, 1)
                    nc.tensor.matmul(ps[0:B, 1, 0:3 * D], sg_t[:, 1, :], wmod[:, 1, 3 * D:6 * D], start=True, stop=True).then_inc(s_mod, 1)
                    pe.wait_ge(s_con, 16)
                    pe.wait_ge(s_seed, 1)
                    pe.wait_ge(s_a, 3 * R * 16)
                    pe.wait_ge(s_modv, 2)
                    for lv in range(LEVELS):
                        m = 1 << lv
                        cur = lv % 2
                        if lv:
                            pe.wait_ge(s_sqc, 4 * lv)
                            pe.wait_ge(s_trc, 4 * lv)
                        for g in range(G):
                            last = nc.tensor.matmul(ps[:, 4 + g // 8, (g % 8) * m:(g % 8 + 1) * m], pw[cur][:, g, :],
                                                    vin[:, g, 0:m], start=True, stop=True)
                        last.then_inc(s_vw, 1)
                        for g in range(G):
                            last = nc.tensor.matmul(ps[:, 6 + g // 8, (g % 8) * m:(g % 8 + 1) * m], pwt[cur][:, g, :],
                                                    wout[:, g, 0:m], start=True, stop=True)
                        last.then_inc(s_vw, 1)
                        for g in range(G):
                            last = nc.tensor.matmul(ps[:, g // 4, (g % 4) * P:(g % 4 + 1) * P], pwt[cur][:, g, :],
                                                    pw[cur][:, g, :], start=True, stop=True)
                            if g % 4 == 3:
                                last.then_inc(s_sq, 1)
                        pe.wait_ge(s_vwc, 2 * lv + 2)
                        if lv < LEVELS - 1:
                            for q in range(4):
                                pe.wait_ge(s_sqc, 4 * lv + q + 1)
                                for g in range(4 * q, 4 * q + 4):
                                    last = nc.tensor.transpose(ps[:, 4 + q, (g % 4) * P:(g % 4 + 1) * P],
                                                               pw[1 - cur][:, g, :], ident)
                                last.then_inc(s_tr, 1)
                    pe.wait_ge(s_sqc, 4 * LEVELS)
                    for g in range(G):
                        last = nc.tensor.matmul(ps[:, g // 4, (g % 4) * P:(g % 4 + 1) * P], a1t[:, g, :], wout[:, g, :],
                                                start=True, stop=True)
                        if g % 4 == 3:
                            last.then_inc(s_fin, 1)
                    for g in range(G):
                        last = nc.tensor.transpose(ps[:, 4 + g // 4, (g % 4) * P:(g % 4 + 1) * P], vin[:, g, :], ident)
                        if g % 4 == 3:
                            last.then_inc(s_fin, 1)
                    for q in range(4):
                        pe.wait_ge(s_sqc, 4 * LEVELS + q + 1)
                        for g in range(4 * q, 4 * q + 4):
                            last = nc.tensor.matmul(ps[0:R, 4 + q, (g % 4) * P:(g % 4 + 1) * P], cbd[:, g, :], vin[:, g, :],
                                                    start=True, stop=True)
                        last.then_inc(s_fin, 1)

        with ExitStack() as sc:
            st = sb("st", [P, U, C, 6], scope=sc)
            mv = sb("mv", [P, U, C, 2], scope=sc)
            rstd = sb("rstd", [P, U * C], scope=sc)
            nrm = [sb(f"nrm{u}", [P, C, D], scope=sc) for u in range(U)]
            h_t = [sb(f"h_t{u}", [P, C * P], scope=sc) for u in range(U)]
            sig = [sb(f"sig{u}", [P, C * P], scope=sc) for u in range(U)]
            xr_t = [sb(f"xr_t{u}", [P, C * P], scope=sc) for u in range(U)]
            s_st = sem("p1_stats")
            s_mv = sem("p1_mean_var")
            s_ve = sem("p1_var_eps")
            s_rs = sem("p1_rstd")
            s_n = sem("p1_normed")
            s_nt = sem("p1_transposed")
            s_h = sem("p1_modulated")
            s_gm = sem("p1_gate_product")
            s_gs = sem("p1_gate")
            s_xr = sem("p1_gated")
            s_xt = sem("p1_back")
            s_w = sem("p1_written")
            with nc.Block() as block:
                @block.vector
                def _(dve):
                    with dve.Fori(0, NI) as i:
                        n = [dve.snap(i * U + u + 1) for u in range(U)]
                        it = dve.snap(i + 1)
                        for u in range(U):
                            for c in range(C):
                                last = nc.vector.bn_stats(st[:, u, c, :], x_tok[:, bass.ds((i * U + u) * C + c, 1), :].squeeze(1))
                        last.then_inc(s_st, 1)
                        hold(dve, s_st, it)
                        for u in range(U):
                            for c in range(C):
                                last = nc.vector.bn_aggr(mv[:, u, c, :], st[:, u, c, :])
                        last.then_inc(s_mv, 1)
                        dve.wait_ge(s_rs, it)
                        for u in range(U):
                            for c in range(C):
                                last = nc.vector.tensor_scalar(nrm[u][:, c, :], x_tok[:, bass.ds((i * U + u) * C + c, 1), :].squeeze(1),
                                                               mv[:, u, c, 0:1], rstd[:, u * C + c:u * C + c + 1],
                                                               ALU.subtract, ALU.mult)
                            last.then_inc(s_n, 1)
                        for u in range(U):
                            dve.wait_ge(s_gs, n[u])
                            nc.vector.tensor_tensor(xr_t[u][:, :].rearrange("p (c t) -> p c t", c=C)[:, :, ::-1],
                                                    h_t[u][:, :].rearrange("p (c t) -> p c t", c=C),
                                                    sig[u][:, :].rearrange("p (c t) -> p c t", c=C), ALU.mult).then_inc(s_xr, 1)
                        for u in range(U):
                            dve.wait_ge(s_xt, n[u])
                            nc.vector.tensor_copy(xg[:, :, bass.ds((i * U + u) * C, C)].rearrange("p d c -> p c d"),
                                                  ps[:, u, :].rearrange("p (c d) -> p c d", c=C)).then_inc(s_w, 1)

                @block.gpsimd
                def _(pool):
                    with pool.Fori(0, NI) as i:
                        it = pool.snap(i + 1)
                        hold(pool, s_mv, it)
                        nc.gpsimd.tensor_scalar(rstd[:, :], mv[:, :, :, 1].rearrange("p u c -> p (u c)"), EPS, None, ALU.add).then_inc(s_ve, 1)
                        pool.wait_ge(s_ve, it)
                        nc.gpsimd.tensor_tensor(rstd[:, :], rstd[:, :], k("minus_half"), ALU.pow).then_inc(s_rs, 1)

                @block.scalar
                def _(act):
                    with act.Fori(0, NI) as i:
                        n = [act.snap(i * U + u + 1) for u in range(U)]
                        for u in range(U):
                            act.wait_ge(s_nt, n[u])
                            b = i * U + u
                            nc.scalar.activation(h_t[u][:, :], ps[:, u, :], ACT.Identity,
                                                 bias=mod_t[:, SA0, bass.ds(b, 1)], scale=mod_t[:, CA0, bass.ds(b, 1)]).then_inc(s_h, 1)
                        for u in range(U):
                            act.wait_ge(s_gm, n[u])
                            nc.scalar.activation(sig[u][:, :], ps[:, 4 + u, :], ACT.Sigmoid, bias=bg[:, :]).then_inc(s_gs, 1)

                @block.tensor
                def _(pe):
                    with pe.Fori(0, NI) as i:
                        n = [pe.snap(i * U + u + 1) for u in range(U)]
                        for u in range(U):
                            pe.wait_ge(s_n, n[u])
                            for c in range(C):
                                last = nc.tensor.transpose(ps[:, u, c * P:(c + 1) * P], nrm[u][:, c, :], ident)
                            last.then_inc(s_nt, 1)
                        for u in range(U):
                            pe.wait_ge(s_h, n[u])
                            nc.tensor.matmul(ps[:, 4 + u, :], wg[:, :], h_t[u][:, :], start=True, stop=True).then_inc(s_gm, 1)
                        for u in range(U):
                            pe.wait_ge(s_xr, n[u])
                            for c in range(C):
                                last = nc.tensor.transpose(ps[:, u, c * P:(c + 1) * P], xr_t[u][:, c * P:(c + 1) * P], ident)
                            last.then_inc(s_xt, 1)

        with ExitStack() as sc:
            TS = B * C
            toep = [sb(f"toep{u}", [P, R, P], scope=sc) for u in range(U)]
            mats = [sb(f"mats{u}", [P, 3, P], scope=sc) for u in range(U)]
            ends = [sb(f"ends{u}", [P, TS], scope=sc) for u in range(U)]
            endm = [sb(f"endm{u}", [P, R, TS], scope=sc) for u in range(U)]
            carry = [sb(f"carry{u}", [P, R, TS], scope=sc) for u in range(U)]
            s_toep = [sem(f"p2_toep{u}") for u in range(U)]
            s_m = sem("p2_matrices")
            s_e = sem("p2_end_products")
            s_em = sem("p2_ends_masked")
            s_er = sem("p2_ends")
            s_c1 = sem("p2_carry_product")
            s_c2 = sem("p2_carried")
            s_cb = sem("p2_carry_spread")
            s_y = sem("p2_outputs")
            s_yc = sem("p2_outputs_kept")
            s_z = sem("p2_cleared")

            def by_chunk(ap, c):
                return ap.rearrange("p (b c) -> p b c", c=C)[:, :, c]

            with nc.Block() as block:
                @block.sync
                def _(sp):
                    with sp.Fori(0, G // U) as i:
                        for u in range(U):
                            sp.wait_ge(s_yc, sp.snap(i * U + u + 1))
                            src = bass.AP(taps_dram, (i * U + u) * (R * 2 * P) + 1, [[1, P], [2 * P, R], [1, P]])
                            sp.dma_start(toep[u][:, :, :], src).then_inc(s_toep[u], 16)
                    for u in range(U):
                        sp.wait_ge(s_toep[u], 16 * (G // U))

                @block.scalar
                def _(act):
                    with act.Fori(0, G // U) as i:
                        n = [act.snap(i * U + u + 1) for u in range(U)]
                        for u in range(U):
                            act.wait_ge(s_yc, n[u])
                            nc.scalar.activation(mats[u][:, :, :].unsqueeze(1), states_of[:, bass.ds(i * U + u, 1), :, :], ACT.Copy).then_inc(s_m, 1)

                @block.vector
                def _(dve):
                    for u in range(U):
                        last = nc.vector.memset(carry[u][:, :, :], 0.0)
                    last.then_inc(s_z, 1)
                    last = nc.vector.memset(ends[0][:, :], 0.0)
                    last.then_inc(s_yc, U)
                    dve.wait_ge(s_yc, U)
                    nc.vector.memset(ends[0][:, :], 0.0).then_inc(s_cb, U)
                    with dve.Fori(0, G // U) as i:
                        n = [dve.snap(i * U + u + 1) for u in range(U)]
                        n5 = [dve.snap(i * U + u + 1 + U) for u in range(U)]
                        c1 = [[dve.snap(i * (2 * U) + j * U + u + 1) for u in range(U)] for j in range(2)]
                        for u in range(U):
                            dve.wait_ge(s_e, n[u])
                            nc.vector.tensor_tensor(endm[u][:, :, :], ps[:, u, 0:R * TS].rearrange("p (r t) -> p r t", r=R),
                                                    k("group_of").unsqueeze(2).to_broadcast([P, R, TS]), ALU.mult).then_inc(s_em, 1)
                        for u in range(U):
                            dve.wait_ge(s_em, n[u])
                            nc.vector.tensor_reduce(ends[u][:, :], endm[u][:, :, :].rearrange("p r t -> p t r"), AX.X, ALU.add).then_inc(s_er, 1)
                        for j in range(2):
                            for u in range(U):
                                dve.wait_ge(s_c1, c1[j][u])
                                nc.vector.tensor_tensor(by_chunk(ends[u][:, :], j + 1), by_chunk(ends[u][:, :], j + 1), ps[:, u, j * B:(j + 1) * B],
                                                        ALU.add).then_inc(s_c2, 1)
                        for u in range(U):
                            dve.wait_ge(s_c2, c1[1][u])
                            for c in range(1, C):
                                src = by_chunk(ends[u][:, :], c - 1)
                                last = nc.vector.tensor_tensor(
                                    carry[u][:, :, :].rearrange("p r (b c) -> p r b c", c=C)[:, :, :, c],
                                    src.unsqueeze(1).to_broadcast([P, R, B]),
                                    k("group_of").unsqueeze(2).to_broadcast([P, R, B]), ALU.mult)
                            last.then_inc(s_cb, 1)
                        for u in range(U):
                            dve.wait_ge(s_y, n[u])
                            nc.vector.tensor_copy(xg[:, bass.ds((i * U + u) * R, R), :], ps[:, 4 + u, 0:R * TS].rearrange("p (r t) -> p r t", r=R)).then_inc(s_yc, 1)

                @block.tensor
                def _(pe):
                    pe.wait_ge(s_z, 1)
                    with pe.Fori(0, G // U) as i:
                        n = [pe.snap(i * U + u + 1) for u in range(U)]
                        n5 = [pe.snap(i * U + u + 1 + U) for u in range(U)]
                        c2 = [[pe.snap(i * (2 * U) + j * U + u + 1) for u in range(U)] for j in range(2)]
                        tp = pe.snap((i + 1) * 16)
                        for u in range(U):
                            pe.wait_ge(s_m, n[u])
                            pe.wait_ge(s_yc, n[u])
                            nc.tensor.matmul(ps[:, u, 0:R * TS], mats[u][:, TO_STATE, :],
                                             xg[:, bass.ds((i * U + u) * R, R), :], start=True, stop=True).then_inc(s_e, 1)
                        for j in range(2):
                            for u in range(U):
                                if j == 0:
                                    pe.wait_ge(s_er, n[u])
                                else:
                                    pe.wait_ge(s_c2, c2[0][u])
                                nc.tensor.matmul(ps[:, u, j * B:(j + 1) * B], mats[u][:, CARRY, :], by_chunk(ends[u][:, :], j),
                                                 start=True, stop=True).then_inc(s_c1, 1)
                        for u in range(U):
                            pe.wait_ge(s_cb, n5[u])
                            pe.wait_ge(s_toep[u], tp)
                            nc.tensor.matmul(ps[:, 4 + u, 0:R * TS], mats[u][:, TO_OUT, :], carry[u][:, :, :], start=True, stop=False)
                            for r in range(R):
                                last = nc.tensor.matmul(ps[:, 4 + u, r * TS:(r + 1) * TS], toep[u][:, r, :],
                                                        xg[:, bass.ds((i * U + u) * R + r, 1), :], start=False, stop=(r == R - 1))
                            last.then_inc(s_y, 1)
        ssm.close()
        end_phase()

        QK = 2 * D
        VE = HD + 1
        PAY = D + 4
        NT = U * C
        CAP = B * C * P + P
        rows_of = nc.dram_tensor("rows_of", [E * CAP, PAY], F32).ap()
        base = sb("base", [P, E])
        far = sb("far", [P, PAY])
        with ExitStack() as sc:
            wqkv = sb("wqkv", [P, 3 * D], scope=sc)
            wo = sb("wo", [P, D], scope=sc)
            ew0 = sb("ew0", [P, E, D], scope=sc)
            eb0 = sb("eb0", [E, D], scope=sc)
            gw = sb("gw", [P, 2, E], scope=sc)
            gb = sb("gb", [P, 2, E], scope=sc)
            bqkv = sb("bqkv", [P, 3 * D], scope=sc)
            scale_ms = sb("scale_ms", [P, D], scope=sc)
            pick = sb("pick", [E, E, P], BF16, scope=sc)
            rows = [sb(f"rows{u}", [P, len(ROWS), D], scope=sc) for u in range(U)]
            st = sb("st", [P, NT, 6], scope=sc)
            mv = sb("mv", [P, NT, 2], scope=sc)
            rstd = sb("rstd", [P, NT], scope=sc)
            nrm = [sb(f"nrm{u}", [P, C, D], scope=sc) for u in range(U)]
            f_t = [sb(f"f_t{u}", [P, C * P], scope=sc) for u in range(U)]
            qk = [sb(f"qk{u}", [P, C, QK], scope=sc) for u in range(U)]
            ex_room = [sb(f"ex{u}", [P, C * QK], scope=sc) for u in range(U)]
            lg_room = [sb(f"lg{u}", [P, C * QK], scope=sc) for u in range(U)]
            ex = [r[:, :].rearrange("p (c d) -> p c d", c=C) for r in ex_room]
            lg = [r[:, :].rearrange("p (c d) -> p c d", c=C) for r in lg_room]
            q_t = [r[:, 0:C * P] for r in ex_room]
            pay = [r[:, 0:C * PAY].rearrange("p (c d) -> p c d", c=C) for r in ex_room]
            hot_t = [r[0:E, 0:C * P] for r in lg_room]
            red = [r[:, 0:C * VE * H].rearrange("p (c e h) -> p c e h", c=C, e=VE) for r in lg_room]
            v1 = [sb(f"v1{u}", [P, C, VE, H], scope=sc) for u in range(U)]
            kv = [sb(f"kv{j}", [P, HD, D], scope=sc) for j in range(2)]
            qc = [sb(f"qc{j}", [P, VE * D], scope=sc) for j in range(2)]
            ds = [sb(f"ds{u}", [P, VE, H], scope=sc) for u in range(U)]
            skv = [sb(f"skv{u}", [P, VE, H], scope=sc) for u in range(U)]
            rden = sb("rden", [P, NT, H], scope=sc)
            masked = [sb(f"masked{u}", [P, C * P], scope=sc) for u in range(U)]
            logit = sb("logit", [P, NT, E], scope=sc)
            top = sb("top", [P, NT, 8], scope=sc)
            idx = sb("idx", [P, NT, 8], U32, scope=sc)
            idf = sb("idf", [P, 2, NT], scope=sc)
            hot = sb("hot", [P, 2, NT, E], scope=sc)
            both = sb("both", [P, NT, E], scope=sc)
            hot_b = [sb(f"hot_b{u}", [E, C * P], BF16, scope=sc) for u in range(U)]
            place = sb("place", [P, NT], scope=sc)
            wts = sb("wts", [P, 4, NT], scope=sc)
            tot = sb("tot", [P, E, NT], scope=sc)
            run = sb("run", [P, E, NT], scope=sc)
            rank = sb("rank", [P, NT, E], scope=sc)
            sel = sb("sel", [P, NT, E], scope=sc)
            pos = sb("pos", [P, 2, NT], scope=sc)
            posu = sb("posu", [P, 2, NT], U32, scope=sc)

            names = ("weights", "init", "x_free", "beta", "gamma", "y_added", "st", "mv", "ve", "rs", "normed", "turned", "feat",
                     "lg_ps", "lg", "max", "idx", "idf", "hot", "hot_ps", "hot_t", "hot_b", "spread", "masked", "moe", "moe_t",
                     "moe_ps", "x2", "qkv_ps", "qkv", "v", "abs", "exp", "ln", "relu", "u1", "cor", "qk", "q_ps", "q_t", "kv",
                     "tri", "qc", "red", "ds_ps", "ds", "skv", "so_ps", "state_in", "rden", "att", "att_ps", "att_t", "wo", "wo_t",
                     "wo_ps", "x3", "cb", "h4", "sq", "sm", "r4", "pay", "pay_ps", "pay_t", "gx", "x4", "ed", "ee", "e1", "p1",
                     "both", "rank_ps", "tot", "run", "excl", "r1", "r2", "sel", "pos", "posu", "extra", "base", "scat", "place", "place2", "pads", "padrow")
            s = {nm: sem(f"p3_{nm}") for nm in names}
            s_rows = [sem(f"p3_rows{u}") for u in range(U)]
            counts = sb("counts", [P, E], I32, scope=sc)

            class At:
                def __init__(self, eng, i):
                    self.eng, self.i, self.made = eng, i, {}

                def __call__(self, per, k):
                    if (per, k) not in self.made:
                        self.made[per, k] = self.eng.snap(self.i * per + k)
                    return self.made[per, k]

            def col(ap, i, u):
                return ap[:, bass.ds(i * U + u, 1)]

            def tile(i, u, c):
                return x_tok[:, bass.ds((i * U + u) * C + c, 1), :].squeeze(1)

            def seq(i, u):
                return x_tok[:, bass.ds((i * U + u) * C, C), :]

            with nc.Block() as block:
                @block.sync
                def _(sp):
                    sp.dma_start(wqkv[:, :], a["Wqkv_t"]).then_inc(s["weights"], 16)
                    sp.dma_start(wo[:, :], a["Wo_t"]).then_inc(s["weights"], 16)
                    sp.dma_start(ew0[:, :, :], a["ew0"]).then_inc(s["weights"], 16)
                    sp.dma_start(eb0[:, :], a["eb0"]).then_inc(s["weights"], 16)
                    for l in range(2):
                        sp.dma_start(gw[:, l, :], a[f"gw{l}"]).then_inc(s["weights"], 16)
                        sp.dma_start(gb[:, l, :], a[f"gb{l}"].partition_broadcast(P)).then_inc(s["weights"], 16)
                    sp.dma_start(bqkv[:, :], a["bqkv"].partition_broadcast(P)).then_inc(s["weights"], 16)
                    sp.dma_start(scale_ms[:, :], a["ns"].partition_broadcast(P)).then_inc(s["weights"], 16)
                    with sp.Fori(0, NI) as i:
                        at = At(sp, i)
                        for u in range(U):
                            sp.wait_ge(s["x_free"], at(U, u + 1))
                            src = rows_dram[bass.ds(i * U + u, 1), :].rearrange("o (j d) -> (o j) d", d=D)
                            sp.dma_start(rows[u][:, :, :], src.partition_broadcast(P)).then_inc(s_rows[u], 16)
                    for u in range(U):
                        sp.wait_ge(s_rows[u], 16 * NI)
                    sp.wait_ge(s["place"], 1)
                    for e in range(E):
                        row = sp.value_load(counts[0:1, e:e + 1], min_val=e * CAP, max_val=(e + 1) * CAP - P)
                        sp.dma_start(rows_of[bass.ds(row, P), :], far[:, :]).then_inc(s["pads"], 16)
                    sp.wait_ge(s["pads"], 16 * E)

                @block.gpsimd
                def _(pool):
                    with pool.Fori(0, NI) as i:
                        at = At(pool, i)

                        def rsqrt(nth):
                            hold(pool, s["mv"], at(4, nth + 1))
                            nc.gpsimd.tensor_scalar(rstd[:, :], mv[:, :, 1], EPS, None, ALU.add).then_inc(s["ve"], 1)
                            pool.wait_ge(s["ve"], at(4, nth + 1))
                            nc.gpsimd.tensor_tensor(rstd[:, :], rstd[:, :], k("minus_half"), ALU.pow).then_inc(s["rs"], 1)

                        for u in range(U):
                            hold(pool, s_rows[u], at(16, 16))
                            nc.gpsimd.tensor_tensor(seq(i, u), seq(i, u), rows[u][:, 1:2, :].to_broadcast([P, C, D]), ALU.add).then_inc(s["beta"], 1)
                        rsqrt(0)
                        rsqrt(1)
                        rsqrt(2)
                        for u in range(U):
                            pool.wait_ge(s["u1"], at(U, u + 1))
                            nc.gpsimd.tensor_tensor(lg[u][:, :, :], ex[u][:, :, :], lg[u][:, :, :], ALU.subtract).then_inc(s["cor"], 1)
                        for c in range(C):
                            for u in range(U):
                                j = (c * U + u) % 2
                                t = c * U + u
                                if t >= 2:
                                    pool.wait_ge(s["tri"], at(NT, t - 1))
                                if c == 0:
                                    pool.wait_ge(s["qk"], at(U, u + 1))
                                k_in = qk[u][:, c, D:QK].rearrange("p (h d) -> p h d", h=H).unsqueeze(1).to_broadcast([P, HD, H, HD])
                                v_in = v1[u][:, c, 0:HD, :].unsqueeze(3).to_broadcast([P, HD, H, HD])
                                nc.gpsimd.tensor_tensor(kv[j][:, :, :].rearrange("p e (h d) -> p e h d", h=H), k_in, v_in, ALU.mult).then_inc(s["kv"], 1)
                        rsqrt(3)
                        for u in range(U):
                            pool.wait_ge(s["cb"], at(U, u + 1))
                            nc.gpsimd.tensor_tensor(nrm[u][:, :, :], nrm[u][:, :, :], rows[u][:, 3:4, :].to_broadcast([P, C, D]), ALU.add).then_inc(s["h4"], 1)
                        hold(pool, s["sq"], at(1, 1))
                        nc.gpsimd.tensor_scalar(rstd[:, :], rstd[:, :], 1.0 / D, EPS, ALU.mult, ALU.add).then_inc(s["sm"], 1)
                        pool.wait_ge(s["sm"], at(1, 1))
                        nc.gpsimd.tensor_tensor(rstd[:, :], rstd[:, :], k("minus_half"), ALU.pow).then_inc(s["r4"], 1)
                        for u in range(U):
                            hold(pool, s["gx"], at(U, u + 1))
                            nc.gpsimd.tensor_tensor(seq(i, u), seq(i, u), masked[u][:, :].rearrange("p (c d) -> p c d", c=C), ALU.add).then_inc(s["x4"], 1)
                        pool.wait_ge(s["posu"], at(1, 1))
                        hold(pool, s["extra"], at(1, 1))
                        for t in range(NT):
                            for slot in range(2):
                                nc.gpsimd.indirect_dma_start(
                                    rows_of, bass.IndirectOffsetOnAxis(ap=posu[:, slot, t:t + 1], axis=0),
                                    pay[t // C][:, t % C, :], None).then_inc(s["scat"], 16)
                        pool.wait_ge(s["scat"], at(16 * 2 * NT, 16 * 2 * NT))

                @block.scalar
                def _(act):
                    with act.Fori(0, NI) as i:
                        at = At(act, i)

                        def feat(nth, bias, scale):
                            for u in range(U):
                                act.wait_ge(s["turned"], at(2 * U, nth * U + u + 1))
                                nc.scalar.activation(f_t[u][:, :], ps[:, u, :], ACT.Identity, bias=col(mod_t[:, bias, :], i, u),
                                                     scale=col(mod_t[:, scale, :], i, u)).then_inc(s["feat"], 1)
                        feat(0, SB0, CB0)
                        for u in range(U):
                            act.wait_ge(s["hot_t"], at(U, u + 1))
                            nc.scalar.activation(hot_b[u][:, :], hot_t[u][:, :], ACT.Copy).then_inc(s["hot_b"], 1)
                        for u in range(U):
                            act.wait_ge(s["moe"], at(U, u + 1))
                            nc.scalar.activation(masked[u][:, :], ps[:, u, :], ACT.Copy, scale=col(mod_t[:, GB0, :], i, u)).then_inc(s["moe_t"], 1)
                        feat(1, SA1, CA1)
                        for u in range(U):
                            act.wait_ge(s["qkv"], at(U, u + 1))
                            nc.scalar.activation(ex[u][:, :, :], qk[u][:, :, :], ACT.Abs).then_inc(s["abs"], 1)
                        for u in range(U):
                            act.wait_ge(s["abs"], at(U, u + 1))
                            nc.scalar.activation(ex[u][:, :, :], ex[u][:, :, :], ACT.Exp, scale=-1.0).then_inc(s["exp"], 1)
                        for u in range(U):
                            act.wait_ge(s["exp"], at(U, u + 1))
                            nc.scalar.activation(lg[u][:, :, :], ex[u][:, :, :], ACT.Ln, bias=1.0).then_inc(s["ln"], 1)
                        for u in range(U):
                            act.wait_ge(s["q_ps"], at(U, u + 1))
                            nc.scalar.activation(q_t[u][:, :], ps[:, u, :], ACT.Copy).then_inc(s["q_t"], 1)
                        for u in range(U):
                            act.wait_ge(s["att_ps"], at(U, u + 1))
                            nc.scalar.activation(f_t[u][:, :], ps[:, u, :], ACT.Copy).then_inc(s["att_t"], 1)
                        for u in range(U):
                            act.wait_ge(s["wo"], at(U, u + 1))
                            nc.scalar.activation(masked[u][:, :], ps[:, 4 + u, :], ACT.Identity, bias=col(mod_t[:, GA_BO, :], i, u),
                                                 scale=col(mod_t[:, GA1, :], i, u)).then_inc(s["wo_t"], 1)
                        for u in range(U):
                            act.wait_ge(s["h4"], at(U, u + 1))
                            for c in range(C):
                                last = nc.scalar.activation(masked[u][:, c * P:(c + 1) * P], nrm[u][:, c, :], ACT.Square,
                                                            accum_out=rstd[:, u * C + c:u * C + c + 1])
                        last.then_inc(s["sq"], 1)
                        for u in range(U):
                            act.wait_ge(s["pay_ps"], at(U, u + 1))
                            nc.scalar.activation(f_t[u][:, :], ps[:, u, :], ACT.Copy).then_inc(s["pay_t"], 1)
                        act.wait_ge(s["ed"], at(1, 1))
                        nc.scalar.activation(wts[:, 1, :], wts[:, 0, :], ACT.Exp).then_inc(s["ee"], 1)

                @block.vector
                def _(dve):
                    dve.wait_ge(s["weights"], 10 * 16)
                    last = nc.vector.tensor_copy(pick[:, :, :], k("ident", E)[:, 0:E].unsqueeze(2).to_broadcast([E, E, P]))
                    for u in range(U):
                        nc.vector.memset(v1[u][:, :, HD:VE, :], 1.0)
                    nc.vector.memset(far[:, :], 0.0).then_inc(s["padrow"], 1)
                    dve.wait_ge(s["padrow"], 1)
                    nc.vector.memset(far[:, D:D + 1], NOWHERE)
                    nc.vector.memset(far[:, D + 1:D + 2], -1.0).then_inc(s["padrow"], 1)
                    nc.vector.tensor_scalar(base[:, :], k("iota"), float(CAP), None, ALU.mult)
                    nc.vector.tensor_copy(place[:, :], k("token")).then_inc(s["init"], 1)
                    nc.vector.memset(ds[0][:, :, :], 0.0).then_inc(s["x_free"], U)
                    with dve.Fori(0, NI) as i:
                        at = At(dve, i)

                        def stats(nth, tiles, ready):
                            for u in range(U):
                                ready(u)
                                for c in range(C):
                                    last = nc.vector.bn_stats(st[:, u * C + c, :], tiles(u, c))
                            last.then_inc(s["st"], 1)
                            hold(dve, s["st"], at(4, nth + 1))
                            for t in range(NT):
                                last = nc.vector.bn_aggr(mv[:, t, :], st[:, t, :])
                            last.then_inc(s["mv"], 1)
                            dve.wait_ge(s["rs"], at(4, nth + 1))
                            for u in range(U):
                                for c in range(C):
                                    t = u * C + c
                                    last = nc.vector.tensor_scalar(nrm[u][:, c, :], tiles(u, c), mv[:, t, 0:1], rstd[:, t:t + 1],
                                                                   ALU.subtract, ALU.mult)
                                last.then_inc(s["normed"], 1)

                        def y_tile(u, c):
                            return xg[:, :, bass.ds((i * U + u) * C + c, 1)].squeeze(2)

                        stats(0, y_tile, lambda u: None)
                        for u in range(U):
                            dve.wait_ge(s["normed"], at(4 * U, u + 1))
                            dve.wait_ge(s_rows[u], at(16, 16))
                            nc.vector.tensor_tensor(nrm[u][:, :, :], nrm[u][:, :, :], rows[u][:, 0:1, :].to_broadcast([P, C, D]), ALU.mult).then_inc(s["gamma"], 1)
                        for u in range(U):
                            dve.wait_ge(s["gamma"], at(U, u + 1))
                            dve.wait_ge(s["beta"], at(U, u + 1))
                            nc.vector.tensor_tensor(seq(i, u), seq(i, u), nrm[u][:, :, :], ALU.add).then_inc(s["y_added"], 1)
                        stats(1, lambda u, c: tile(i, u, c), lambda u: hold(dve, s["y_added"], at(U, u + 1)))

                        def best(nth, bias):
                            dve.wait_ge(s["lg_ps"], at(2, nth + 1))
                            nc.vector.tensor_tensor(logit[:, :, :], ps[:, 4, 0:NT * E].rearrange("p (t e) -> p t e", e=E),
                                                    bias.to_broadcast([P, NT, E]), ALU.add).then_inc(s["lg"], 1)
                            hold(dve, s["lg"], at(2, nth + 1))
                            for t in range(NT):
                                last = nc.vector.max(top[:, t, :], logit[:, t, :])
                            last.then_inc(s["max"], 1)
                            hold(dve, s["max"], at(2, nth + 1))
                            for t in range(NT):
                                last = nc.vector.max_index(idx[:, t, :], top[:, t, :], logit[:, t, :])
                            last.then_inc(s["idx"], 1)
                            dve.wait_ge(s["idx"], at(2, nth + 1))
                            nc.vector.tensor_copy(idf[:, :, :], idx[:, :, 0:2].rearrange("p t j -> p j t")).then_inc(s["idf"], 1)
                            dve.wait_ge(s["idf"], at(2, nth + 1))
                            for j in range(1 + nth):
                                last = nc.vector.tensor_tensor(hot[:, j, :, :], k("iota").unsqueeze(1).to_broadcast([P, NT, E]),
                                                               idf[:, j, :].unsqueeze(2).to_broadcast([P, NT, E]), ALU.is_equal)
                            last.then_inc(s["hot"], 1)

                        best(0, gb[:, 0:1, :])
                        for u in range(U):
                            dve.wait_ge(s["hot_ps"], at(U, u + 1))
                            nc.vector.tensor_copy(hot_t[u][:, :], ps[0:E, 4 + u, :]).then_inc(s["hot_t"], 1)
                        for e in range(E):
                            for u in range(U):
                                dve.wait_ge(s["spread"], at(E * U, e * U + u + 1))
                                nc.vector.tensor_tensor(masked[u][:, :], f_t[u][:, :], ps[:, 4 + u, :], ALU.mult).then_inc(s["masked"], 1)
                        for u in range(U):
                            dve.wait_ge(s["moe_ps"], at(U, u + 1))
                            nc.vector.tensor_tensor(seq(i, u), seq(i, u), ps[:, 4 + u, :].rearrange("p (c d) -> p c d", c=C), ALU.add).then_inc(s["x2"], 1)
                        stats(2, lambda u, c: tile(i, u, c), lambda u: hold(dve, s["x2"], at(U, u + 1)))

                        for u in range(U):
                            dve.wait_ge(s["qkv_ps"], at(U, u + 1))
                            bank = 4 * (u % 2)
                            nc.vector.tensor_tensor(qk[u][:, :, :], ps[:, bank:bank + C, 0:QK],
                                                    bqkv[:, 0:QK].unsqueeze(1).to_broadcast([P, C, QK]), ALU.add).then_inc(s["qkv"], 1)
                            for c in range(C):
                                last = nc.vector.tensor_tensor(v1[u][:, c, 0:HD, :].rearrange("p e h -> p h e"),
                                                        ps[:, bank + c, QK:3 * D].rearrange("p (h e) -> p h e", h=H),
                                                        bqkv[:, QK:3 * D].rearrange("p (h e) -> p h e", h=H), ALU.add)
                            last.then_inc(s["v"], 1)
                        for u in range(U):
                            dve.wait_ge(s["ln"], at(U, u + 1))
                            nc.vector.scalar_tensor_tensor(qk[u][:, :, :], qk[u][:, :, :], 0.0, lg[u][:, :, :], ALU.max, ALU.add).then_inc(s["relu"], 1)
                            dve.wait_ge(s["relu"], at(U, u + 1))
                            nc.vector.tensor_scalar(lg[u][:, :, :], ex[u][:, :, :], 1.0, -1.0, ALU.add, ALU.add).then_inc(s["u1"], 1)
                        for u in range(U):
                            dve.wait_ge(s["cor"], at(U, u + 1))
                            nc.vector.tensor_tensor(qk[u][:, :, :], qk[u][:, :, :], lg[u][:, :, :], ALU.add).then_inc(s["qk"], 1)
                        for c in range(C):
                            for u in range(U):
                                t = c * U + u
                                j = t % 2
                                if c < C - 1:
                                    dve.wait_ge(s["ds_ps"], at((C - 1) * U, t + 1))
                                    mask = k("head_of").unsqueeze(1).to_broadcast([P, VE, H])
                                    dst = skv[u] if c == 0 else ds[u]
                                    nc.vector.tensor_tensor(dst[:, :, :], ps[:, 6, 0:VE * H].rearrange("p (e h) -> p e h", h=H), mask, ALU.mult).then_inc(s["ds"], 1)
                                dve.wait_ge(s["tri"], at(NT, t + 1))
                                q_in = qk[u][:, c, 0:D].unsqueeze(1).to_broadcast([P, VE, D])
                                nc.vector.tensor_tensor(qc[j][:, :].rearrange("p (e d) -> p e d", d=D),
                                                        ps3(j)[:, 0:VE * D].rearrange("p (e d) -> p e d", d=D), q_in, ALU.mult).then_inc(s["qc"], 1)
                                dve.wait_ge(s["qc"], at(NT, t + 1))
                                nc.vector.tensor_reduce(red[u][:, c, :, :].rearrange("p e h -> p (e h)"),
                                                        qc[j][:, :].rearrange("p (g d) -> p g d", d=HD), AX.X, ALU.add).then_inc(s["red"], 1)
                                if c:
                                    dve.wait_ge(s["so_ps"], at((C - 1) * U, t - U + 1))
                                    dve.wait_ge(s["red"], at(NT, t + 1))
                                    nc.vector.tensor_tensor(red[u][:, c, :, :].rearrange("p e h -> p (e h)"), red[u][:, c, :, :].rearrange("p e h -> p (e h)"),
                                                            ps[:, 7, 0:VE * H], ALU.add).then_inc(s["state_in"], 1)
                                if 0 < c < C - 1:
                                    dve.wait_ge(s["ds"], at((C - 1) * U, t + 1))
                                    nc.vector.tensor_tensor(skv[u][:, :, :], skv[u][:, :, :], ds[u][:, :, :], ALU.add).then_inc(s["skv"], 1)
                        for u in range(U):
                            dve.wait_ge(s["red"], at(NT, NT))
                            dve.wait_ge(s["state_in"], at((C - 1) * U, (C - 1) * U))
                            nc.vector.reciprocal(rden[:, u * C:(u + 1) * C, :], red[u][:, :, HD, :]).then_inc(s["rden"], 1)
                        for u in range(U):
                            dve.wait_ge(s["rden"], at(U, u + 1))
                            for c in range(C):
                                last = nc.vector.tensor_tensor(nrm[u][:, c, :].rearrange("p (h e) -> p h e", h=H),
                                                        red[u][:, c, 0:HD, :].rearrange("p e h -> p h e"),
                                                        rden[:, u * C + c, :].unsqueeze(2).to_broadcast([P, H, HD]), ALU.mult)
                            last.then_inc(s["att"], 1)
                        for u in range(U):
                            dve.wait_ge(s["wo_ps"], at(U, u + 1))
                            nc.vector.tensor_tensor(seq(i, u), seq(i, u), ps[:, u, :].rearrange("p (c d) -> p c d", c=C), ALU.add).then_inc(s["x3"], 1)
                        stats(3, lambda u, c: tile(i, u, c), lambda u: hold(dve, s["x3"], at(U, u + 1)))
                        for u in range(U):
                            dve.wait_ge(s["normed"], at(4 * U, 3 * U + u + 1))
                            nc.vector.tensor_tensor(nrm[u][:, :, :], nrm[u][:, :, :], rows[u][:, 2:3, :].to_broadcast([P, C, D]), ALU.mult).then_inc(s["cb"], 1)
                        dve.wait_ge(s["r4"], at(1, 1))
                        for u in range(U):
                            for c in range(C):
                                last = nc.vector.scalar_tensor_tensor(pay[u][:, c, 0:D], nrm[u][:, c, :], rstd[:, u * C + c:u * C + c + 1],
                                                                      scale_ms[:, :], ALU.mult, ALU.mult)
                            last.then_inc(s["pay"], 1)
                        for u in range(U):
                            nc.vector.tensor_tensor(masked[u][:, :].rearrange("p (c d) -> p c d", c=C), nrm[u][:, :, :],
                                                    rows[u][:, 4:5, :].to_broadcast([P, C, D]), ALU.mult).then_inc(s["gx"], 1)
                        best(1, gb[:, 1:2, :])
                        nc.vector.tensor_tensor(wts[:, 0, :], top[:, :, 1], top[:, :, 0], ALU.subtract).then_inc(s["ed"], 1)
                        dve.wait_ge(s["hot"], at(2, 2))
                        nc.vector.tensor_tensor(both[:, :, :], hot[:, 0, :, :], hot[:, 1, :, :], ALU.add).then_inc(s["both"], 1)
                        dve.wait_ge(s["ee"], at(1, 1))
                        nc.vector.tensor_scalar(wts[:, 2, :], wts[:, 1, :], 1.0, None, ALU.add).then_inc(s["e1"], 1)
                        dve.wait_ge(s["e1"], at(1, 1))
                        nc.vector.reciprocal(wts[:, 3, :], wts[:, 2, :]).then_inc(s["p1"], 1)
                        dve.wait_ge(s["rank_ps"], at(1, 1))
                        nc.vector.tensor_copy(tot[:, :, :], ps[:, 6, 0:NT * E].rearrange("p (t e) -> p e t", e=E)).then_inc(s["tot"], 1)
                        dve.wait_ge(s["p1"], at(1, 1))
                        for u in range(U):
                            ts = slice(u * C, (u + 1) * C)
                            nc.vector.tensor_copy(pay[u][:, :, D:D + 1], place[:, ts].unsqueeze(2))
                            nc.vector.tensor_copy(pay[u][:, :, D + 1:D + 2], idf[:, 1, ts].unsqueeze(2))
                            nc.vector.tensor_copy(pay[u][:, :, D + 2:D + 3], wts[:, 3, ts].unsqueeze(2))
                            last = nc.vector.scalar_tensor_tensor(pay[u][:, :, D + 3:D + 4], wts[:, 1, ts].unsqueeze(2), -1.0,
                                                                  wts[:, 3, ts].unsqueeze(2), ALU.add, ALU.mult)
                        last.then_inc(s["extra"], 1)
                        dve.wait_ge(s["tot"], at(1, 1))
                        nc.vector.tensor_tensor_scan(run[:, :, :].rearrange("p e t -> p (e t)"), k("restart"),
                                                     tot[:, :, :].rearrange("p e t -> p (e t)"), 0.0, ALU.mult, ALU.add).then_inc(s["run"], 1)
                        dve.wait_ge(s["run"], at(1, 1))
                        nc.vector.tensor_tensor(tot[:, :, :], run[:, :, :], tot[:, :, :], ALU.subtract).then_inc(s["excl"], 1)
                        dve.wait_ge(s["excl"], at(1, 1))
                        nc.vector.tensor_tensor(rank[:, :, :], ps[:, 5, 0:NT * E].rearrange("p (t e) -> p t e", e=E),
                                                tot[:, :, :].rearrange("p e t -> p t e"), ALU.add).then_inc(s["r1"], 1)
                        dve.wait_ge(s["r1"], at(1, 1))
                        nc.vector.tensor_tensor(rank[:, :, :], rank[:, :, :], base[:, :].unsqueeze(1).to_broadcast([P, NT, E]), ALU.add).then_inc(s["r2"], 1)
                        dve.wait_ge(s["r2"], at(1, 1))
                        nc.vector.tensor_tensor(base[:, :], base[:, :], run[:, :, NT - 1], ALU.add).then_inc(s["base"], 1)
                        for j in range(2):
                            nc.vector.tensor_tensor(sel[:, :, :], rank[:, :, :], hot[:, j, :, :], ALU.mult).then_inc(s["sel"], 1)
                            dve.wait_ge(s["sel"], at(2, j + 1))
                            nc.vector.tensor_reduce(pos[:, j, :], sel[:, :, :], AX.X, ALU.add).then_inc(s["pos"], 1)
                            dve.wait_ge(s["pos"], at(2, j + 1))
                        nc.vector.tensor_copy(posu[:, :, :], pos[:, :, :]).then_inc(s["posu"], 1)
                        nc.vector.tensor_scalar(place[:, :], place[:, :], float(NT * P), None, ALU.add).then_inc(s["place2"], 1)
                        dve.wait_ge(s["place2"], at(1, 1))
                        dve.wait_ge(s["base"], at(1, 1))
                        dve.wait_ge(s["scat"], at(16 * 2 * NT, 16 * 2 * NT))
                        dve.wait_ge(s["x4"], at(U, U))
                        nc.vector.memset(ds[0][:, :, :], 0.0).then_inc(s["x_free"], U)
                    nc.vector.tensor_copy(counts[:, :], base[:, :]).then_inc(s["place"], 1)

                @block.tensor
                def _(pe):
                    pe.wait_ge(s["weights"], 10 * 16)
                    pe.wait_ge(s["init"], 1)
                    with pe.Fori(0, NI) as i:
                        at = At(pe, i)

                        def turn(src, u, bank):
                            for c in range(C):
                                last = nc.tensor.transpose(ps[:, bank, c * P:(c + 1) * P], src[u][:, c * P:(c + 1) * P], ident)
                            return last

                        def turn_tok(src, u, bank):
                            for c in range(C):
                                last = nc.tensor.transpose(ps[:, bank, c * P:(c + 1) * P], src[u][:, c, 0:D], ident)
                            return last

                        def logits(l):
                            for u in range(U):
                                pe.wait_ge(s["pay_t" if l else "feat"], at(U if l else 2 * U, u + 1))
                                for c in range(C):
                                    t = u * C + c
                                    last = nc.tensor.matmul(ps[:, 4, t * E:(t + 1) * E], f_t[u][:, c * P:(c + 1) * P], gw[:, l, :],
                                                            start=True, stop=True)
                            last.then_inc(s["lg_ps"], 1)

                        for u in range(U):
                            pe.wait_ge(s["normed"], at(4 * U, U + u + 1))
                            turn_tok(nrm, u, u).then_inc(s["turned"], 1)
                        logits(0)
                        pe.wait_ge(s["hot"], at(2, 1))
                        for u in range(U):
                            for c in range(C):
                                last = nc.tensor.transpose(ps[0:E, 4 + u, c * P:(c + 1) * P], hot[:, 0, u * C + c, :], ident)
                            last.then_inc(s["hot_ps"], 1)
                        for u in range(U):
                            pe.wait_ge(s["hot_t"], at(U, u + 1))
                            nc.tensor.matmul(ps[:, u, :], eb0[:, :], hot_t[u][:, :], start=True, stop=False)
                            pe.wait_ge(s["hot_b"], at(U, u + 1))
                            nc.tensor.matmul(ps[:, 4 + u, :], pick[:, 0, :], hot_b[u][:, :], start=True, stop=True).then_inc(s["spread"], 1)
                        for e in range(E):
                            for u in range(U):
                                pe.wait_ge(s["masked"], at(E * U, e * U + u + 1))
                                last = nc.tensor.matmul(ps[:, u, :], ew0[:, e, :], masked[u][:, :], start=False, stop=(e == E - 1))
                                if e < E - 1:
                                    nc.tensor.matmul(ps[:, 4 + u, :], pick[:, e + 1, :], hot_b[u][:, :], start=True, stop=True).then_inc(s["spread"], 1)
                                else:
                                    last.then_inc(s["moe"], 1)
                        for u in range(U):
                            pe.wait_ge(s["moe_t"], at(U, u + 1))
                            turn(masked, u, 4 + u).then_inc(s["moe_ps"], 1)
                        for u in range(U):
                            pe.wait_ge(s["normed"], at(4 * U, 2 * U + u + 1))
                            turn_tok(nrm, u, u).then_inc(s["turned"], 1)
                        for u in range(U):
                            bank = 4 * (u % 2)
                            pe.wait_ge(s["feat"], at(2 * U, U + u + 1))
                            if u == 0:
                                pe.wait_ge(s["feat"], at(2 * U, 2 * U))
                            if u >= 2:
                                pe.wait_ge(s["v"], at(U, u - 1))
                            for c in range(C):
                                last = nc.tensor.matmul(ps[:, bank + c, 0:3 * D], f_t[u][:, c * P:(c + 1) * P], wqkv[:, :], start=True, stop=True)
                            last.then_inc(s["qkv_ps"], 1)
                        for u in range(U):
                            pe.wait_ge(s["qk"], at(U, u + 1))
                            turn_tok(qk, u, u).then_inc(s["q_ps"], 1)
                        pe.wait_ge(s["q_t"], at(U, U))
                        for c in range(C):
                            for u in range(U):
                                t = c * U + u
                                j = t % 2
                                if c < C - 1:
                                    pe.wait_ge(s["v"], at(U, u + 1))
                                    if t:
                                        pe.wait_ge(s["ds"], at((C - 1) * U, t))
                                    nc.tensor.matmul(ps[:, 6, 0:VE * H], qk[u][:, c, D:QK], v1[u][:, c, :, :].rearrange("p e h -> p (e h)"),
                                                     start=True, stop=True).then_inc(s["ds_ps"], 1)
                                if c:
                                    if c == 1:
                                        pe.wait_ge(s["ds"], at((C - 1) * U, u + 1))
                                    else:
                                        pe.wait_ge(s["skv"], at((C - 2) * U, (c - 2) * U + u + 1))
                                    if t > U:
                                        pe.wait_ge(s["state_in"], at((C - 1) * U, t - U))
                                    nc.tensor.matmul(ps[:, 7, 0:VE * H], q_t[u][:, c * P:(c + 1) * P], skv[u][:, :, :].rearrange("p e h -> p (e h)"),
                                                     start=True, stop=True).then_inc(s["so_ps"], 1)
                                if t >= 2:
                                    pe.wait_ge(s["qc"], at(NT, t - 1))
                                pe.wait_ge(s["kv"], at(NT, t + 1))
                                for m in range(2):
                                    nc.tensor.matmul(ps[:, 3 * j + m, :], k("upto"), kv[j][:, 4 * m:4 * m + 4, :].rearrange("p e d -> p (e d)"),
                                                     start=True, stop=True)
                                nc.tensor.matmul(ps[:, 3 * j + 2, 0:D], k("upto"), qk[u][:, c, D:QK], start=True, stop=True).then_inc(s["tri"], 1)
                        for u in range(U):
                            pe.wait_ge(s["att"], at(U, u + 1))
                            turn_tok(nrm, u, u).then_inc(s["att_ps"], 1)
                        for u in range(U):
                            pe.wait_ge(s["att_t"], at(U, u + 1))
                            nc.tensor.matmul(ps[:, 4 + u, :], wo[:, :], f_t[u][:, :], start=True, stop=True).then_inc(s["wo"], 1)
                        for u in range(U):
                            pe.wait_ge(s["wo_t"], at(U, u + 1))
                            turn(masked, u, u).then_inc(s["wo_ps"], 1)
                        for u in range(U):
                            pe.wait_ge(s["pay"], at(U, u + 1))
                            turn_tok(pay, u, u).then_inc(s["pay_ps"], 1)
                        logits(1)
                        pe.wait_ge(s["both"], at(1, 1))
                        nc.tensor.matmul(ps[:, 5, 0:NT * E], k("before"), both[:, :, :].rearrange("p t e -> p (t e)"), start=True, stop=True)
                        nc.tensor.matmul(ps[:, 6, 0:NT * E], k("ones"), both[:, :, :].rearrange("p t e -> p (t e)"), start=True, stop=True).then_inc(s["rank_ps"], 1)

        end_phase()

        V = 4
        BT = -(-(2 * TILES + E - 1) // V) * V
        I1 = I2 // 2
        parts = nc.dram_tensor("parts", [(2 * TILES + BT) * P, D], F32).ap()
        with ExitStack() as sc:
            w1 = sb("w1", [P, E * I2], scope=sc)
            w2 = sb("w2", [P, E * 2, D], scope=sc)
            b1 = sb("b1", [P, E * I2], scope=sc)
            b2 = sb("b2", [P, E, D], scope=sc)
            number = sb("number", [P, BT], scope=sc)
            cnt = sb("cnt", [P, E], scope=sc)
            cnti = sb("cnti", [P, E], I32, scope=sc)
            nti = sb("nti", [P, E], I32, scope=sc)
            ntile = sb("ntile", [P, E], scope=sc)
            upto = sb("upto_e", [P, E], scope=sc)
            first = sb("first", [P, E], scope=sc)
            step = sb("step", [P, E], scope=sc)
            last_tile = sb("last_tile", [P, 1], scope=sc)
            surplus = sb("surplus", [P, BT], scope=sc)
            beside = sb("beside", [P, BT], scope=sc)
            ge = sb("ge", [P, BT, E], scope=sc)
            gst = sb("gst", [P, BT, E], scope=sc)
            expert = sb("expert", [P, BT], scope=sc)
            row = sb("row", [P, BT], scope=sc)
            meta = sb("meta", [P, 4, BT], I32, scope=sc)
            ROW, EXP, W1AT, W2AT = range(4)
            metaf = sb("metaf", [P, 2, BT], scope=sc)
            xt = sb("xt", [P, V, PAY], scope=sc)
            x_t = [sb(f"x_t{v}", [P, P], scope=sc) for v in range(V)]
            hid = [sb(f"hid{v}", [P, I2], scope=sc) for v in range(V)]
            sg = [sb(f"sg{v}", [P, I1], scope=sc) for v in range(V)]
            act_t = [sb(f"act_t{v}", [P, 2, P], scope=sc) for v in range(V)]
            y = [sb(f"y{v}", [P, D], scope=sc) for v in range(V)]
            yw = [sb(f"yw{v}", [P, D], scope=sc) for v in range(V)]
            sent = sb("sent", [P, 1], scope=sc)
            own = sb("own", [P, 4, V], scope=sc)
            dest = sb("dest", [P, V], U32, scope=sc)
            names = ("weights", "count", "plan", "meta", "x_ps", "x_t", "h_ps", "h", "clip", "sig", "lin", "gs", "a", "a_ps",
                     "a_t", "y_ps", "y", "yw", "second", "own", "dest", "sent")
            s = {nm: sem(f"p4_{nm}") for nm in names}
            s_in = [sem(f"p4_rows{v}") for v in range(V)]
            s_out = [sem(f"p4_out{v}") for v in range(V)]
            with nc.Block() as block:
                @block.sync
                def _(sp):
                    sp.dma_start(w1[:, :], a["w1"].rearrange("p e i -> p (e i)")).then_inc(s["weights"], 16)
                    sp.dma_start(w2[:, :, :], a["w2"].rearrange("p e k d -> p (e k) d")).then_inc(s["weights"], 16)
                    sp.dma_start(b1[:, :], a["b1"].rearrange("e i -> (e i)").partition_broadcast(P)).then_inc(s["weights"], 16)
                    sp.dma_start(b2[:, :, :].rearrange("p e d -> p (e d)"), a["b2"].rearrange("e d -> (e d)").partition_broadcast(P)).then_inc(s["weights"], 16)
                    sp.dma_start(number[:, :], a["numbers"].partition_broadcast(P)).then_inc(s["weights"], 16)
                    sp.wait_ge(s["meta"], 4)

                    def load(t, v):
                        at = sp.value_load(meta[0:1, ROW, t], min_val=0, max_val=E * CAP - P)
                        sp.dma_start(xt[:, v, :], rows_of[bass.ds(at, P), :]).then_inc(s_in[v], 16)
                    for v in range(V):
                        load(slice(v, v + 1), v)
                    with sp.Fori(1, BT // V) as i:
                        for v in range(V):
                            used = sp.snap(i * V + (v + 1 - V))
                            sp.wait_ge(s["x_ps"], used)
                            sp.wait_ge(s["dest"], i)
                            load(bass.ds(i * V + v, 1), v)
                    for v in range(V):
                        sp.wait_ge(s_in[v], 16 * (BT // V))

                @block.gpsimd
                def _(pool):
                    with pool.Fori(0, BT // V) as i:
                        landed = pool.snap(i * 16 + 16)
                        n = [pool.snap(i * V + v + 1) for v in range(V)]
                        nv = [pool.snap(i * V + v + 1 + V) for v in range(V)]
                        for v in range(V):
                            pool.wait_ge(s["sig"], n[v])
                            nc.gpsimd.tensor_tensor(sg[v][:, :], sg[v][:, :], hid[v][:, 0:I1], ALU.mult).then_inc(s["gs"], 1)
                        for v in range(V):
                            hold(pool, s["yw"], nv[v], i)
                            nc.gpsimd.indirect_dma_start(parts, bass.IndirectOffsetOnAxis(ap=dest[:, v:v + 1], axis=0),
                                                         yw[v][:, :], None).then_inc(s_out[v], 16)
                        for v in range(V - 1):
                            pool.wait_ge(s_out[v], landed)
                        hold(pool, s_out[V - 1], landed)
                        nc.gpsimd.tensor_tensor(sent[:, :], k("ones")[:, 0:1], k("ones")[:, 0:1], ALU.mult).then_inc(s["sent"], 1)

                @block.scalar
                def _(act):
                    with act.Fori(0, BT // V) as i:
                        it = act.snap(i + 1)
                        n = [act.snap(i * V + v + 1) for v in range(V)]
                        nv = [act.snap(i * V + v + 1 + V) for v in range(V)]
                        landed = act.snap(i * 16 + 16)
                        for v in range(V):
                            act.wait_ge(s["x_ps"], n[v])
                            nc.scalar.activation(x_t[v][:, :], ps[:, v, 0:P], ACT.Copy).then_inc(s["x_t"], 1)
                        for v in range(V):
                            act.wait_ge(s["clip"], n[v])
                            nc.scalar.activation(sg[v][:, :], hid[v][:, 0:I1], ACT.Sigmoid, scale=1.702).then_inc(s["sig"], 1)
                        for v in range(V):
                            act.wait_ge(s["a_ps"], n[v])
                            nc.scalar.activation(act_t[v][:, :, :], ps[:, v, P:3 * P].rearrange("p (k t) -> p k t", k=2), ACT.Copy).then_inc(s["a_t"], 1)
                        for v in range(V):
                            act.wait_ge(s["y"], nv[v])
                            act.wait_ge(s["sent"], it)
                            nc.scalar.activation(yw[v][:, :], y[v][:, :], ACT.Copy, scale=own[:, 2, v:v + 1]).then_inc(s["yw"], 1)

                @block.vector
                def _(dve):
                    c = [0]

                    def link(ins):
                        c[0] += 1
                        ins.then_inc(s["plan"], 1)
                        dve.wait_ge(s["plan"], c[0])
                    link(nc.vector.scalar_tensor_tensor(cnt[:, :], k("iota"), float(-CAP), base[:, :], ALU.mult, ALU.add))
                    link(nc.vector.tensor_scalar(cnt[:, :], cnt[:, :], float(P - 1), None, ALU.add))
                    link(nc.vector.tensor_copy(cnti[:, :], cnt[:, :]))
                    link(nc.vector.tensor_scalar(nti[:, :], cnti[:, :], 7, None, ALU.arith_shift_right))
                    link(nc.vector.tensor_copy(ntile[:, :], nti[:, :]))
                    link(nc.vector.tensor_tensor_scan(upto[:, :], k("ones")[:, 0:E], ntile[:, :], 0.0, ALU.mult, ALU.add))
                    nc.vector.tensor_scalar(last_tile[:, :], upto[:, E - 1:E], -1.0, None, ALU.add)
                    nc.vector.tensor_copy(step[:, 1:E], ntile[:, 0:E - 1])
                    nc.vector.memset(step[:, 0:1], 0.0)
                    link(nc.vector.tensor_tensor(first[:, :], upto[:, :], ntile[:, :], ALU.subtract))
                    dve.wait_ge(s["weights"], 5 * 16)
                    nc.vector.tensor_scalar(surplus[:, :], number[:, :], last_tile[:, :], NOWHERE, ALU.is_gt, ALU.mult)
                    link(nc.vector.tensor_scalar(beside[:, :], number[:, :], float(P), k("token")[:, 0:1], ALU.mult, ALU.add))
                    link(nc.vector.tensor_scalar(beside[:, :], beside[:, :], float(2 * TILES * P), None, ALU.add))
                    link(nc.vector.tensor_scalar(number[:, :], number[:, :], last_tile[:, :], None, ALU.min))
                    link(nc.vector.tensor_tensor(ge[:, :, :], number[:, :].unsqueeze(2).to_broadcast([P, BT, E]),
                                                 first[:, :].unsqueeze(1).to_broadcast([P, BT, E]), ALU.is_ge))
                    link(nc.vector.tensor_tensor(gst[:, :, :], ge[:, :, :], step[:, :].unsqueeze(1).to_broadcast([P, BT, E]), ALU.mult))
                    nc.vector.tensor_reduce(expert[:, :], ge[:, :, :], AX.X, ALU.add)
                    link(nc.vector.tensor_reduce(row[:, :], gst[:, :, :], AX.X, ALU.add))
                    link(nc.vector.tensor_scalar(expert[:, :], expert[:, :], -1.0, None, ALU.add))
                    link(nc.vector.tensor_tensor(row[:, :], number[:, :], row[:, :], ALU.subtract))
                    nc.vector.tensor_scalar(metaf[:, 0, :], expert[:, :], float(I2), None, ALU.mult)
                    nc.vector.tensor_scalar(metaf[:, 1, :], expert[:, :], 2.0, None, ALU.mult)
                    link(nc.vector.tensor_scalar(row[:, :], row[:, :], float(P), None, ALU.mult))
                    link(nc.vector.scalar_tensor_tensor(row[:, :], expert[:, :], float(CAP), row[:, :], ALU.mult, ALU.add))
                    nc.vector.tensor_copy(meta[:, ROW, :], row[:, :]).then_inc(s["meta"], 1)
                    nc.vector.tensor_copy(meta[:, EXP, :], expert[:, :]).then_inc(s["meta"], 1)
                    nc.vector.tensor_copy(meta[:, W1AT, :], metaf[:, 0, :]).then_inc(s["meta"], 1)
                    nc.vector.tensor_copy(meta[:, W2AT, :], metaf[:, 1, :]).then_inc(s["meta"], 1)
                    dve.wait_ge(s["meta"], 4)
                    nc.vector.memset(own[:, 0, :], 0.0).then_inc(s["y"], V)
                    nc.vector.memset(own[:, 1, :], 0.0).then_inc(s["yw"], V)
                    nc.vector.memset(own[:, 2, :], 0.0).then_inc(s["sent"], 1)
                    with dve.Fori(0, BT // V) as i:
                        n = [dve.snap(i * V + v + 1) for v in range(V)]
                        own1, own2, own3, own4 = (dve.snap(i * 4 + j) for j in range(1, 5))
                        it = dve.snap(i + 1)
                        landed = dve.snap(i * 16 + 16)
                        for v in range(V):
                            w1_at = dve.value_load(meta[0:1, W1AT, bass.ds(i * V + v, 1)], min_val=0, max_val=(E - 1) * I2)
                            dve.wait_ge(s["h_ps"], n[v])
                            nc.vector.tensor_tensor(hid[v][:, :], ps[:, 4 + v, :], b1[:, bass.ds(w1_at, I2)], ALU.add).then_inc(s["h"], 1)
                            dve.wait_ge(s["h"], n[v])
                            nc.vector.tensor_scalar(hid[v][:, 0:I1], hid[v][:, 0:I1], 7.0, None, ALU.min).then_inc(s["clip"], 1)
                            nc.vector.tensor_scalar(hid[v][:, I1:I2], hid[v][:, I1:I2], 7.0, -7.0, ALU.min, ALU.max).then_inc(s["lin"], 1)
                        for v in range(V):
                            dve.wait_ge(s_in[v], landed)
                        nc.vector.tensor_tensor(own[:, 0, :], xt[:, :, D + 1], expert[:, bass.ds(i * V, V)], ALU.is_equal).then_inc(s["second"], 1)
                        dve.wait_ge(s["second"], it)
                        nc.vector.tensor_scalar(own[:, 1, :], own[:, 0, :], float(TILES * P), None, ALU.mult)
                        nc.vector.tensor_tensor(own[:, 3, :], own[:, 0, :], xt[:, :, D + 3], ALU.mult).then_inc(s["own"], 1)
                        dve.wait_ge(s["own"], own1)
                        nc.vector.tensor_tensor(own[:, 1, :], own[:, 1, :], xt[:, :, D], ALU.add).then_inc(s["own"], 1)
                        dve.wait_ge(s["yw"], n[V - 1])
                        nc.vector.tensor_tensor(own[:, 2, :], own[:, 3, :], xt[:, :, D + 2], ALU.add)
                        dve.wait_ge(s["own"], own2)
                        nc.vector.tensor_tensor(own[:, 1, :], own[:, 1, :], surplus[:, bass.ds(i * V, V)], ALU.max).then_inc(s["own"], 1)
                        dve.wait_ge(s["own"], own3)
                        nc.vector.tensor_tensor(own[:, 1, :], own[:, 1, :], beside[:, bass.ds(i * V, V)], ALU.min).then_inc(s["own"], 1)
                        dve.wait_ge(s["own"], own4)
                        dve.wait_ge(s["sent"], it)
                        nc.vector.tensor_copy(dest[:, :], own[:, 1, :]).then_inc(s["dest"], 1)
                        for v in range(V):
                            dve.wait_ge(s["gs"], n[v])
                            dve.wait_ge(s["lin"], n[v])
                            nc.vector.scalar_tensor_tensor(hid[v][:, 0:I1], hid[v][:, I1:I2], 1.0, sg[v][:, :], ALU.add, ALU.mult).then_inc(s["a"], 1)
                        for v in range(V):
                            e = dve.value_load(meta[0:1, EXP, bass.ds(i * V + v, 1)], min_val=0, max_val=E - 1)
                            dve.wait_ge(s["y_ps"], n[v])
                            nc.vector.tensor_tensor(y[v][:, :].unsqueeze(1), ps[:, v, 3 * P:4 * P].unsqueeze(1), b2[:, bass.ds(e, 1), :], ALU.add).then_inc(s["y"], 1)

                @block.tensor
                def _(pe):
                    pe.wait_ge(s["weights"], 5 * 16)
                    pe.wait_ge(s["meta"], 4)
                    with pe.Fori(0, BT // V) as i:
                        n = [pe.snap(i * V + v + 1) for v in range(V)]
                        landed = pe.snap(i * 16 + 16)
                        for v in range(V):
                            pe.wait_ge(s["y"], n[v])
                            pe.wait_ge(s_in[v], landed)
                            nc.tensor.transpose(ps[:, v, 0:P], xt[:, v, 0:D], ident).then_inc(s["x_ps"], 1)
                        for v in range(V):
                            w1_at = pe.value_load(meta[0:1, W1AT, bass.ds(i * V + v, 1)], min_val=0, max_val=(E - 1) * I2)
                            pe.wait_ge(s["x_t"], n[v])
                            nc.tensor.matmul(ps[:, 4 + v, :], x_t[v][:, :], w1[:, bass.ds(w1_at, I2)], start=True, stop=True).then_inc(s["h_ps"], 1)
                        for v in range(V):
                            pe.wait_ge(s["a"], n[v])
                            for j in range(2):
                                last = nc.tensor.transpose(ps[:, v, (1 + j) * P:(2 + j) * P], hid[v][:, j * P:(j + 1) * P], ident)
                            last.then_inc(s["a_ps"], 1)
                        for v in range(V):
                            w2_at = pe.value_load(meta[0:1, W2AT, bass.ds(i * V + v, 1)], min_val=0, max_val=(E - 1) * 2)
                            pe.wait_ge(s["a_t"], n[v])
                            for j in range(2):
                                last = nc.tensor.matmul(ps[:, v, 3 * P:4 * P], act_t[v][:, j, :], w2[:, bass.ds(w2_at + j, 1), :],
                                                        start=(j == 0), stop=(j == 1))
                            last.then_inc(s["y_ps"], 1)

        with ExitStack() as sc:
            part = [[sb(f"part{u}{j}", [P, C, D], scope=sc) for j in range(2)] for u in range(U)]
            gates = [sb(f"gates{u}", [P, D], scope=sc) for u in range(U)]
            s_part = [sem(f"p5_part{u}") for u in range(U)]
            s_sum = sem("p5_sum")
            s_scaled = sem("p5_scaled")
            s_total = sem("p5_total")
            s_out = [sem(f"p5_out{u}") for u in range(U)]
            parts_v = parts.rearrange("(t p) d -> p t d", p=P)
            with nc.Block() as block:
                @block.sync
                def _(sp):
                    with sp.Fori(0, NI) as i:
                        for u in range(U):
                            sp.wait_ge(s_total, sp.snap(i * U + u + 1))
                            for j in range(2):
                                sp.dma_start(part[u][j][:, :, :], parts_v[:, bass.ds((i * U + u) * C + j * TILES, C), :]).then_inc(s_part[u], 16)
                            src = rows_dram[bass.ds(i * U + u, 1), 4 * D:5 * D].squeeze(0)
                            sp.dma_start(gates[u][:, :], src.partition_broadcast(P)).then_inc(s_part[u], 16)
                    for u in range(U):
                        sp.wait_ge(s_part[u], 3 * 16 * NI)

                @block.scalar
                def _(act):
                    with act.Fori(0, NI) as i:
                        for u in range(U):
                            act.wait_ge(s_total, act.snap(i * U + U + u + 1))
                            act.dma_start(out[bass.ds(i * U + u, 1)].rearrange("o (c p) d -> p (o c) d", p=P), x_tok[:, bass.ds((i * U + u) * C, C), :]).then_inc(s_out[u], 16)
                    for u in range(U):
                        act.wait_ge(s_out[u], 16 * NI)

                @block.vector
                def _(dve):
                    nc.vector.memset(part[0][0][:, 0, 0:1], 0.0).then_inc(s_total, U)
                    with dve.Fori(0, NI) as i:
                        n = [dve.snap(i * U + u + 1) for u in range(U)]
                        landed = dve.snap((i + 1) * 48)
                        for u in range(U):
                            dve.wait_ge(s_part[u], landed)
                            nc.vector.tensor_tensor(part[u][0][:, :, :], part[u][0][:, :, :], part[u][1][:, :, :], ALU.add).then_inc(s_sum, 1)
                        for u in range(U):
                            dve.wait_ge(s_sum, n[u])
                            nc.vector.tensor_tensor(part[u][1][:, :, :], part[u][0][:, :, :], gates[u][:, :].unsqueeze(1).to_broadcast([P, C, D]),
                                                    ALU.mult).then_inc(s_scaled, 1)
                        for u in range(U):
                            dve.wait_ge(s_scaled, n[u])
                            xs = x_tok[:, bass.ds((i * U + u) * C, C), :]
                            nc.vector.tensor_tensor(xs, xs, part[u][1][:, :, :], ALU.add).then_inc(s_total, 1)


def constants():
    import numpy as np
    q = np.arange(P)
    parts = dict(
        ident=np.eye(P),
        upto=q[:, None] <= q[None],
        before=q[:, None] < q[None],
        ones=np.ones((P, P)),
        group_of=q[:, None] // N == np.arange(R)[None],
        head_of=q[:, None] // HD == np.arange(H)[None],
        iota=np.broadcast_to(np.arange(E), (P, E)),
        token=q[:, None] + P * np.arange(16)[None],
        restart=np.broadcast_to(np.arange(128) % 16 > 0, (P, 128)),
        minus_half=np.full((P, 16), -0.5))
    return np.concatenate([parts[name] for name in CON], 1).astype(np.float32)


def layouts(i):
    import numpy as np

    def by_state(v):
        return v.reshape(G, R, N).transpose(1, 2, 0).reshape(P, G)

    mats = i["L0_attn_A"].reshape(G, R, N, N)
    w1, b1 = i["L1_ffn_mlp1_w"], i["L1_ffn_mlp1_b"]
    tiles = i["L0_attn_x"].shape[0] * C
    return dict(
        con=constants(),
        numbers=np.arange(-(-(2 * tiles + E - 1) // 4) * 4).astype(np.float32),
        x=i["L0_attn_x"],
        A=mats.transpose(1, 2, 0, 3), A_t=mats.transpose(1, 3, 0, 2),
        B_col=by_state(i["L0_attn_Bp"]), C_col=by_state(i["L0_attn_Cp"]), D_col=i["L0_attn_Dp"].reshape(G, R).T,
        Wg_t=i["L0_attn_Wg"].T, bg=i["L0_attn_bg"][:, None],
        gamma=i["L0_attn_gamma"], beta=i["L0_attn_beta"], bo=i["L1_attn_bo"][:, None],
        c_t=np.stack([i["L0_c"].T, i["L1_c"].T], 1), wmod=np.stack([i["L0_wmod"], i["L1_wmod"]], 1),
        gw0=i["L0_ffn_gate_w"], gb0=i["L0_ffn_gate_b"], ew0=i["L0_ffn_expert_w"].transpose(1, 0, 2), eb0=i["L0_ffn_expert_b"],
        Wqkv_t=np.concatenate([i["L1_attn_Wq"].T, i["L1_attn_Wk"].T, i["L1_attn_Wv"].T], 1),
        bqkv=np.concatenate([i["L1_attn_bq"], i["L1_attn_bk"], i["L1_attn_bv"]]), Wo_t=i["L1_attn_Wo"].T,
        ns=i["L1_ffn_norm_scale"], gw1=i["L1_ffn_gate_w"], gb1=i["L1_ffn_gate_b"],
        w1=np.concatenate([w1[:, :, 0::2], w1[:, :, 1::2]], 2).transpose(1, 0, 2),
        b1=np.concatenate([b1[:, 0::2], b1[:, 1::2]], 1),
        w2=i["L1_ffn_mlp2_w"].reshape(E, 2, P, D).transpose(2, 0, 1, 3), b2=i["L1_ffn_mlp2_b"])


def kernel(**inputs):
    import numpy as np
    import concourse.bacc as bacc
    from concourse.bass_utils import run_bass_kernel_spmd

    nc = bacc.Bacc("TRN2", target_bir_lowering=False, num_devices=1)
    arrays, args = {}, {}
    for name, v in layouts({n: np.asarray(v) for n, v in inputs.items()}).items():
        arrays[f"in_{name}_dram"] = np.ascontiguousarray(v)
        args[name] = nc.dram_tensor(f"in_{name}_dram", v.shape, mybir.dt.from_np(v.dtype), kind="ExternalInput").ap()
    shape = inputs["L0_attn_x"].shape
    out = nc.dram_tensor("out_0_dram", shape, F32, kind="ExternalOutput").ap()
    build(nc, args, out)
    r = run_bass_kernel_spmd(nc, [arrays], core_ids=[0])
    return r.results[0]["out_0_dram"]
```

```python
from contextlib import ExitStack

import concourse.bass as bass
from concourse import mybir
from concourse.alu_op_type import AluOpType as ALU

F32 = mybir.dt.float32
BF16 = mybir.dt.bfloat16
I32 = mybir.dt.int32
U32 = mybir.dt.uint32
ACT = mybir.ActivationFunctionType
AX = mybir.AxisListType

P = 128
D = 128
C = 4
N = 16
R = 8
G = D // R
H = 16
HD = D // H
E = 8
I2 = 512
U = 4
EPS = 1e-5
LEVELS = 7
NOWHERE = 1e6
CON = {}
for _name, _width in (("ident", P), ("upto", P), ("before", P), ("ones", P), ("group_of", R), ("head_of", H), ("iota", E), ("powers", E), ("token", 16), ("restart", 128), ("minus_half", 16)):
    CON[_name] = (sum(w for _, w in CON.values()), _width)
CON_W = sum(w for _, w in CON.values())
ROWS = ("ga_gamma", "ga_beta", "cb1", "sb1", "gb1")


def build(nc, a, out):
    B = a["x"].shape[0]
    NI = B // U
    TILES = B * C
    rows_dram = nc.dram_tensor("rows_dram", [B, len(ROWS) * D], F32).ap()
    taps_dram = nc.dram_tensor("taps_dram", [D, 2 * P], F32)

    ctx = ExitStack()
    names_used = []
    with ctx:
        def sb(name, shape, dt=F32, scope=ctx):
            names_used.append(name)
            return scope.enter_context(nc.sbuf_tensor(f"{name}_{len(names_used)}", shape, dt))

        phase_sems = []
        passed = nc.alloc_semaphore(name="passed")

        def sem(name):
            phase_sems.append(nc.alloc_semaphore(name=name))
            return phase_sems[-1]

        def hold(eng, semaphore, value, i=None):
            eng.wait_ge(semaphore, value)
            eng.sem_inc(passed, 1)

        def end_phase():
            nc.all_engine_barrier()
            nc.clear_and_free_semaphores(phase_sems)
            nc.all_engine_barrier()
            phase_sems.clear()

        ps = ctx.enter_context(nc.psum_tensor("ps", [P, 8, 512], F32))
        con = sb("con", [P, CON_W])

        def k(name, parts=P):
            at, width = CON[name]
            return con[0:parts, at:at + width]

        ident = k("ident")

        def ps3(j):
            return ps[:, 3 * j:3 * j + 3, :].rearrange("p k n -> p (k n)")
        x_tok = sb("x_tok", [P, TILES, D])
        xg = sb("xg", [P, D, TILES])
        mod_t = sb("mod_t", [P, 9, B])
        SA0, CA0, SB0, CB0, GB0, SA1, CA1, GA1, GA_BO = range(9)

        ssm = ExitStack()
        states_of = sb("states_of", [P, G, 3, P], scope=ssm)
        TO_STATE, TO_OUT, CARRY = range(3)
        wg = sb("wg", [P, D], scope=ssm)
        bg = sb("bg", [P, 1], scope=ssm)
        with ExitStack() as sc:
            power = sb("power", [P, G, 2 * P], scope=sc)
            power_t = sb("power_t", [P, G, 2 * P], scope=sc)
            wout, vin = power[:, :, P:2 * P], power_t[:, :, P:2 * P]
            a1t = sb("a1t", [P, G, P], scope=sc)
            bcol = sb("bcol", [P, G], scope=sc)
            ccol = sb("ccol", [P, G], scope=sc)
            dcol = sb("dcol", [R, G], scope=sc)
            cbd = sb("cbd", [P, G, R], scope=sc)
            taps = sb("taps", [R, G, 2 * P], scope=sc)
            c_t = sb("c_t", [P, 2, B], scope=sc)
            sg_t = sb("sg_t", [P, 2, B], scope=sc)
            wmod = sb("wmod", [P, 2, 6 * D], scope=sc)
            vecs = sb("vecs", [B, 2, D], scope=sc)
            bo = sb("bo", [P, 1], scope=sc)
            ga0 = sb("ga0", [B, D], scope=sc)
            rowv = sb("rowv", [B, len(ROWS), D], scope=sc)
            sign = sb("sign", [P, 2 * D + 2 * B], scope=sc)
            s_x = [sem(f"s_x{j}") for j in range(2)]
            s_con = sem("s_con")
            s_zero = sem("s_zero")
            s_zero_t = sem("s_zero_t")
            s_a = sem("s_a")
            s_c = sem("s_c")
            s_par = sem("s_par")
            s_sig = sem("s_sig")
            s_silu = sem("s_silu")
            s_mod = sem("s_mod")
            s_modT = sem("s_modT")
            s_modv = sem("s_modv")
            s_rows = sem("s_rows")
            s_rout = sem("s_rout")
            s_seed = sem("s_seed")
            s_sqt = sem("s_sqt")
            s_sqtc = sem("s_sqtc")
            s_a1 = sem("s_a1")
            s_sqc = sem("s_sqc")
            s_fin = sem("s_fin")
            s_fint = sem("s_fint")
            s_tap = sem("s_tap")
            s_dv = sem("s_dv")
            s_tout = sem("s_tout")
            with nc.Block() as block:
                @block.sync
                def _(sp):
                    sp.dma_start(con[:, :], a["con"]).then_inc(s_con, 16)
                    sp.dma_start(c_t[:, :, :], a["c_t"]).then_inc(s_c, 16)
                    sp.dma_start(wmod[:, :, :], a["wmod"]).then_inc(s_c, 16)
                    sp.wait_ge(s_zero, 1)
                    with nc.allow_non_contiguous_dma(reason="small state matrices"):
                        for r in range(R):
                            d0 = slice(16 * r, 16 * r + 16)
                            sp.dma_start(power[d0, :, d0], a["A"][r]).then_inc(s_a, 16)
                    sp.dma_start(bcol[:, :], a["B_col"]).then_inc(s_par, 16)
                    sp.dma_start(ccol[:, :], a["C_col"]).then_inc(s_par, 16)
                    sp.dma_start(dcol[:, :], a["D_col"]).then_inc(s_par, 16)
                    sp.dma_start(wg[:, :], a["Wg_t"]).then_inc(s_par, 16)
                    sp.dma_start(bg[:, :], a["bg"]).then_inc(s_par, 16)
                    sp.dma_start(bo[:, :], a["bo"]).then_inc(s_par, 16)
                    for j, name in enumerate(("gamma", "beta")):
                        sp.dma_start(vecs[:, j, :], a[name].partition_broadcast(B)).then_inc(s_par, 16)
                    for j in range(2):
                        h0 = slice(j * B // 2, (j + 1) * B // 2)
                        sp.dma_start(x_tok[:, j * TILES // 2:(j + 1) * TILES // 2, :],
                                     a["x"][h0].rearrange("b (c p) d -> p (b c) d", p=P)).then_inc(s_x[j], 16)
                    sp.wait_ge(s_rows, 1)
                    sp.dma_start(rows_dram, rowv[:, :, :].rearrange("b j d -> b (j d)")).then_inc(s_rout, 16)
                    sp.wait_ge(s_tap, 2)
                    sp.dma_start(taps_dram.ap().rearrange("(g r) t -> r g t", r=R), taps[:, :, :]).then_inc(s_tout, 16)
                    sp.wait_ge(s_par, 8 * 16)
                    sp.wait_ge(s_x[0], 16)
                    sp.wait_ge(s_x[1], 16)
                    sp.wait_ge(s_rout, 16)
                    sp.wait_ge(s_tout, 16)

                @block.gpsimd
                def _(pool):
                    nc.gpsimd.memset(power_t[:, :, 0:P], 0.0).then_inc(s_zero_t, 1)
                    nc.gpsimd.memset(taps[:, :, :], 0.0).then_inc(s_zero_t, 1)

                @block.vector
                def _(dve):
                    nc.vector.memset(power[:, :, 0:P], 0.0).then_inc(s_zero, 1)
                    dve.wait_ge(s_sig, 1)
                    nc.vector.tensor_tensor(sg_t[:, :, :], c_t[:, :, :], sg_t[:, :, :], ALU.mult).then_inc(s_silu, 1)
                    n = [0]

                    def link(ins):
                        n[0] += 1
                        ins.then_inc(s_dv, 1)
                        dve.wait_ge(s_dv, n[0])
                    dve.wait_ge(s_modv, 2)
                    dve.wait_ge(s_par, 8 * 16)
                    gates = [(ga0[:, :], sign[0:B, 0:D]), (rowv[:, 4, :], sign[0:B, D:2 * D]),
                             (mod_t[:, GB0, :], sign[:, 2 * D:2 * D + B]), (mod_t[:, GA1, :], sign[:, 2 * D + B:2 * D + 2 * B])]
                    for g, sg in gates:
                        last = nc.vector.tensor_scalar(sg, g, 0.0, 2.0, ALU.is_ge, ALU.mult)
                    link(last)
                    for g, sg in gates:
                        nc.vector.tensor_scalar(sg, sg, -1.0, None, ALU.add)
                        last = nc.vector.scalar_tensor_tensor(g, g, -1.0, g, ALU.mult, ALU.max)
                    link(last)
                    for g, sg in gates:
                        last = nc.vector.tensor_scalar(g, g, 0.25, None, ALU.max)
                    link(last)
                    for g, sg in gates:
                        last = nc.vector.tensor_tensor(g, g, sg, ALU.mult)
                    link(last)
                    nc.vector.tensor_scalar(mod_t[:, GA_BO, :], mod_t[:, GA1, :], bo[:, :], None, ALU.mult)
                    nc.vector.tensor_tensor(rowv[:, 0, :], ga0[:, :], vecs[:, 0, :], ALU.mult)
                    nc.vector.tensor_tensor(rowv[:, 1, :], ga0[:, :], vecs[:, 1, :], ALU.mult).then_inc(s_rows, 1)
                    nc.vector.tensor_tensor(cbd[:, :, :], ccol[:, :].unsqueeze(2).to_broadcast([P, G, R]),
                                            k("group_of").unsqueeze(1).to_broadcast([P, G, R]), ALU.mult)
                    nc.vector.tensor_copy(power_t[:, :, P:P + 1], bcol[:, :].unsqueeze(2))
                    nc.vector.tensor_copy(power[:, :, P:P + 1], ccol[:, :].unsqueeze(2)).then_inc(s_seed, 1)
                    dve.wait_ge(s_zero_t, 2)
                    dve.wait_ge(s_a, 2 * R * 16)
                    nc.vector.tensor_copy(a1t[:, :, :], power_t[:, :, 0:P]).then_inc(s_a1, 1)
                    dve.wait_ge(s_a1, 1)
                    for lv in range(LEVELS):
                        m = 1 << lv
                        for q in range(4):
                            dve.wait_ge(s_sqt, 4 * lv + q + 1)
                            gs, b0 = slice(4 * q, 4 * q + 4), 4 * (q % 2) + 2
                            src = ps[:, b0:b0 + 2, :].rearrange("p b (g n) -> p b g n", g=2)
                            if lv < LEVELS - 1:
                                nc.vector.tensor_copy(power_t[:, gs, 0:P].rearrange("p (b g) n -> p b g n", b=2), src[:, :, :, 0:P])
                            nc.vector.tensor_copy(power_t[:, gs, P + m:P + 2 * m].rearrange("p (b g) n -> p b g n", b=2),
                                                  src[:, :, :, P:P + m]).then_inc(s_sqtc, 1)
                    for q in range(4):
                        dve.wait_ge(s_fin, q + 1)
                        nc.vector.tensor_copy(states_of[:, 4 * q:4 * q + 4, TO_OUT, :],
                                              ps[:, q, :].rearrange("p (g m) -> p g m", m=P)).then_inc(s_fint, 1)
                    dve.wait_ge(s_fin, 12)
                    link(nc.vector.tensor_copy(taps[:, :, P:2 * P].rearrange("r (k g) m -> r k g m", k=4),
                                               ps[0:R, 4:8, :].rearrange("r k (g m) -> r k g m", m=P)))
                    nc.vector.tensor_tensor(taps[:, :, P:P + 1], taps[:, :, P:P + 1], dcol[:, :].unsqueeze(2), ALU.add).then_inc(s_tap, 1)
                    dve.wait_ge(s_tap, 1)
                    nc.vector.tensor_scalar(taps[:, :, P:P + 1], taps[:, :, P:P + 1], 1.0, None, ALU.add).then_inc(s_tap, 1)

                @block.scalar
                def _(act):
                    act.wait_ge(s_zero_t, 1)
                    with nc.allow_non_contiguous_dma(reason="small state matrices"):
                        for r in range(R):
                            d0 = slice(16 * r, 16 * r + 16)
                            act.dma_start(power_t[d0, :, d0], a["A_t"][r]).then_inc(s_a, 16)
                    act.wait_ge(s_c, 32)
                    nc.scalar.activation(sg_t[:, :, :], c_t[:, :, :], ACT.Sigmoid).then_inc(s_sig, 1)
                    act.wait_ge(s_modT, 1)
                    for j in range(8):
                        last = nc.scalar.activation(mod_t[:, j, :], ps[:, 4, 16 * j:16 * j + B], ACT.Copy,
                                                    bias=float(j in (CA0, CB0, CA1)))
                    last.then_inc(s_modv, 1)
                    act.wait_ge(s_mod, 2)
                    nc.scalar.activation(ga0[:, :], ps[0:B, 0, 0:D], ACT.Copy)
                    nc.scalar.activation(rowv[:, 3, :], ps[0:B, 1, 0:D], ACT.Copy)
                    nc.scalar.activation(rowv[:, 2, :], ps[0:B, 1, D:2 * D], ACT.Copy, bias=1.0)
                    nc.scalar.activation(rowv[:, 4, :], ps[0:B, 1, 2 * D:3 * D], ACT.Copy).then_inc(s_modv, 1)
                    for lv in range(LEVELS):
                        m = 1 << lv
                        for q in range(4):
                            act.wait_ge(s_sqt, 4 * lv + q + 1)
                            gs, b0 = slice(4 * q, 4 * q + 4), 4 * (q % 2)
                            src = ps[:, b0:b0 + 2, :].rearrange("p b (g n) -> p b g n", g=2)
                            dst = states_of[:, gs, CARRY, :] if lv == LEVELS - 1 else power[:, gs, 0:P]
                            nc.scalar.activation(dst.rearrange("p (b g) n -> p b g n", b=2), src[:, :, :, 0:P], ACT.Copy)
                            nc.scalar.activation(power[:, gs, P + m:P + 2 * m].rearrange("p (b g) n -> p b g n", b=2),
                                                 src[:, :, :, P:P + m], ACT.Copy).then_inc(s_sqc, 1)
                    for q in range(4):
                        act.wait_ge(s_fin, 5 + q)
                        nc.scalar.activation(states_of[:, 4 * q:4 * q + 4, TO_STATE, :],
                                             ps[:, 4 + q, :].rearrange("p (g m) -> p g m", m=P), ACT.Copy).then_inc(s_sqc, 1)

                @block.tensor
                def _(pe):
                    pe.wait_ge(s_silu, 1)
                    for j, (l, part) in enumerate(((0, 0), (0, 1), (0, 3), (0, 4), (0, 5), (1, 0), (1, 1), (1, 2))):
                        last = nc.tensor.matmul(ps[:, 4, 16 * j:16 * j + B], wmod[:, l, part * D:(part + 1) * D],
                                                sg_t[:, l, :], start=True, stop=True)
                    last.then_inc(s_modT, 1)
                    nc.tensor.matmul(ps[0:B, 0, 0:D], sg_t[:, 0, :], wmod[:, 0, 2 * D:3 * D], start=True, stop=True).then_inc(s_mod, 1)
                    nc.tensor.matmul(ps[0:B, 1, 0:3 * D], sg_t[:, 1, :], wmod[:, 1, 3 * D:6 * D], start=True, stop=True).then_inc(s_mod, 1)
                    pe.wait_ge(s_con, 16)
                    pe.wait_ge(s_seed, 1)
                    pe.wait_ge(s_modv, 2)
                    pe.wait_ge(s_a1, 1)
                    for lv in range(LEVELS):
                        m = 1 << lv
                        for q in range(4):
                            done = 4 * lv + q - 1
                            if done > 0:
                                pe.wait_ge(s_sqc, done)
                                pe.wait_ge(s_sqtc, done)
                            for g in range(4 * q, 4 * q + 4):
                                bank, at = 4 * (q % 2) + (g % 4) // 2, (g % 2) * 256
                                nc.tensor.matmul(ps[:, bank, at:at + P + m], power_t[:, g, 0:P], power[:, g, 0:P + m], start=True, stop=True)
                            for g in range(4 * q, 4 * q + 4):
                                bank, at = 4 * (q % 2) + 2 + (g % 4) // 2, (g % 2) * 256
                                lo = 0 if lv < LEVELS - 1 else P
                                last = nc.tensor.matmul(ps[:, bank, at + lo:at + P + m], power[:, g, 0:P], power_t[:, g, lo:P + m], start=True, stop=True)
                            last.then_inc(s_sqt, 1)
                    pe.wait_ge(s_sqtc, 4 * LEVELS)
                    pe.wait_ge(s_sqc, 4 * LEVELS)
                    for g in range(G):
                        last = nc.tensor.matmul(ps[:, g // 4, (g % 4) * P:(g % 4 + 1) * P], a1t[:, g, :], wout[:, g, :],
                                                start=True, stop=True)
                        if g % 4 == 3:
                            last.then_inc(s_fin, 1)
                    for g in range(G):
                        last = nc.tensor.transpose(ps[:, 4 + g // 4, (g % 4) * P:(g % 4 + 1) * P], vin[:, g, :], ident)
                        if g % 4 == 3:
                            last.then_inc(s_fin, 1)
                    for q in range(4):
                        pe.wait_ge(s_sqc, 4 * LEVELS + q + 1)
                        for g in range(4 * q, 4 * q + 4):
                            last = nc.tensor.matmul(ps[0:R, 4 + q, (g % 4) * P:(g % 4 + 1) * P], cbd[:, g, :], vin[:, g, :],
                                                    start=True, stop=True)
                        last.then_inc(s_fin, 1)

        with ExitStack() as sc:
            st = sb("st", [P, U, C, 6], scope=sc)
            mv = sb("mv", [P, U, C, 2], scope=sc)
            rstd = sb("rstd", [P, U * C], scope=sc)
            nrm = [sb(f"nrm{u}", [P, C, D], scope=sc) for u in range(U)]
            h_t = [sb(f"h_t{u}", [P, C * P], scope=sc) for u in range(U)]
            sig = [sb(f"sig{u}", [P, C * P], scope=sc) for u in range(U)]
            xr_t = [sb(f"xr_t{u}", [P, C * P], scope=sc) for u in range(U)]
            s_st = sem("p1_stats")
            s_mv = sem("p1_mean_var")
            s_ve = sem("p1_var_eps")
            s_rs = sem("p1_rstd")
            s_n = sem("p1_normed")
            s_nt = sem("p1_transposed")
            s_h = sem("p1_modulated")
            s_gm = sem("p1_gate_product")
            s_gs = sem("p1_gate")
            s_xr = sem("p1_gated")
            s_xt = sem("p1_back")
            s_w = sem("p1_written")
            with nc.Block() as block:
                @block.vector
                def _(dve):
                    with dve.Fori(0, NI) as i:
                        n = [dve.snap(i * U + u + 1) for u in range(U)]
                        it = dve.snap(i + 1)
                        for u in range(U):
                            for c in range(C):
                                last = nc.vector.bn_stats(st[:, u, c, :], x_tok[:, bass.ds((i * U + u) * C + c, 1), :].squeeze(1))
                        last.then_inc(s_st, 1)
                        hold(dve, s_st, it)
                        for u in range(U):
                            for c in range(C):
                                last = nc.vector.bn_aggr(mv[:, u, c, :], st[:, u, c, :])
                        last.then_inc(s_mv, 1)
                        dve.wait_ge(s_rs, it)
                        for u in range(U):
                            for c in range(C):
                                last = nc.vector.tensor_scalar(nrm[u][:, c, :], x_tok[:, bass.ds((i * U + u) * C + c, 1), :].squeeze(1),
                                                               mv[:, u, c, 0:1], rstd[:, u * C + c:u * C + c + 1],
                                                               ALU.subtract, ALU.mult)
                            last.then_inc(s_n, 1)
                        for u in range(U):
                            dve.wait_ge(s_gs, n[u])
                            nc.vector.tensor_tensor(xr_t[u][:, :].rearrange("p (c t) -> p c t", c=C)[:, :, ::-1],
                                                    h_t[u][:, :].rearrange("p (c t) -> p c t", c=C),
                                                    sig[u][:, :].rearrange("p (c t) -> p c t", c=C), ALU.mult).then_inc(s_xr, 1)
                        for u in range(U):
                            dve.wait_ge(s_xt, n[u])
                            nc.vector.tensor_copy(xg[:, :, bass.ds((i * U + u) * C, C)].rearrange("p d c -> p c d"),
                                                  ps[:, u, :].rearrange("p (c d) -> p c d", c=C)).then_inc(s_w, 1)

                @block.gpsimd
                def _(pool):
                    with pool.Fori(0, NI) as i:
                        it = pool.snap(i + 1)
                        hold(pool, s_mv, it)
                        nc.gpsimd.tensor_scalar(rstd[:, :], mv[:, :, :, 1].rearrange("p u c -> p (u c)"), EPS, None, ALU.add).then_inc(s_ve, 1)
                        pool.wait_ge(s_ve, it)
                        nc.gpsimd.tensor_tensor(rstd[:, :], rstd[:, :], k("minus_half"), ALU.pow).then_inc(s_rs, 1)

                @block.scalar
                def _(act):
                    with act.Fori(0, NI) as i:
                        n = [act.snap(i * U + u + 1) for u in range(U)]
                        for u in range(U):
                            act.wait_ge(s_nt, n[u])
                            b = i * U + u
                            nc.scalar.activation(h_t[u][:, :], ps[:, u, :], ACT.Identity,
                                                 bias=mod_t[:, SA0, bass.ds(b, 1)], scale=mod_t[:, CA0, bass.ds(b, 1)]).then_inc(s_h, 1)
                        for u in range(U):
                            act.wait_ge(s_gm, n[u])
                            nc.scalar.activation(sig[u][:, :], ps[:, 4 + u, :], ACT.Sigmoid, bias=bg[:, :]).then_inc(s_gs, 1)

                @block.tensor
                def _(pe):
                    with pe.Fori(0, NI) as i:
                        n = [pe.snap(i * U + u + 1) for u in range(U)]
                        for u in range(U):
                            pe.wait_ge(s_n, n[u])
                            for c in range(C):
                                last = nc.tensor.transpose(ps[:, u, c * P:(c + 1) * P], nrm[u][:, c, :], ident)
                            last.then_inc(s_nt, 1)
                        for u in range(U):
                            pe.wait_ge(s_h, n[u])
                            nc.tensor.matmul(ps[:, 4 + u, :], wg[:, :], h_t[u][:, :], start=True, stop=True).then_inc(s_gm, 1)
                        for u in range(U):
                            pe.wait_ge(s_xr, n[u])
                            for c in range(C):
                                last = nc.tensor.transpose(ps[:, u, c * P:(c + 1) * P], xr_t[u][:, c * P:(c + 1) * P], ident)
                            last.then_inc(s_xt, 1)

        with ExitStack() as sc:
            TS = B * C
            toep = [sb(f"toep{u}", [P, R, P], scope=sc) for u in range(U)]
            mats = [sb(f"mats{u}", [P, 3, P], scope=sc) for u in range(U)]
            ends = [sb(f"ends{u}", [P, TS], scope=sc) for u in range(U)]
            endm = [sb(f"endm{u}", [P, R, TS], scope=sc) for u in range(U)]
            carry = [sb(f"carry{u}", [P, R, TS], scope=sc) for u in range(U)]
            s_toep = [sem(f"p2_toep{u}") for u in range(U)]
            s_m = sem("p2_matrices")
            s_e = sem("p2_end_products")
            s_em = sem("p2_ends_masked")
            s_er = sem("p2_ends")
            s_c1 = sem("p2_carry_product")
            s_c2 = sem("p2_carried")
            s_cb = sem("p2_carry_spread")
            s_y = sem("p2_outputs")
            s_yc = sem("p2_outputs_kept")
            s_z = sem("p2_cleared")

            def by_chunk(ap, c):
                return ap.rearrange("p (b c) -> p b c", c=C)[:, :, c]

            with nc.Block() as block:
                @block.sync
                def _(sp):
                    with sp.Fori(0, G // U) as i:
                        for u in range(U):
                            sp.wait_ge(s_yc, sp.snap(i * U + u + 1))
                            src = bass.AP(taps_dram, (i * U + u) * (R * 2 * P) + 1, [[1, P], [2 * P, R], [1, P]])
                            sp.dma_start(toep[u][:, :, :], src).then_inc(s_toep[u], 16)
                    for u in range(U):
                        sp.wait_ge(s_toep[u], 16 * (G // U))

                @block.scalar
                def _(act):
                    with act.Fori(0, G // U) as i:
                        n = [act.snap(i * U + u + 1) for u in range(U)]
                        for u in range(U):
                            act.wait_ge(s_yc, n[u])
                            nc.scalar.activation(mats[u][:, :, :].unsqueeze(1), states_of[:, bass.ds(i * U + u, 1), :, :], ACT.Copy).then_inc(s_m, 1)

                @block.vector
                def _(dve):
                    for u in range(U):
                        last = nc.vector.memset(carry[u][:, :, :], 0.0)
                    last.then_inc(s_z, 1)
                    last = nc.vector.memset(ends[0][:, :], 0.0)
                    last.then_inc(s_yc, U)
                    dve.wait_ge(s_yc, U)
                    nc.vector.memset(ends[0][:, :], 0.0).then_inc(s_cb, U)
                    with dve.Fori(0, G // U) as i:
                        n = [dve.snap(i * U + u + 1) for u in range(U)]
                        n5 = [dve.snap(i * U + u + 1 + U) for u in range(U)]
                        c1 = [[dve.snap(i * (2 * U) + j * U + u + 1) for u in range(U)] for j in range(2)]
                        for u in range(U):
                            dve.wait_ge(s_e, n[u])
                            nc.vector.tensor_tensor(endm[u][:, :, :], ps[:, u, 0:R * TS].rearrange("p (r t) -> p r t", r=R),
                                                    k("group_of").unsqueeze(2).to_broadcast([P, R, TS]), ALU.mult).then_inc(s_em, 1)
                        for u in range(U):
                            dve.wait_ge(s_em, n[u])
                            nc.vector.tensor_reduce(ends[u][:, :], endm[u][:, :, :].rearrange("p r t -> p t r"), AX.X, ALU.add).then_inc(s_er, 1)
                        for j in range(2):
                            for u in range(U):
                                dve.wait_ge(s_c1, c1[j][u])
                                nc.vector.tensor_tensor(by_chunk(ends[u][:, :], j + 1), by_chunk(ends[u][:, :], j + 1), ps[:, u, j * B:(j + 1) * B],
                                                        ALU.add).then_inc(s_c2, 1)
                        for u in range(U):
                            dve.wait_ge(s_c2, c1[1][u])
                            for c in range(1, C):
                                src = by_chunk(ends[u][:, :], c - 1)
                                last = nc.vector.tensor_tensor(
                                    carry[u][:, :, :].rearrange("p r (b c) -> p r b c", c=C)[:, :, :, c],
                                    src.unsqueeze(1).to_broadcast([P, R, B]),
                                    k("group_of").unsqueeze(2).to_broadcast([P, R, B]), ALU.mult)
                            last.then_inc(s_cb, 1)
                        for u in range(U):
                            dve.wait_ge(s_y, n[u])
                            nc.vector.tensor_copy(xg[:, bass.ds((i * U + u) * R, R), :], ps[:, 4 + u, 0:R * TS].rearrange("p (r t) -> p r t", r=R)).then_inc(s_yc, 1)

                @block.tensor
                def _(pe):
                    pe.wait_ge(s_z, 1)
                    with pe.Fori(0, G // U) as i:
                        n = [pe.snap(i * U + u + 1) for u in range(U)]
                        n5 = [pe.snap(i * U + u + 1 + U) for u in range(U)]
                        c2 = [[pe.snap(i * (2 * U) + j * U + u + 1) for u in range(U)] for j in range(2)]
                        tp = pe.snap((i + 1) * 16)
                        for u in range(U):
                            pe.wait_ge(s_m, n[u])
                            pe.wait_ge(s_yc, n[u])
                            nc.tensor.matmul(ps[:, u, 0:R * TS], mats[u][:, TO_STATE, :],
                                             xg[:, bass.ds((i * U + u) * R, R), :], start=True, stop=True).then_inc(s_e, 1)
                        for j in range(2):
                            for u in range(U):
                                if j == 0:
                                    pe.wait_ge(s_er, n[u])
                                else:
                                    pe.wait_ge(s_c2, c2[0][u])
                                nc.tensor.matmul(ps[:, u, j * B:(j + 1) * B], mats[u][:, CARRY, :], by_chunk(ends[u][:, :], j),
                                                 start=True, stop=True).then_inc(s_c1, 1)
                        for u in range(U):
                            pe.wait_ge(s_cb, n5[u])
                            pe.wait_ge(s_toep[u], tp)
                            nc.tensor.matmul(ps[:, 4 + u, 0:R * TS], mats[u][:, TO_OUT, :], carry[u][:, :, :], start=True, stop=False)
                            for r in range(R):
                                last = nc.tensor.matmul(ps[:, 4 + u, r * TS:(r + 1) * TS], toep[u][:, r, :],
                                                        xg[:, bass.ds((i * U + u) * R + r, 1), :], start=False, stop=(r == R - 1))
                            last.then_inc(s_y, 1)
        ssm.close()
        end_phase()

        mean_x = sb("mean_x", [P, TILES])
        rstd_x = sb("rstd_x", [P, TILES])
        NT = U * C
        with ExitStack() as sc:
            st = sb("st", [P, 2, NT, 6], scope=sc)
            mv = sb("mv", [P, NT, 2], scope=sc)
            mv2 = sb("mv2", [P, NT, 2], scope=sc)
            var_eps = sb("var_eps", [P, NT], scope=sc)
            rstd = sb("rstd", [P, NT], scope=sc)
            shift = sb("shift", [P, NT], scope=sc)
            nrm = [sb(f"nrm{u}", [P, C, D], scope=sc) for u in range(U)]
            rows = [sb(f"rows{u}", [P, 2, D], scope=sc) for u in range(U)]
            names = ("y_stats", "y_mv", "y_ve", "y_rs", "shift", "normed", "gamma", "beta", "added", "x_stats", "x_mv", "x_ve", "x_rs")
            s = {nm: sem(f"join_{nm}") for nm in names}
            s_rows = [sem(f"join_rows{u}") for u in range(U)]

            def value(eng, i, per, k):
                return i * per + k if isinstance(i, int) else eng.snap(i * per + k)

            def tiles(ap, i, many):
                return ap[:, i * NT:i * NT + many] if isinstance(i, int) else ap[:, bass.ds(i * NT, many)]

            def tile_of(ap, i, t):
                return ap[:, i * NT + t] if isinstance(i, int) else ap[:, bass.ds(i * NT + t, 1)].squeeze(1)

            def seq_of(i, u):
                return x_tok[:, (i * U + u) * C:(i * U + u + 1) * C, :] if isinstance(i, int) else x_tok[:, bass.ds((i * U + u) * C, C), :]

            with nc.Block() as block:
                @block.sync
                def _(sp):
                    def load(i, u):
                        src = rows_dram[i * U + u:i * U + u + 1, 0:2 * D] if isinstance(i, int) else rows_dram[bass.ds(i * U + u, 1), 0:2 * D]
                        sp.dma_start(rows[u][:, :, :], src.rearrange("o (j d) -> (o j) d", d=D).partition_broadcast(P)).then_inc(s_rows[u], 16)
                    for u in range(U):
                        load(0, u)
                    with sp.Fori(1, NI) as i:
                        for u in range(U):
                            sp.wait_ge(s["beta"], value(sp, i, U, u + 1 - U))
                            sp.wait_ge(s["gamma"], value(sp, i, U, u + 1 - U))
                            load(i, u)
                    for u in range(U):
                        sp.wait_ge(s_rows[u], 16 * NI)

                @block.gpsimd
                def _(pool):
                    def body(i):
                        for u in range(U):
                            hold(pool, s_rows[u], value(pool, i, 16, 16))
                            nc.gpsimd.tensor_tensor(seq_of(i, u), seq_of(i, u), rows[u][:, 1:2, :].to_broadcast([P, C, D]), ALU.add).then_inc(s["beta"], 1)
                        hold(pool, s["y_mv"], value(pool, i, 1, 1))
                        nc.gpsimd.tensor_scalar(rstd[:, :], mv[:, :, 1], EPS, None, ALU.add).then_inc(s["y_ve"], 1)
                        pool.wait_ge(s["y_ve"], value(pool, i, 1, 1))
                        nc.gpsimd.tensor_tensor(rstd[:, :], rstd[:, :], k("minus_half"), ALU.pow).then_inc(s["y_rs"], 1)

                    def finish(i):
                        hold(pool, s["x_ve"], value(pool, i, 1, 1))
                        nc.gpsimd.tensor_tensor(tiles(rstd_x, i, NT), var_eps[:, :], k("minus_half"), ALU.pow).then_inc(s["x_rs"], 1)
                    body(0)
                    with pool.Fori(1, NI) as i:
                        body(i)
                        finish(i - 1)
                    finish(NI - 1)

                @block.scalar
                def _(act):
                    def body(i, first=False):
                        for u in range(U):
                            if not first:
                                act.wait_ge(s["added"], value(act, i, U, u + 1 - U))
                            hold(act, s["shift"], value(act, i, 1, 1))
                            for c in range(C):
                                t = u * C + c
                                last = nc.scalar.activation(nrm[u][:, c, :], xg[:, :, i * NT + t] if first else xg[:, :, bass.ds(i * NT + t, 1)].squeeze(2),
                                                            ACT.Identity, bias=shift[:, t:t + 1], scale=rstd[:, t:t + 1])
                            last.then_inc(s["normed"], 1)
                    body(0, first=True)
                    with act.Fori(1, NI) as i:
                        body(i)

                @block.vector
                def _(dve):
                    def stats_y(i):
                        for t in range(NT):
                            src = xg[:, :, i * NT + t] if isinstance(i, int) else xg[:, :, bass.ds(i * NT + t, 1)].squeeze(2)
                            last = nc.vector.bn_stats(st[:, 0, t, :], src)
                        last.then_inc(s["y_stats"], 1)
                        if not (isinstance(i, int) and i == 0):
                            dve.wait_ge(s["normed"], value(dve, i, U, 0))
                        hold(dve, s["y_stats"], value(dve, i, 1, 1))
                        for t in range(NT):
                            last = nc.vector.bn_aggr(mv[:, t, :], st[:, 0, t, :])
                        last.then_inc(s["y_mv"], 1)

                    def shift_y(i):
                        dve.wait_ge(s["y_rs"], value(dve, i, 1, 1))
                        nc.vector.scalar_tensor_tensor(shift[:, :], mv[:, :, 0], -1.0, rstd[:, :], ALU.mult, ALU.mult).then_inc(s["shift"], 1)

                    def join(i):
                        for u in range(U):
                            dve.wait_ge(s["normed"], value(dve, i, U, u + 1))
                            dve.wait_ge(s_rows[u], value(dve, i, 16, 16))
                            nc.vector.tensor_tensor(nrm[u][:, :, :], nrm[u][:, :, :], rows[u][:, 0:1, :].to_broadcast([P, C, D]), ALU.mult).then_inc(s["gamma"], 1)
                        for u in range(U):
                            dve.wait_ge(s["gamma"], value(dve, i, U, u + 1))
                            dve.wait_ge(s["beta"], value(dve, i, U, u + 1))
                            nc.vector.tensor_tensor(seq_of(i, u), seq_of(i, u), nrm[u][:, :, :], ALU.add).then_inc(s["added"], 1)

                    def stats_x(i, more=True):
                        for u in range(U):
                            hold(dve, s["added"], value(dve, i, U, u + 1))
                            for c in range(C):
                                last = nc.vector.bn_stats(st[:, 1, u * C + c, :], tile_of(x_tok, i, u * C + c))
                        last.then_inc(s["x_stats"], 1)
                        hold(dve, s["x_stats"], value(dve, i, 1, 1))
                        for t in range(NT):
                            last = nc.vector.bn_aggr(mv2[:, t, :], st[:, 1, t, :])
                        last.then_inc(s["x_mv"], 1)
                        dve.wait_ge(s["x_mv"], value(dve, i, 1, 1))
                        nc.vector.tensor_copy(tiles(mean_x, i, NT), mv2[:, :, 0])
                        if more:
                            dve.wait_ge(s["x_rs"], value(dve, i, 1, 0))
                        nc.vector.tensor_scalar(var_eps[:, :], mv2[:, :, 1], EPS, None, ALU.add).then_inc(s["x_ve"], 1)
                    stats_y(0)
                    shift_y(0)
                    join(0)
                    stats_y(1)
                    shift_y(1)
                    stats_x(0, more=False)
                    with dve.Fori(2, NI) as i:
                        join(i - 1)
                        stats_y(i)
                        shift_y(i)
                        stats_x(i - 1)
                    join(NI - 1)
                    stats_x(NI - 1)

        end_phase()

        QK = 2 * D
        VE = HD + 1
        PAY = D + 4
        CAP = B * C * P + P
        rows_of = nc.dram_tensor("rows_of", [E * CAP, PAY], F32).ap()
        room = xg[:, :, :].rearrange("p d t -> p (d t)") if D * TILES >= 2 * E * I2 else sb("room", [P, 2 * E * I2])
        w1, b1 = room[:, 0:E * I2], room[:, E * I2:2 * E * I2]
        base = sb("base", [P, E])
        far = sb("far", [P, PAY])
        with ExitStack() as sc:
            wqkv = sb("wqkv", [P, 3 * D], scope=sc)
            wo = sb("wo", [P, D], scope=sc)
            ew0 = sb("ew0", [P, E, D], scope=sc)
            eb0 = sb("eb0", [E, D], scope=sc)
            gw = sb("gw", [P, 2, E], scope=sc)
            gb = sb("gb", [P, 2, E], scope=sc)
            bqkv = sb("bqkv", [P, 3 * D], scope=sc)
            scale_ms = sb("scale_ms", [P, D], scope=sc)
            pick = sb("pick", [E, E, P], BF16, scope=sc)
            rows = [sb(f"rows{u}", [P, 3, D], scope=sc) for u in range(U)]
            st = sb("st", [P, NT, 6], scope=sc)
            mv = sb("mv", [P, NT, 2], scope=sc)
            rstd = sb("rstd", [P, NT], scope=sc)
            nrm = [sb(f"nrm{u}", [P, C, D], scope=sc) for u in range(U)]
            f_t = [sb(f"f_t{u}", [P, C * P], scope=sc) for u in range(U)]
            qk = [sb(f"qk{u}", [P, C, QK], scope=sc) for u in range(U)]
            ex_room = [sb(f"ex{u}", [P, C * QK], scope=sc) for u in range(U)]
            lg_room = [sb(f"lg{u}", [P, C * QK], scope=sc) for u in range(U)]
            ex = [r[:, :].rearrange("p (c d) -> p c d", c=C) for r in ex_room]
            lg = [r[:, :].rearrange("p (c d) -> p c d", c=C) for r in lg_room]
            q_t = [r[:, 0:C * P] for r in ex_room]
            pay = [r[:, 0:C * PAY].rearrange("p (c d) -> p c d", c=C) for r in ex_room]
            hot_t = [r[0:E, 0:C * P] for r in lg_room]
            red = [r[:, 0:C * VE * H].rearrange("p (c e h) -> p c e h", c=C, e=VE) for r in lg_room]
            v1 = [sb(f"v1{u}", [P, C, VE, H], scope=sc) for u in range(U)]
            kv = [sb(f"kv{j}", [P, HD, D], scope=sc) for j in range(2)]
            qc = [sb(f"qc{j}", [P, VE * D], scope=sc) for j in range(2)]
            ds = [sb(f"ds{u}", [P, VE, H], scope=sc) for u in range(U)]
            skv = [sb(f"skv{u}", [P, VE, H], scope=sc) for u in range(U)]
            rden = sb("rden", [P, NT, H], scope=sc)
            masked = [sb(f"masked{u}", [P, C * P], scope=sc) for u in range(U)]
            logit = sb("logit", [P, NT, E], scope=sc)
            top = sb("top", [P, NT, 8], scope=sc)
            idx = sb("idx", [P, NT, 8], U32, scope=sc)
            idf = sb("idf", [P, 2, NT], scope=sc)
            hot = sb("hot", [P, 2, NT, E], scope=sc)
            both = sb("both", [P, NT, E], scope=sc)
            hot_b = [sb(f"hot_b{u}", [E, C * P], BF16, scope=sc) for u in range(U)]
            place = sb("place", [P, NT], scope=sc)
            wts = sb("wts", [P, 4, NT], scope=sc)
            tot = sb("tot", [P, E, NT], scope=sc)
            run = sb("run", [P, E, NT], scope=sc)
            rank = sb("rank", [P, NT, E], scope=sc)
            sel = sb("sel", [P, NT, E], scope=sc)
            pos = sb("pos", [P, 2, NT], scope=sc)
            posu = sb("posu", [P, 2, NT], U32, scope=sc)

            names = ("weights", "init", "sent", "st", "mv", "ve", "rs", "normed", "turned", "feat",
                     "lg_ps", "lg", "max", "idx", "idf", "hot", "hot_ps", "hot_t", "hot_b", "spread", "masked", "moe", "moe_t",
                     "moe_ps", "x2", "qkv_ps", "qkv", "v", "abs", "exp", "ln", "relu", "u1", "cor", "qk", "q_ps", "q_t", "kv",
                     "tri", "qc", "red", "ds_ps", "ds", "skv", "so_ps", "state_in", "rden", "att", "att_ps", "att_t", "wo", "wo_t",
                     "wo_ps", "x3", "cb", "h4", "sq", "sm", "r4", "pay", "pay_ps", "pay_t", "gx", "x4", "ed", "ee", "e1", "p1",
                     "both", "rank_ps", "tot", "run", "excl", "r1", "r2", "sel", "pos", "posu", "extra", "base", "scat", "place", "place2", "pads", "experts", "padrow")
            s = {nm: sem(f"p3_{nm}") for nm in names}
            s_rows = [sem(f"p3_rows{u}") for u in range(U)]
            counts = sb("counts", [P, E], I32, scope=sc)
            sent = sb("sent", [P, 1], scope=sc)

            class At:
                def __init__(self, eng, i):
                    self.eng, self.i, self.made = eng, i, {}

                def __call__(self, per, k):
                    if (per, k) not in self.made:
                        self.made[per, k] = self.eng.snap(self.i * per + k)
                    return self.made[per, k]

            def col(ap, i, u):
                return ap[:, bass.ds(i * U + u, 1)]

            def tile(i, u, c):
                return x_tok[:, bass.ds((i * U + u) * C + c, 1), :].squeeze(1)

            def seq(i, u):
                return x_tok[:, bass.ds((i * U + u) * C, C), :]

            with nc.Block() as block:
                @block.sync
                def _(sp):
                    sp.dma_start(wqkv[:, :], a["Wqkv_t"]).then_inc(s["weights"], 16)
                    sp.dma_start(wo[:, :], a["Wo_t"]).then_inc(s["weights"], 16)
                    sp.dma_start(ew0[:, :, :], a["ew0"]).then_inc(s["weights"], 16)
                    sp.dma_start(eb0[:, :], a["eb0"]).then_inc(s["weights"], 16)
                    for l in range(2):
                        sp.dma_start(gw[:, l, :], a[f"gw{l}"]).then_inc(s["weights"], 16)
                        sp.dma_start(gb[:, l, :], a[f"gb{l}"].partition_broadcast(P)).then_inc(s["weights"], 16)
                    sp.dma_start(bqkv[:, :], a["bqkv"].partition_broadcast(P)).then_inc(s["weights"], 16)
                    sp.dma_start(scale_ms[:, :], a["ns"].partition_broadcast(P)).then_inc(s["weights"], 16)
                    def load(src, u):
                        sp.dma_start(rows[u][:, :, :], src.rearrange("o (j d) -> (o j) d", d=D).partition_broadcast(P)).then_inc(s_rows[u], 16)
                    for u in range(U):
                        load(rows_dram[u:u + 1, 2 * D:5 * D], u)
                    sp.dma_start(w1, a["w1"].rearrange("p e i -> p (e i)")).then_inc(s["experts"], 16)
                    sp.dma_start(b1, a["b1"].rearrange("e i -> (e i)").partition_broadcast(P)).then_inc(s["experts"], 16)
                    with sp.Fori(1, NI) as i:
                        for u in range(U):
                            sp.wait_ge(s["gx"], sp.snap(i * U + (u + 1 - U)))
                            load(rows_dram[bass.ds(i * U + u, 1), 2 * D:5 * D], u)
                    for u in range(U):
                        sp.wait_ge(s_rows[u], 16 * NI)
                    sp.wait_ge(s["place"], 1)
                    for e in range(E):
                        row = sp.value_load(counts[0:1, e:e + 1], min_val=e * CAP, max_val=(e + 1) * CAP - P)
                        sp.dma_start(rows_of[bass.ds(row, P), :], far[:, :]).then_inc(s["pads"], 16)
                    sp.wait_ge(s["pads"], 16 * E)
                    sp.wait_ge(s["experts"], 32)

                @block.gpsimd
                def _(pool):
                    with pool.Fori(0, NI) as i:
                        at = At(pool, i)

                        def rsqrt(nth):
                            hold(pool, s["mv"], at(2, nth + 1))
                            nc.gpsimd.tensor_scalar(rstd[:, :], mv[:, :, 1], EPS, None, ALU.add).then_inc(s["ve"], 1)
                            pool.wait_ge(s["ve"], at(2, nth + 1))
                            nc.gpsimd.tensor_tensor(rstd[:, :], rstd[:, :], k("minus_half"), ALU.pow).then_inc(s["rs"], 1)

                        rsqrt(0)
                        for u in range(U):
                            pool.wait_ge(s["u1"], at(U, u + 1))
                            nc.gpsimd.tensor_tensor(lg[u][:, :, :], ex[u][:, :, :], lg[u][:, :, :], ALU.subtract).then_inc(s["cor"], 1)
                        for c in range(C):
                            for u in range(U):
                                j = (c * U + u) % 2
                                t = c * U + u
                                if t >= 2:
                                    pool.wait_ge(s["tri"], at(NT, t - 1))
                                if c == 0:
                                    pool.wait_ge(s["qk"], at(U, u + 1))
                                k_in = qk[u][:, c, D:QK].rearrange("p (h d) -> p h d", h=H).unsqueeze(1).to_broadcast([P, HD, H, HD])
                                v_in = v1[u][:, c, 0:HD, :].unsqueeze(3).to_broadcast([P, HD, H, HD])
                                nc.gpsimd.tensor_tensor(kv[j][:, :, :].rearrange("p e (h d) -> p e h d", h=H), k_in, v_in, ALU.mult).then_inc(s["kv"], 1)
                        rsqrt(1)
                        for u in range(U):
                            pool.wait_ge(s["cb"], at(U, u + 1))
                            nc.gpsimd.tensor_tensor(nrm[u][:, :, :], nrm[u][:, :, :], rows[u][:, 1:2, :].to_broadcast([P, C, D]), ALU.add).then_inc(s["h4"], 1)
                        hold(pool, s["sq"], at(1, 1))
                        nc.gpsimd.tensor_scalar(rstd[:, :], rstd[:, :], 1.0 / D, EPS, ALU.mult, ALU.add).then_inc(s["sm"], 1)
                        pool.wait_ge(s["sm"], at(1, 1))
                        nc.gpsimd.tensor_tensor(rstd[:, :], rstd[:, :], k("minus_half"), ALU.pow).then_inc(s["r4"], 1)
                        for u in range(U):
                            hold(pool, s["gx"], at(U, u + 1))
                            nc.gpsimd.tensor_tensor(seq(i, u), seq(i, u), masked[u][:, :].rearrange("p (c d) -> p c d", c=C), ALU.add).then_inc(s["x4"], 1)
                        pool.wait_ge(s["posu"], at(1, 1))
                        hold(pool, s["extra"], at(1, 1))
                        for t in range(NT):
                            for slot in range(2):
                                nc.gpsimd.indirect_dma_start(
                                    rows_of, bass.IndirectOffsetOnAxis(ap=posu[:, slot, t:t + 1], axis=0),
                                    pay[t // C][:, t % C, :], None).then_inc(s["scat"], 16)
                        hold(pool, s["scat"], at(16 * 2 * NT, 16 * 2 * NT))
                        nc.gpsimd.tensor_tensor(sent[:, :], k("ones")[:, 0:1], k("ones")[:, 0:1], ALU.mult).then_inc(s["sent"], 1)

                @block.scalar
                def _(act):
                    with act.Fori(0, NI) as i:
                        at = At(act, i)

                        def feat(nth, bias, scale):
                            for u in range(U):
                                act.wait_ge(s["turned"], at(2 * U, nth * U + u + 1))
                                nc.scalar.activation(f_t[u][:, :], ps[:, u, :], ACT.Identity, bias=col(mod_t[:, bias, :], i, u),
                                                     scale=col(mod_t[:, scale, :], i, u)).then_inc(s["feat"], 1)
                        feat(0, SB0, CB0)
                        for u in range(U):
                            act.wait_ge(s["hot_t"], at(U, u + 1))
                            nc.scalar.activation(hot_b[u][:, :], hot_t[u][:, :], ACT.Copy).then_inc(s["hot_b"], 1)
                        for u in range(U):
                            act.wait_ge(s["moe"], at(U, u + 1))
                            nc.scalar.activation(masked[u][:, :], ps[:, u, :], ACT.Copy, scale=col(mod_t[:, GB0, :], i, u)).then_inc(s["moe_t"], 1)
                        feat(1, SA1, CA1)
                        for u in range(U):
                            if u == 0:
                                act.wait_ge(s["sent"], at(1, 1))
                            act.wait_ge(s["qkv"], at(U, u + 1))
                            nc.scalar.activation(ex[u][:, :, :], qk[u][:, :, :], ACT.Abs).then_inc(s["abs"], 1)
                        for u in range(U):
                            act.wait_ge(s["abs"], at(U, u + 1))
                            nc.scalar.activation(ex[u][:, :, :], ex[u][:, :, :], ACT.Exp, scale=-1.0).then_inc(s["exp"], 1)
                        for u in range(U):
                            act.wait_ge(s["exp"], at(U, u + 1))
                            nc.scalar.activation(lg[u][:, :, :], ex[u][:, :, :], ACT.Ln, bias=1.0).then_inc(s["ln"], 1)
                        for u in range(U):
                            act.wait_ge(s["q_ps"], at(U, u + 1))
                            nc.scalar.activation(q_t[u][:, :], ps[:, u, :], ACT.Copy).then_inc(s["q_t"], 1)
                        for u in range(U):
                            act.wait_ge(s["att_ps"], at(U, u + 1))
                            nc.scalar.activation(f_t[u][:, :], ps[:, u, :], ACT.Copy).then_inc(s["att_t"], 1)
                        for u in range(U):
                            act.wait_ge(s["wo"], at(U, u + 1))
                            nc.scalar.activation(masked[u][:, :], ps[:, 4 + u, :], ACT.Identity, bias=col(mod_t[:, GA_BO, :], i, u),
                                                 scale=col(mod_t[:, GA1, :], i, u)).then_inc(s["wo_t"], 1)
                        for u in range(U):
                            act.wait_ge(s["h4"], at(U, u + 1))
                            for c in range(C):
                                last = nc.scalar.activation(masked[u][:, c * P:(c + 1) * P], nrm[u][:, c, :], ACT.Square,
                                                            accum_out=rstd[:, u * C + c:u * C + c + 1])
                        last.then_inc(s["sq"], 1)
                        for u in range(U):
                            act.wait_ge(s["pay_ps"], at(U, u + 1))
                            nc.scalar.activation(f_t[u][:, :], ps[:, u, :], ACT.Copy).then_inc(s["pay_t"], 1)
                        act.wait_ge(s["ed"], at(1, 1))
                        nc.scalar.activation(wts[:, 1, :], wts[:, 0, :], ACT.Exp).then_inc(s["ee"], 1)

                @block.vector
                def _(dve):
                    dve.wait_ge(s["weights"], 10 * 16)
                    last = nc.vector.tensor_copy(pick[:, :, :], k("ident", E)[:, 0:E].unsqueeze(2).to_broadcast([E, E, P]))
                    for u in range(U):
                        nc.vector.memset(v1[u][:, :, HD:VE, :], 1.0)
                    nc.vector.memset(far[:, :], 0.0).then_inc(s["padrow"], 1)
                    dve.wait_ge(s["padrow"], 1)
                    nc.vector.memset(far[:, D:D + 1], NOWHERE)
                    nc.vector.memset(far[:, D + 1:D + 2], -1.0).then_inc(s["padrow"], 1)
                    nc.vector.tensor_scalar(base[:, :], k("iota"), float(CAP), None, ALU.mult)
                    nc.vector.tensor_copy(place[:, :], k("token")).then_inc(s["init"], 1)
                    nc.vector.memset(ds[0][:, :, :], 0.0).then_inc(s["sent"], 1)
                    with dve.Fori(0, NI) as i:
                        at = At(dve, i)

                        def stats(nth, tiles, ready):
                            for u in range(U):
                                ready(u)
                                for c in range(C):
                                    last = nc.vector.bn_stats(st[:, u * C + c, :], tiles(u, c))
                            last.then_inc(s["st"], 1)
                            hold(dve, s["st"], at(2, nth + 1))
                            for t in range(NT):
                                last = nc.vector.bn_aggr(mv[:, t, :], st[:, t, :])
                            last.then_inc(s["mv"], 1)
                            dve.wait_ge(s["rs"], at(2, nth + 1))
                            for u in range(U):
                                for c in range(C):
                                    t = u * C + c
                                    last = nc.vector.tensor_scalar(nrm[u][:, c, :], tiles(u, c), mv[:, t, 0:1], rstd[:, t:t + 1],
                                                                   ALU.subtract, ALU.mult)
                                last.then_inc(s["normed"], 1)

                        for u in range(U):
                            for c in range(C):
                                tt = (i * U + u) * C + c
                                last = nc.vector.tensor_scalar(nrm[u][:, c, :], tile(i, u, c), mean_x[:, bass.ds(tt, 1)], rstd_x[:, bass.ds(tt, 1)],
                                                               ALU.subtract, ALU.mult)
                            last.then_inc(s["normed"], 1)

                        def best(nth, bias):
                            dve.wait_ge(s["lg_ps"], at(2, nth + 1))
                            nc.vector.tensor_tensor(logit[:, :, :], ps[:, 4, 0:NT * E].rearrange("p (t e) -> p t e", e=E),
                                                    bias.to_broadcast([P, NT, E]), ALU.add).then_inc(s["lg"], 1)
                            hold(dve, s["lg"], at(2, nth + 1))
                            for t in range(NT):
                                last = nc.vector.max(top[:, t, :], logit[:, t, :])
                            last.then_inc(s["max"], 1)
                            hold(dve, s["max"], at(2, nth + 1))
                            for t in range(NT):
                                last = nc.vector.max_index(idx[:, t, :], top[:, t, :], logit[:, t, :])
                            last.then_inc(s["idx"], 1)
                            dve.wait_ge(s["idx"], at(2, nth + 1))
                            nc.vector.tensor_copy(idf[:, :, :], idx[:, :, 0:2].rearrange("p t j -> p j t")).then_inc(s["idf"], 1)
                            dve.wait_ge(s["idf"], at(2, nth + 1))
                            for j in range(1 + nth):
                                last = nc.vector.tensor_tensor(hot[:, j, :, :], k("iota").unsqueeze(1).to_broadcast([P, NT, E]),
                                                               idf[:, j, :].unsqueeze(2).to_broadcast([P, NT, E]), ALU.is_equal)
                            last.then_inc(s["hot"], 1)

                        best(0, gb[:, 0:1, :])
                        for u in range(U):
                            dve.wait_ge(s["hot_ps"], at(U, u + 1))
                            nc.vector.tensor_copy(hot_t[u][:, :], ps[0:E, 4 + u, :]).then_inc(s["hot_t"], 1)
                        for e in range(E):
                            for u in range(U):
                                dve.wait_ge(s["spread"], at(E * U, e * U + u + 1))
                                nc.vector.tensor_tensor(masked[u][:, :], f_t[u][:, :], ps[:, 4 + u, :], ALU.mult).then_inc(s["masked"], 1)
                        for u in range(U):
                            dve.wait_ge(s["moe_ps"], at(U, u + 1))
                            nc.vector.tensor_tensor(seq(i, u), seq(i, u), ps[:, 4 + u, :].rearrange("p (c d) -> p c d", c=C), ALU.add).then_inc(s["x2"], 1)
                        stats(0, lambda u, c: tile(i, u, c), lambda u: hold(dve, s["x2"], at(U, u + 1)))

                        for u in range(U):
                            dve.wait_ge(s["qkv_ps"], at(U, u + 1))
                            bank = 4 * (u % 2)
                            nc.vector.tensor_tensor(qk[u][:, :, :], ps[:, bank:bank + C, 0:QK],
                                                    bqkv[:, 0:QK].unsqueeze(1).to_broadcast([P, C, QK]), ALU.add).then_inc(s["qkv"], 1)
                            for c in range(C):
                                last = nc.vector.tensor_tensor(v1[u][:, c, 0:HD, :].rearrange("p e h -> p h e"),
                                                        ps[:, bank + c, QK:3 * D].rearrange("p (h e) -> p h e", h=H),
                                                        bqkv[:, QK:3 * D].rearrange("p (h e) -> p h e", h=H), ALU.add)
                            last.then_inc(s["v"], 1)
                        for u in range(U):
                            dve.wait_ge(s["ln"], at(U, u + 1))
                            nc.vector.scalar_tensor_tensor(qk[u][:, :, :], qk[u][:, :, :], 0.0, lg[u][:, :, :], ALU.max, ALU.add).then_inc(s["relu"], 1)
                            dve.wait_ge(s["relu"], at(U, u + 1))
                            nc.vector.tensor_scalar(lg[u][:, :, :], ex[u][:, :, :], 1.0, -1.0, ALU.add, ALU.add).then_inc(s["u1"], 1)
                        for u in range(U):
                            dve.wait_ge(s["cor"], at(U, u + 1))
                            nc.vector.tensor_tensor(qk[u][:, :, :], qk[u][:, :, :], lg[u][:, :, :], ALU.add).then_inc(s["qk"], 1)
                        for c in range(C):
                            for u in range(U):
                                t = c * U + u
                                j = t % 2
                                dve.wait_ge(s["tri"], at(NT, t + 1))
                                q_in = qk[u][:, c, 0:D].unsqueeze(1).to_broadcast([P, VE, D])
                                nc.vector.tensor_tensor(qc[j][:, :].rearrange("p (e d) -> p e d", d=D),
                                                        ps3(j)[:, 0:VE * D].rearrange("p (e d) -> p e d", d=D), q_in, ALU.mult).then_inc(s["qc"], 1)
                                dve.wait_ge(s["qc"], at(NT, t + 1))
                                nc.vector.tensor_reduce(red[u][:, c, :, :].rearrange("p e h -> p (e h)"),
                                                        qc[j][:, :].rearrange("p (g d) -> p g d", d=HD), AX.X, ALU.add).then_inc(s["red"], 1)
                                if c < C - 1:
                                    dve.wait_ge(s["ds_ps"], at((C - 1) * U, t + 1))
                                    mask = k("head_of").unsqueeze(1).to_broadcast([P, VE, H])
                                    dst = skv[u] if c == 0 else ds[u]
                                    nc.vector.tensor_tensor(dst[:, :, :], ps[:, 6, 0:VE * H].rearrange("p (e h) -> p e h", h=H), mask, ALU.mult).then_inc(s["ds"], 1)
                                if c:
                                    dve.wait_ge(s["so_ps"], at((C - 1) * U, t - U + 1))
                                    dve.wait_ge(s["red"], at(NT, t + 1))
                                    nc.vector.tensor_tensor(red[u][:, c, :, :].rearrange("p e h -> p (e h)"), red[u][:, c, :, :].rearrange("p e h -> p (e h)"),
                                                            ps[:, 7, 0:VE * H], ALU.add).then_inc(s["state_in"], 1)
                                if 0 < c < C - 1:
                                    dve.wait_ge(s["ds"], at((C - 1) * U, t + 1))
                                    nc.vector.tensor_tensor(skv[u][:, :, :], skv[u][:, :, :], ds[u][:, :, :], ALU.add).then_inc(s["skv"], 1)
                        for u in range(U):
                            dve.wait_ge(s["red"], at(NT, NT))
                            dve.wait_ge(s["state_in"], at((C - 1) * U, (C - 1) * U))
                            nc.vector.reciprocal(rden[:, u * C:(u + 1) * C, :], red[u][:, :, HD, :]).then_inc(s["rden"], 1)
                        for u in range(U):
                            dve.wait_ge(s["rden"], at(U, u + 1))
                            for c in range(C):
                                last = nc.vector.tensor_tensor(nrm[u][:, c, :].rearrange("p (h e) -> p h e", h=H),
                                                        red[u][:, c, 0:HD, :].rearrange("p e h -> p h e"),
                                                        rden[:, u * C + c, :].unsqueeze(2).to_broadcast([P, H, HD]), ALU.mult)
                            last.then_inc(s["att"], 1)
                        for u in range(U):
                            dve.wait_ge(s["wo_ps"], at(U, u + 1))
                            nc.vector.tensor_tensor(seq(i, u), seq(i, u), ps[:, u, :].rearrange("p (c d) -> p c d", c=C), ALU.add).then_inc(s["x3"], 1)
                        stats(1, lambda u, c: tile(i, u, c), lambda u: hold(dve, s["x3"], at(U, u + 1)))
                        for u in range(U):
                            dve.wait_ge(s_rows[u], at(16, 16))
                            dve.wait_ge(s["normed"], at(3 * U, 2 * U + u + 1))
                            nc.vector.tensor_tensor(nrm[u][:, :, :], nrm[u][:, :, :], rows[u][:, 0:1, :].to_broadcast([P, C, D]), ALU.mult).then_inc(s["cb"], 1)
                        dve.wait_ge(s["r4"], at(1, 1))
                        for u in range(U):
                            for c in range(C):
                                last = nc.vector.scalar_tensor_tensor(pay[u][:, c, 0:D], nrm[u][:, c, :], rstd[:, u * C + c:u * C + c + 1],
                                                                      scale_ms[:, :], ALU.mult, ALU.mult)
                            last.then_inc(s["pay"], 1)
                        for u in range(U):
                            nc.vector.tensor_tensor(masked[u][:, :].rearrange("p (c d) -> p c d", c=C), nrm[u][:, :, :],
                                                    rows[u][:, 2:3, :].to_broadcast([P, C, D]), ALU.mult).then_inc(s["gx"], 1)
                        best(1, gb[:, 1:2, :])
                        nc.vector.tensor_tensor(wts[:, 0, :], top[:, :, 1], top[:, :, 0], ALU.subtract).then_inc(s["ed"], 1)
                        dve.wait_ge(s["hot"], at(2, 2))
                        nc.vector.tensor_tensor(both[:, :, :], hot[:, 0, :, :], hot[:, 1, :, :], ALU.add).then_inc(s["both"], 1)
                        dve.wait_ge(s["ee"], at(1, 1))
                        nc.vector.tensor_scalar(wts[:, 2, :], wts[:, 1, :], 1.0, None, ALU.add).then_inc(s["e1"], 1)
                        dve.wait_ge(s["e1"], at(1, 1))
                        nc.vector.reciprocal(wts[:, 3, :], wts[:, 2, :]).then_inc(s["p1"], 1)
                        dve.wait_ge(s["rank_ps"], at(1, 1))
                        nc.vector.tensor_copy(tot[:, :, :], ps[:, 6, 0:NT * E].rearrange("p (t e) -> p e t", e=E)).then_inc(s["tot"], 1)
                        dve.wait_ge(s["p1"], at(1, 1))
                        for u in range(U):
                            ts = slice(u * C, (u + 1) * C)
                            nc.vector.tensor_copy(pay[u][:, :, D:D + 1], place[:, ts].unsqueeze(2))
                            nc.vector.tensor_copy(pay[u][:, :, D + 1:D + 2], idf[:, 1, ts].unsqueeze(2))
                            nc.vector.tensor_copy(pay[u][:, :, D + 2:D + 3], wts[:, 3, ts].unsqueeze(2))
                            last = nc.vector.scalar_tensor_tensor(pay[u][:, :, D + 3:D + 4], wts[:, 1, ts].unsqueeze(2), -1.0,
                                                                  wts[:, 3, ts].unsqueeze(2), ALU.add, ALU.mult)
                        last.then_inc(s["extra"], 1)
                        dve.wait_ge(s["tot"], at(1, 1))
                        nc.vector.tensor_tensor_scan(run[:, :, :].rearrange("p e t -> p (e t)"), k("restart"),
                                                     tot[:, :, :].rearrange("p e t -> p (e t)"), 0.0, ALU.mult, ALU.add).then_inc(s["run"], 1)
                        dve.wait_ge(s["run"], at(1, 1))
                        nc.vector.tensor_tensor(tot[:, :, :], run[:, :, :], tot[:, :, :], ALU.subtract).then_inc(s["excl"], 1)
                        dve.wait_ge(s["excl"], at(1, 1))
                        nc.vector.tensor_tensor(rank[:, :, :], ps[:, 5, 0:NT * E].rearrange("p (t e) -> p t e", e=E),
                                                tot[:, :, :].rearrange("p e t -> p t e"), ALU.add).then_inc(s["r1"], 1)
                        dve.wait_ge(s["r1"], at(1, 1))
                        nc.vector.tensor_tensor(rank[:, :, :], rank[:, :, :], base[:, :].unsqueeze(1).to_broadcast([P, NT, E]), ALU.add).then_inc(s["r2"], 1)
                        dve.wait_ge(s["r2"], at(1, 1))
                        nc.vector.tensor_tensor(base[:, :], base[:, :], run[:, :, NT - 1], ALU.add).then_inc(s["base"], 1)
                        for j in range(2):
                            nc.vector.tensor_tensor(sel[:, :, :], rank[:, :, :], hot[:, j, :, :], ALU.mult).then_inc(s["sel"], 1)
                            dve.wait_ge(s["sel"], at(2, j + 1))
                            nc.vector.tensor_reduce(pos[:, j, :], sel[:, :, :], AX.X, ALU.add).then_inc(s["pos"], 1)
                            dve.wait_ge(s["pos"], at(2, j + 1))
                        nc.vector.tensor_copy(posu[:, :, :], pos[:, :, :]).then_inc(s["posu"], 1)
                        nc.vector.tensor_scalar(place[:, :], place[:, :], float(NT * P), None, ALU.add).then_inc(s["place2"], 1)
                        dve.wait_ge(s["place2"], at(1, 1))
                        dve.wait_ge(s["base"], at(1, 1))
                        dve.wait_ge(s["x4"], at(U, U))
                        nc.vector.memset(ds[0][0:1, 0, 0:1], 0.0)
                    nc.vector.tensor_copy(counts[:, :], base[:, :]).then_inc(s["place"], 1)

                @block.tensor
                def _(pe):
                    pe.wait_ge(s["weights"], 10 * 16)
                    pe.wait_ge(s["init"], 1)
                    with pe.Fori(0, NI) as i:
                        at = At(pe, i)

                        def turn(src, u, bank):
                            for c in range(C):
                                last = nc.tensor.transpose(ps[:, bank, c * P:(c + 1) * P], src[u][:, c * P:(c + 1) * P], ident)
                            return last

                        def turn_tok(src, u, bank):
                            for c in range(C):
                                last = nc.tensor.transpose(ps[:, bank, c * P:(c + 1) * P], src[u][:, c, 0:D], ident)
                            return last

                        def logits(l):
                            for u in range(U):
                                pe.wait_ge(s["pay_t" if l else "feat"], at(U if l else 2 * U, u + 1))
                                for c in range(C):
                                    t = u * C + c
                                    last = nc.tensor.matmul(ps[:, 4, t * E:(t + 1) * E], f_t[u][:, c * P:(c + 1) * P], gw[:, l, :],
                                                            start=True, stop=True)
                            last.then_inc(s["lg_ps"], 1)

                        for u in range(U):
                            pe.wait_ge(s["normed"], at(3 * U, u + 1))
                            turn_tok(nrm, u, u).then_inc(s["turned"], 1)
                        logits(0)
                        pe.wait_ge(s["hot"], at(2, 1))
                        for u in range(U):
                            for c in range(C):
                                last = nc.tensor.transpose(ps[0:E, 4 + u, c * P:(c + 1) * P], hot[:, 0, u * C + c, :], ident)
                            last.then_inc(s["hot_ps"], 1)
                        for u in range(U):
                            pe.wait_ge(s["hot_t"], at(U, u + 1))
                            nc.tensor.matmul(ps[:, u, :], eb0[:, :], hot_t[u][:, :], start=True, stop=False)
                            pe.wait_ge(s["hot_b"], at(U, u + 1))
                            nc.tensor.matmul(ps[:, 4 + u, :], pick[:, 0, :], hot_b[u][:, :], start=True, stop=True).then_inc(s["spread"], 1)
                        for e in range(E):
                            for u in range(U):
                                pe.wait_ge(s["masked"], at(E * U, e * U + u + 1))
                                last = nc.tensor.matmul(ps[:, u, :], ew0[:, e, :], masked[u][:, :], start=False, stop=(e == E - 1))
                                if e < E - 1:
                                    nc.tensor.matmul(ps[:, 4 + u, :], pick[:, e + 1, :], hot_b[u][:, :], start=True, stop=True).then_inc(s["spread"], 1)
                                else:
                                    last.then_inc(s["moe"], 1)
                        for u in range(U):
                            pe.wait_ge(s["moe_t"], at(U, u + 1))
                            turn(masked, u, 4 + u).then_inc(s["moe_ps"], 1)
                        for u in range(U):
                            pe.wait_ge(s["normed"], at(3 * U, U + u + 1))
                            turn_tok(nrm, u, u).then_inc(s["turned"], 1)
                        for u in range(U):
                            bank = 4 * (u % 2)
                            pe.wait_ge(s["feat"], at(2 * U, U + u + 1))
                            if u == 0:
                                pe.wait_ge(s["feat"], at(2 * U, 2 * U))
                            if u >= 2:
                                pe.wait_ge(s["v"], at(U, u - 1))
                            for c in range(C):
                                last = nc.tensor.matmul(ps[:, bank + c, 0:3 * D], f_t[u][:, c * P:(c + 1) * P], wqkv[:, :], start=True, stop=True)
                            last.then_inc(s["qkv_ps"], 1)
                        for u in range(U):
                            pe.wait_ge(s["qk"], at(U, u + 1))
                            turn_tok(qk, u, u).then_inc(s["q_ps"], 1)
                        pe.wait_ge(s["q_t"], at(U, U))
                        for c in range(C):
                            for u in range(U):
                                t = c * U + u
                                j = t % 2
                                if t >= 2:
                                    pe.wait_ge(s["qc"], at(NT, t - 1))
                                pe.wait_ge(s["kv"], at(NT, t + 1))
                                for m in range(2):
                                    nc.tensor.matmul(ps[:, 3 * j + m, :], k("upto"), kv[j][:, 4 * m:4 * m + 4, :].rearrange("p e d -> p (e d)"),
                                                     start=True, stop=True)
                                nc.tensor.matmul(ps[:, 3 * j + 2, 0:D], k("upto"), qk[u][:, c, D:QK], start=True, stop=True).then_inc(s["tri"], 1)
                                if c < C - 1:
                                    pe.wait_ge(s["v"], at(U, u + 1))
                                    if t:
                                        pe.wait_ge(s["ds"], at((C - 1) * U, t))
                                    nc.tensor.matmul(ps[:, 6, 0:VE * H], qk[u][:, c, D:QK], v1[u][:, c, :, :].rearrange("p e h -> p (e h)"),
                                                     start=True, stop=True).then_inc(s["ds_ps"], 1)
                                if c:
                                    if c == 1:
                                        pe.wait_ge(s["ds"], at((C - 1) * U, u + 1))
                                    else:
                                        pe.wait_ge(s["skv"], at((C - 2) * U, (c - 2) * U + u + 1))
                                    if t > U:
                                        pe.wait_ge(s["state_in"], at((C - 1) * U, t - U))
                                    nc.tensor.matmul(ps[:, 7, 0:VE * H], q_t[u][:, c * P:(c + 1) * P], skv[u][:, :, :].rearrange("p e h -> p (e h)"),
                                                     start=True, stop=True).then_inc(s["so_ps"], 1)
                        for u in range(U):
                            pe.wait_ge(s["att"], at(U, u + 1))
                            turn_tok(nrm, u, u).then_inc(s["att_ps"], 1)
                        for u in range(U):
                            pe.wait_ge(s["att_t"], at(U, u + 1))
                            nc.tensor.matmul(ps[:, 4 + u, :], wo[:, :], f_t[u][:, :], start=True, stop=True).then_inc(s["wo"], 1)
                        for u in range(U):
                            pe.wait_ge(s["wo_t"], at(U, u + 1))
                            turn(masked, u, u).then_inc(s["wo_ps"], 1)
                        for u in range(U):
                            pe.wait_ge(s["pay"], at(U, u + 1))
                            turn_tok(pay, u, u).then_inc(s["pay_ps"], 1)
                        logits(1)
                        pe.wait_ge(s["both"], at(1, 1))
                        nc.tensor.matmul(ps[:, 5, 0:NT * E], k("before"), both[:, :, :].rearrange("p t e -> p (t e)"), start=True, stop=True)
                        nc.tensor.matmul(ps[:, 6, 0:NT * E], k("ones"), both[:, :, :].rearrange("p t e -> p (t e)"), start=True, stop=True).then_inc(s["rank_ps"], 1)

        end_phase()

        V = 8
        GT = 4
        BT = -(-(2 * TILES + E - 1) // V) * V
        NP = BT // V
        I1 = I2 // 2
        parts = nc.dram_tensor("parts", [(2 * TILES + BT) * P, D], F32).ap()
        with ExitStack() as sc:
            w2 = sb("w2", [P, E * 2 * D], scope=sc)
            b2 = sb("b2", [P, E * D], scope=sc)
            number = sb("number", [P, BT], scope=sc)
            cnt = sb("cnt", [P, E], scope=sc)
            cnti = sb("cnti", [P, E], I32, scope=sc)
            nti = sb("nti", [P, E], I32, scope=sc)
            ntile = sb("ntile", [P, E], scope=sc)
            upto = sb("upto_e", [P, E], scope=sc)
            first = sb("first", [P, E], scope=sc)
            step = sb("step", [P, E], scope=sc)
            last_tile = sb("last_tile", [P, 1], scope=sc)
            surplus = sb("surplus", [P, BT], scope=sc)
            beside = sb("beside", [P, BT], scope=sc)
            ge = sb("ge", [P, BT, E], scope=sc)
            gst = sb("gst", [P, BT, E], scope=sc)
            expert = sb("expert", [P, BT], scope=sc)
            row = sb("row", [P, BT], scope=sc)
            meta = sb("meta", [P, BT], I32, scope=sc)
            digits = sb("digits", [P, NP, V], scope=sc)
            packf = sb("packf", [P, NP], scope=sc)
            packs = sb("packs", [P, NP], I32, scope=sc)
            xt = sb("xt", [P, V, PAY], scope=sc)
            x_t = [sb(f"x_t{v}", [P, P], scope=sc) for v in range(V)]
            hid = [sb(f"hid{v}", [P, I2], scope=sc) for v in range(V)]
            glu = [h[:, 0:I1] for h in hid]
            lin = [h[:, I1:I2] for h in hid]
            act_t = [sb(f"act_t{v}", [P, I1], scope=sc) for v in range(V)]
            sg = [sb(f"sg{v}", [P, I1], scope=sc) for v in range(V)]
            yw = [sb(f"yw{v}", [P, D], scope=sc) for v in range(V)]
            own = sb("own", [P, 4, V], scope=sc)
            dest = sb("dest", [P, V], U32, scope=sc)
            names = ("weights", "plan", "meta", "x_ps", "x_t", "h_ps", "h", "glu", "lin", "sig", "gs", "a", "a_ps", "a_t",
                     "y_ps", "yw", "second", "own", "dest")
            s = {nm: sem(f"p4_{nm}") for nm in names}
            s_in = [sem(f"p4_rows{v}") for v in range(V)]
            s_out = [sem(f"p4_out{v}") for v in range(V)]

            def wait(eng, semaphore, value):
                eng.wait_ge(semaphore, value)

            class Tiles:
                def __init__(self, eng, i):
                    self.eng, self.i, self.made = eng, i, {}

                def value(self, per, k):
                    if isinstance(self.i, int):
                        return self.i * per + k
                    if (per, k) not in self.made:
                        self.made[per, k] = self.eng.snap(self.i * per + k)
                    return self.made[per, k]

                def exists(self, v):
                    return not isinstance(self.i, int) or 0 <= self.i * V + v < BT

                def done(self, name, v, alone=False):
                    if self.exists(v):
                        (hold if alone else wait)(self.eng, s[name], self.value(V, v + 1))

                def landed(self, sems, v, alone=False):
                    if self.exists(v):
                        (hold if alone else wait)(self.eng, sems[v % V], self.value(16, 16 * (v // V) + 16))

                def grouped(self, name, v, per=1, k=1):
                    if self.exists(v):
                        self.eng.wait_ge(s[name], self.value(per * V // GT, per * (v // GT) + k))

                def at(self, v, many=1):
                    return slice(self.i * V + v, self.i * V + v + many) if isinstance(self.i, int) else bass.ds(self.i * V + v, many)

                def row(self, v):
                    return self.eng.value_load(meta[0:1, self.at(v)], min_val=0, max_val=E * CAP - P)

                def experts(self, ahead=0):
                    i = self.i + ahead
                    at = slice(i, i + 1) if isinstance(i, int) else bass.ds(i, 1)
                    packed = self.eng.value_load(packs[0:1, at], min_val=0, max_val=E ** V - 1)
                    return [self.eng.snap((packed >> (3 * v)) & (E - 1), min_val=0, max_val=E - 1) for v in range(V)]

            def passes(eng, body, back=0):
                body(Tiles(eng, 0), range(V))
                with eng.Fori(1, NP - 1) as i:
                    body(Tiles(eng, i), range(V))
                body(Tiles(eng, NP - 1), range(V))
                body(Tiles(eng, NP), range(back))

            with nc.Block() as block:
                @block.sync
                def _(sp):
                    sp.dma_start(w2[:, :], a["w2"].rearrange("p e k d -> p (e k d)")).then_inc(s["weights"], 16)
                    sp.dma_start(b2[:, :], a["b2"].rearrange("e d -> (e d)").partition_broadcast(P)).then_inc(s["weights"], 16)
                    sp.dma_start(number[:, :], a["numbers"].partition_broadcast(P)).then_inc(s["weights"], 16)
                    sp.wait_ge(s["meta"], 1)

                    def body(t, steps):
                        for v in steps:
                            at = t.row(v)
                            t.done("x_ps", v - V)
                            t.grouped("dest", v - V)
                            sp.dma_start(xt[:, v, :], rows_of[bass.ds(at, P), :]).then_inc(s_in[v], 16)
                    passes(sp, body)
                    for v in range(V):
                        sp.wait_ge(s_in[v], 16 * NP)

                @block.gpsimd
                def _(pool):
                    def body(t, steps):
                        for v in steps:
                            if t.exists(v):
                                t.done("sig", v)
                                nc.gpsimd.tensor_tensor(sg[v][:, :], sg[v][:, :], glu[v], ALU.mult).then_inc(s["gs"], 1)
                            if t.exists(v - 5):
                                u = (v - 5) % V
                                t.done("yw", v - 5, alone=True)
                                nc.gpsimd.indirect_dma_start(parts, bass.IndirectOffsetOnAxis(ap=dest[:, u:u + 1], axis=0),
                                                             yw[u][:, :], None).then_inc(s_out[u], 16)
                    passes(pool, body, back=5)
                    for v in range(V):
                        pool.wait_ge(s_out[v], 16 * NP)

                @block.scalar
                def _(act):
                    def turned(t, v):
                        if t.exists(v):
                            t.done("h_ps", v - V)
                            t.done("x_ps", v)
                            nc.scalar.activation(x_t[v % V][:, :], ps[:, 2 + v % 2, 0:P], ACT.Copy).then_inc(s["x_t"], 1)

                    def body(t, steps):
                        for v in steps:
                            if v == 0 and isinstance(t.i, int) and t.i == 0:
                                turned(t, 0)
                            turned(t, v + 1)
                            if t.exists(v):
                                t.done("a", v - V)
                                t.done("glu", v)
                                nc.scalar.activation(sg[v][:, :], glu[v], ACT.Sigmoid, scale=1.702).then_inc(s["sig"], 1)
                            if t.exists(v - 3):
                                t.done("a_ps", v - 3)
                                nc.scalar.activation(act_t[(v - 3) % V][:, :], ps[:, 4 + (v - 3) % 2, 0:I1], ACT.Copy).then_inc(s["a_t"], 1)
                            if t.exists(v - 4):
                                u = (v - 4) % V
                                t.grouped("dest", v - 4)
                                t.done("y_ps", v - 4)
                                nc.scalar.activation(yw[u][:, :], ps[:, 6 + u % 2, 0:D], ACT.Copy, scale=own[:, 2, u:u + 1]).then_inc(s["yw"], 1)
                    passes(act, body, back=4)

                @block.vector
                def _(dve):
                    c = [0]

                    def link(ins):
                        c[0] += 1
                        ins.then_inc(s["plan"], 1)
                        dve.wait_ge(s["plan"], c[0])
                    link(nc.vector.scalar_tensor_tensor(cnt[:, :], k("iota"), float(-CAP), base[:, :], ALU.mult, ALU.add))
                    link(nc.vector.tensor_scalar(cnt[:, :], cnt[:, :], float(P - 1), None, ALU.add))
                    link(nc.vector.tensor_copy(cnti[:, :], cnt[:, :]))
                    link(nc.vector.tensor_scalar(nti[:, :], cnti[:, :], 7, None, ALU.arith_shift_right))
                    link(nc.vector.tensor_copy(ntile[:, :], nti[:, :]))
                    link(nc.vector.tensor_tensor_scan(upto[:, :], k("ones")[:, 0:E], ntile[:, :], 0.0, ALU.mult, ALU.add))
                    nc.vector.tensor_scalar(last_tile[:, :], upto[:, E - 1:E], -1.0, None, ALU.add)
                    nc.vector.tensor_copy(step[:, 1:E], ntile[:, 0:E - 1])
                    nc.vector.memset(step[:, 0:1], 0.0)
                    link(nc.vector.tensor_tensor(first[:, :], upto[:, :], ntile[:, :], ALU.subtract))
                    dve.wait_ge(s["weights"], 3 * 16)
                    nc.vector.tensor_scalar(surplus[:, :], number[:, :], last_tile[:, :], NOWHERE, ALU.is_gt, ALU.mult)
                    link(nc.vector.tensor_scalar(beside[:, :], number[:, :], float(P), k("token")[:, 0:1], ALU.mult, ALU.add))
                    link(nc.vector.tensor_scalar(beside[:, :], beside[:, :], float(2 * TILES * P), None, ALU.add))
                    link(nc.vector.tensor_scalar(number[:, :], number[:, :], last_tile[:, :], None, ALU.min))
                    link(nc.vector.tensor_tensor(ge[:, :, :], number[:, :].unsqueeze(2).to_broadcast([P, BT, E]),
                                                 first[:, :].unsqueeze(1).to_broadcast([P, BT, E]), ALU.is_ge))
                    link(nc.vector.tensor_tensor(gst[:, :, :], ge[:, :, :], step[:, :].unsqueeze(1).to_broadcast([P, BT, E]), ALU.mult))
                    nc.vector.tensor_reduce(expert[:, :], ge[:, :, :], AX.X, ALU.add)
                    link(nc.vector.tensor_reduce(row[:, :], gst[:, :, :], AX.X, ALU.add))
                    link(nc.vector.tensor_scalar(expert[:, :], expert[:, :], -1.0, None, ALU.add))
                    link(nc.vector.tensor_tensor(row[:, :], number[:, :], row[:, :], ALU.subtract))
                    nc.vector.tensor_tensor(digits[:, :, :], expert[:, :].rearrange("p (i v) -> p i v", v=V),
                                            k("powers").unsqueeze(1).to_broadcast([P, NP, V]), ALU.mult)
                    link(nc.vector.tensor_scalar(row[:, :], row[:, :], float(P), None, ALU.mult))
                    link(nc.vector.scalar_tensor_tensor(row[:, :], expert[:, :], float(CAP), row[:, :], ALU.mult, ALU.add))
                    link(nc.vector.tensor_reduce(packf[:, :], digits[:, :, :], AX.X, ALU.add))
                    nc.vector.tensor_copy(packs[:, :], packf[:, :])
                    nc.vector.tensor_copy(meta[:, :], row[:, :]).then_inc(s["meta"], 1)
                    dve.wait_ge(s["meta"], 1)

                    def weights_and_places(t, v):
                        gs, tiles = slice(v, v + GT), t.at(v, GT)
                        for u in range(v, v + GT):
                            t.landed(s_in, u)
                            t.landed(s_out, u - V)
                        nc.vector.tensor_tensor(own[:, 0, gs], xt[:, gs, D + 1], expert[:, tiles], ALU.is_equal).then_inc(s["second"], 1)
                        t.grouped("second", v)
                        nc.vector.tensor_scalar(own[:, 1, gs], own[:, 0, gs], float(TILES * P), None, ALU.mult)
                        nc.vector.tensor_tensor(own[:, 3, gs], own[:, 0, gs], xt[:, gs, D + 3], ALU.mult).then_inc(s["own"], 1)
                        t.grouped("own", v, 4, 1)
                        nc.vector.tensor_tensor(own[:, 1, gs], own[:, 1, gs], xt[:, gs, D], ALU.add).then_inc(s["own"], 1)
                        t.done("yw", v + GT - 1 - V)
                        nc.vector.tensor_tensor(own[:, 2, gs], own[:, 3, gs], xt[:, gs, D + 2], ALU.add)
                        t.grouped("own", v, 4, 2)
                        nc.vector.tensor_tensor(own[:, 1, gs], own[:, 1, gs], surplus[:, tiles], ALU.max).then_inc(s["own"], 1)
                        t.grouped("own", v, 4, 3)
                        nc.vector.tensor_tensor(own[:, 1, gs], own[:, 1, gs], beside[:, tiles], ALU.min).then_inc(s["own"], 1)
                        t.grouped("own", v, 4, 4)
                        nc.vector.tensor_copy(dest[:, gs], own[:, 1, gs]).then_inc(s["dest"], 1)

                    def body(t, steps):
                        es = t.experts() if t.exists(0) else None
                        for v in steps:
                            if t.exists(v):
                                t.done("a_ps", v - V)
                                t.done("h_ps", v)
                                nc.vector.tensor_tensor(hid[v][:, :], ps[:, v % 2, :], b1[:, bass.ds(es[v] * I2, I2)], ALU.add).then_inc(s["h"], 1)
                                t.done("h", v)
                                nc.vector.tensor_scalar(glu[v], glu[v], 7.0, None, ALU.min).then_inc(s["glu"], 1)
                                nc.vector.tensor_scalar(lin[v], lin[v], 7.0, -7.0, ALU.min, ALU.max).then_inc(s["lin"], 1)
                            if t.exists(v - 2):
                                u = (v - 2) % V
                                t.done("lin", v - 2)
                                t.done("gs", v - 2)
                                nc.vector.scalar_tensor_tensor(glu[u], lin[u], 1.0, sg[u][:, :], ALU.add, ALU.mult).then_inc(s["a"], 1)
                            if t.exists(v) and v % GT == GT - 1:
                                weights_and_places(t, v + 1 - GT)
                    passes(dve, body, back=2)

                @block.tensor
                def _(pe):
                    pe.wait_ge(s["weights"], 3 * 16)
                    pe.wait_ge(s["meta"], 1)

                    def turn(t, v):
                        if t.exists(v):
                            t.done("x_t", v - 2)
                            t.landed(s_in, v)
                            nc.tensor.transpose(ps[:, 2 + v % 2, 0:P], xt[:, v % V, 0:D], ident).then_inc(s["x_ps"], 1)

                    def body(t, steps):
                        es = t.experts() if t.exists(0) else None
                        before = t.experts(-1) if t.exists(-1) else None
                        for v in steps:
                            if v == 0 and isinstance(t.i, int) and t.i == 0:
                                turn(t, 0)
                            turn(t, v + 1)
                            if t.exists(v):
                                t.done("x_t", v)
                                t.done("h", v - 2)
                                nc.tensor.matmul(ps[:, v % 2, :], x_t[v][:, :], w1[:, bass.ds(es[v] * I2, I2)], start=True, stop=True).then_inc(s["h_ps"], 1)
                            if t.exists(v - 3):
                                t.done("a_t", v - 5)
                                t.done("a", v - 3)
                                for j in range(2):
                                    last = nc.tensor.transpose(ps[:, 4 + (v - 3) % 2, j * P:(j + 1) * P], glu[(v - 3) % V][:, j * P:(j + 1) * P], ident)
                                last.then_inc(s["a_ps"], 1)
                            if t.exists(v - 4):
                                u = (v - 4) % V
                                e = es[v - 4] if v >= 4 else before[v + 4]
                                t.done("yw", v - 6)
                                t.done("a_t", v - 4)
                                nc.tensor.matmul(ps[:, 6 + u % 2, 0:D], ident, b2[:, bass.ds(e * D, D)], start=True, stop=False)
                                for j in range(2):
                                    last = nc.tensor.matmul(ps[:, 6 + u % 2, 0:D], act_t[u][:, j * P:(j + 1) * P], w2[:, bass.ds(e * (2 * D) + j * D, D)],
                                                            start=False, stop=(j == 1))
                                last.then_inc(s["y_ps"], 1)
                    passes(pe, body, back=4)

        with ExitStack() as sc:
            part = [[sb(f"part{u}{j}", [P, C, D], scope=sc) for j in range(2)] for u in range(U)]
            gates = [sb(f"gates{u}", [P, D], scope=sc) for u in range(U)]
            s_part = [sem(f"p5_part{u}") for u in range(U)]
            s_sum = sem("p5_sum")
            s_scaled = sem("p5_scaled")
            s_total = sem("p5_total")
            s_out = [sem(f"p5_out{u}") for u in range(U)]
            parts_v = parts.rearrange("(t p) d -> p t d", p=P)
            with nc.Block() as block:
                @block.sync
                def _(sp):
                    with sp.Fori(0, NI) as i:
                        for u in range(U):
                            sp.wait_ge(s_total, sp.snap(i * U + u + 1))
                            for j in range(2):
                                sp.dma_start(part[u][j][:, :, :], parts_v[:, bass.ds((i * U + u) * C + j * TILES, C), :]).then_inc(s_part[u], 16)
                            src = rows_dram[bass.ds(i * U + u, 1), 4 * D:5 * D].squeeze(0)
                            sp.dma_start(gates[u][:, :], src.partition_broadcast(P)).then_inc(s_part[u], 16)
                    for u in range(U):
                        sp.wait_ge(s_part[u], 3 * 16 * NI)

                @block.scalar
                def _(act):
                    with act.Fori(0, NI) as i:
                        for u in range(U):
                            act.wait_ge(s_total, act.snap(i * U + U + u + 1))
                            act.dma_start(out[bass.ds(i * U + u, 1)].rearrange("o (c p) d -> p (o c) d", p=P), x_tok[:, bass.ds((i * U + u) * C, C), :]).then_inc(s_out[u], 16)
                    for u in range(U):
                        act.wait_ge(s_out[u], 16 * NI)

                @block.vector
                def _(dve):
                    nc.vector.memset(part[0][0][:, 0, 0:1], 0.0).then_inc(s_total, U)
                    with dve.Fori(0, NI) as i:
                        n = [dve.snap(i * U + u + 1) for u in range(U)]
                        landed = dve.snap((i + 1) * 48)
                        for u in range(U):
                            dve.wait_ge(s_part[u], landed)
                            nc.vector.tensor_tensor(part[u][0][:, :, :], part[u][0][:, :, :], part[u][1][:, :, :], ALU.add).then_inc(s_sum, 1)
                        for u in range(U):
                            dve.wait_ge(s_sum, n[u])
                            nc.vector.tensor_tensor(part[u][1][:, :, :], part[u][0][:, :, :], gates[u][:, :].unsqueeze(1).to_broadcast([P, C, D]),
                                                    ALU.mult).then_inc(s_scaled, 1)
                        for u in range(U):
                            dve.wait_ge(s_scaled, n[u])
                            xs = x_tok[:, bass.ds((i * U + u) * C, C), :]
                            nc.vector.tensor_tensor(xs, xs, part[u][1][:, :, :], ALU.add).then_inc(s_total, 1)


def constants():
    import numpy as np
    q = np.arange(P)
    parts = dict(
        ident=np.eye(P),
        upto=q[:, None] <= q[None],
        before=q[:, None] < q[None],
        ones=np.ones((P, P)),
        group_of=q[:, None] // N == np.arange(R)[None],
        head_of=q[:, None] // HD == np.arange(H)[None],
        iota=np.broadcast_to(np.arange(E), (P, E)),
        powers=np.broadcast_to(float(E) ** np.arange(E), (P, E)),
        token=q[:, None] + P * np.arange(16)[None],
        restart=np.broadcast_to(np.arange(128) % 16 > 0, (P, 128)),
        minus_half=np.full((P, 16), -0.5))
    return np.concatenate([parts[name] for name in CON], 1).astype(np.float32)


def layouts(i):
    import numpy as np

    def by_state(v):
        return v.reshape(G, R, N).transpose(1, 2, 0).reshape(P, G)

    mats = i["L0_attn_A"].reshape(G, R, N, N)
    w1, b1 = i["L1_ffn_mlp1_w"], i["L1_ffn_mlp1_b"]
    tiles = i["L0_attn_x"].shape[0] * C
    return dict(
        con=constants(),
        numbers=np.arange(-(-(2 * tiles + E - 1) // 8) * 8).astype(np.float32),
        x=i["L0_attn_x"],
        A=mats.transpose(1, 2, 0, 3), A_t=mats.transpose(1, 3, 0, 2),
        B_col=by_state(i["L0_attn_Bp"]), C_col=by_state(i["L0_attn_Cp"]), D_col=i["L0_attn_Dp"].reshape(G, R).T,
        Wg_t=i["L0_attn_Wg"].T, bg=i["L0_attn_bg"][:, None],
        gamma=i["L0_attn_gamma"], beta=i["L0_attn_beta"], bo=i["L1_attn_bo"][:, None],
        c_t=np.stack([i["L0_c"].T, i["L1_c"].T], 1), wmod=np.stack([i["L0_wmod"], i["L1_wmod"]], 1),
        gw0=i["L0_ffn_gate_w"], gb0=i["L0_ffn_gate_b"], ew0=i["L0_ffn_expert_w"].transpose(1, 0, 2), eb0=i["L0_ffn_expert_b"],
        Wqkv_t=np.concatenate([i["L1_attn_Wq"].T, i["L1_attn_Wk"].T, i["L1_attn_Wv"].T], 1),
        bqkv=np.concatenate([i["L1_attn_bq"], i["L1_attn_bk"], i["L1_attn_bv"]]), Wo_t=i["L1_attn_Wo"].T,
        ns=i["L1_ffn_norm_scale"], gw1=i["L1_ffn_gate_w"], gb1=i["L1_ffn_gate_b"],
        w1=np.concatenate([w1[:, :, 0::2], w1[:, :, 1::2]], 2).transpose(1, 0, 2),
        b1=np.concatenate([b1[:, 0::2], b1[:, 1::2]], 1),
        w2=i["L1_ffn_mlp2_w"].reshape(E, 2, P, D).transpose(2, 0, 1, 3), b2=i["L1_ffn_mlp2_b"])


def kernel(**inputs):
    import numpy as np
    import concourse.bacc as bacc
    from concourse.bass_utils import run_bass_kernel_spmd

    nc = bacc.Bacc("TRN2", target_bir_lowering=False, num_devices=1)
    arrays, args = {}, {}
    for name, v in layouts({n: np.asarray(v) for n, v in inputs.items()}).items():
        arrays[f"in_{name}_dram"] = np.ascontiguousarray(v)
        args[name] = nc.dram_tensor(f"in_{name}_dram", v.shape, mybir.dt.from_np(v.dtype), kind="ExternalInput").ap()
    shape = inputs["L0_attn_x"].shape
    out = nc.dram_tensor("out_0_dram", shape, F32, kind="ExternalOutput").ap()
    build(nc, args, out)
    r = run_bass_kernel_spmd(nc, [arrays], core_ids=[0])
    return r.results[0]["out_0_dram"]
```

```python
from contextlib import ExitStack

import concourse.bass as bass
from concourse import mybir
from concourse.alu_op_type import AluOpType as ALU

F32 = mybir.dt.float32
BF16 = mybir.dt.bfloat16
I32 = mybir.dt.int32
U32 = mybir.dt.uint32
ACT = mybir.ActivationFunctionType
AX = mybir.AxisListType

P = 128
D = 128
C = 4
N = 16
R = 8
G = D // R
H = 16
HD = D // H
E = 8
I2 = 512
U = 4
EPS = 1e-5
LEVELS = 7
NOWHERE = 1e6
CON = {}
for _name, _width in (("ident", P), ("upto", P), ("before", P), ("ones", P), ("group_of", R), ("head_of", H), ("iota", E), ("powers", E), ("token", 16), ("restart", 128), ("minus_half", 16)):
    CON[_name] = (sum(w for _, w in CON.values()), _width)
CON_W = sum(w for _, w in CON.values())
ROWS = ("ga_gamma", "ga_beta", "cb1", "sb1", "gb1")


def build(nc, a, out):
    B = a["x"].shape[0]
    NI = B // U
    TILES = B * C
    rows_dram = nc.dram_tensor("rows_dram", [B, len(ROWS) * D], F32).ap()
    taps_dram = nc.dram_tensor("taps_dram", [D, 2 * P], F32)

    ctx = ExitStack()
    names_used = []
    with ctx:
        def sb(name, shape, dt=F32, scope=ctx):
            names_used.append(name)
            return scope.enter_context(nc.sbuf_tensor(f"{name}_{len(names_used)}", shape, dt))

        phase_sems = []
        passed = nc.alloc_semaphore(name="passed")

        def sem(name):
            phase_sems.append(nc.alloc_semaphore(name=name))
            return phase_sems[-1]

        def hold(eng, semaphore, value):
            eng.wait_ge(semaphore, value)
            eng.sem_inc(passed, 1)

        def wait(eng, semaphore, value):
            eng.wait_ge(semaphore, value)

        def end_phase():
            nc.all_engine_barrier()
            nc.clear_and_free_semaphores(phase_sems)
            nc.all_engine_barrier()
            phase_sems.clear()

        ps = ctx.enter_context(nc.psum_tensor("ps", [P, 8, 512], F32))
        con = sb("con", [P, CON_W])

        def k(name, parts=P):
            at, width = CON[name]
            return con[0:parts, at:at + width]

        ident = k("ident")

        def ps3(j):
            return ps[:, 3 * j:3 * j + 3, :].rearrange("p k n -> p (k n)")
        x_tok = sb("x_tok", [P, TILES, D])
        xg = sb("xg", [P, D, TILES])
        mod_t = sb("mod_t", [P, 9, B])
        SA0, CA0, SB0, CB0, GB0, SA1, CA1, GA1, GA_BO = range(9)

        ssm = ExitStack()
        states_of = sb("states_of", [P, G, 3, P], scope=ssm)
        TO_STATE, CARRY, TO_OUT = range(3)
        wg = sb("wg", [P, D], scope=ssm)
        bg = sb("bg", [P, 1], scope=ssm)
        with ExitStack() as sc:
            power = sb("power", [P, G, 2 * P], scope=sc)
            power_t = sb("power_t", [P, G, 2 * P], scope=sc)
            wout, vin = power[:, :, P:2 * P], power_t[:, :, P:2 * P]
            a1t = sb("a1t", [P, G, P], scope=sc)
            bcol = sb("bcol", [P, G], scope=sc)
            ccol = sb("ccol", [P, G], scope=sc)
            dcol = sb("dcol", [R, G], scope=sc)
            cbd = sb("cbd", [P, G, R], scope=sc)
            taps = sb("taps", [R, G, 2 * P], scope=sc)
            c_t = sb("c_t", [P, 2, B], scope=sc)
            sg_t = sb("sg_t", [P, 2, B], scope=sc)
            wmod = sb("wmod", [P, 2, 6 * D], scope=sc)
            vecs = sb("vecs", [B, 2, D], scope=sc)
            bo = sb("bo", [P, 1], scope=sc)
            ga0 = sb("ga0", [B, D], scope=sc)
            rowv = sb("rowv", [B, len(ROWS), D], scope=sc)
            sign = sb("sign", [P, 2 * D + 2 * B], scope=sc)
            s_x = [sem(f"s_x{j}") for j in range(2)]
            s_con = sem("s_con")
            s_zero = sem("s_zero")
            s_zero_t = sem("s_zero_t")
            s_a = sem("s_a")
            s_c = sem("s_c")
            s_par = sem("s_par")
            s_sig = sem("s_sig")
            s_silu = sem("s_silu")
            s_mod = sem("s_mod")
            s_modT = sem("s_modT")
            s_modv = sem("s_modv")
            s_rows = sem("s_rows")
            s_rout = sem("s_rout")
            s_seed = sem("s_seed")
            s_sqt = sem("s_sqt")
            s_sqtc = sem("s_sqtc")
            s_a1 = sem("s_a1")
            s_sqc = sem("s_sqc")
            s_fin = sem("s_fin")
            s_fint = sem("s_fint")
            s_tap = sem("s_tap")
            s_dv = sem("s_dv")
            s_tout = sem("s_tout")
            with nc.Block() as block:
                @block.sync
                def _(sp):
                    sp.dma_start(con[:, :], a["con"]).then_inc(s_con, 16)
                    sp.dma_start(c_t[:, :, :], a["c_t"]).then_inc(s_c, 16)
                    sp.dma_start(wmod[:, :, :], a["wmod"]).then_inc(s_c, 16)
                    sp.wait_ge(s_zero, 1)
                    with nc.allow_non_contiguous_dma(reason="small state matrices"):
                        for r in range(R):
                            d0 = slice(16 * r, 16 * r + 16)
                            sp.dma_start(power[d0, :, d0], a["A"][r]).then_inc(s_a, 16)
                    sp.dma_start(bcol[:, :], a["B_col"]).then_inc(s_par, 16)
                    sp.dma_start(ccol[:, :], a["C_col"]).then_inc(s_par, 16)
                    sp.dma_start(dcol[:, :], a["D_col"]).then_inc(s_par, 16)
                    sp.dma_start(wg[:, :], a["Wg_t"]).then_inc(s_par, 16)
                    sp.dma_start(bg[:, :], a["bg"]).then_inc(s_par, 16)
                    sp.dma_start(bo[:, :], a["bo"]).then_inc(s_par, 16)
                    for j, name in enumerate(("gamma", "beta")):
                        sp.dma_start(vecs[:, j, :], a[name].partition_broadcast(B)).then_inc(s_par, 16)
                    for j in range(2):
                        h0 = slice(j * B // 2, (j + 1) * B // 2)
                        sp.dma_start(x_tok[:, j * TILES // 2:(j + 1) * TILES // 2, :],
                                     a["x"][h0].rearrange("b (c p) d -> p (b c) d", p=P)).then_inc(s_x[j], 16)
                    sp.wait_ge(s_rows, 1)
                    sp.dma_start(rows_dram, rowv[:, :, :].rearrange("b j d -> b (j d)")).then_inc(s_rout, 16)
                    sp.wait_ge(s_tap, 2)
                    sp.dma_start(taps_dram.ap().rearrange("(g r) t -> r g t", r=R), taps[:, :, :]).then_inc(s_tout, 16)
                    sp.wait_ge(s_par, 8 * 16)
                    sp.wait_ge(s_x[0], 16)
                    sp.wait_ge(s_x[1], 16)
                    sp.wait_ge(s_rout, 16)
                    sp.wait_ge(s_tout, 16)

                @block.gpsimd
                def _(pool):
                    nc.gpsimd.memset(power_t[:, :, 0:P], 0.0).then_inc(s_zero_t, 1)
                    nc.gpsimd.memset(taps[:, :, :], 0.0).then_inc(s_zero_t, 1)

                @block.vector
                def _(dve):
                    nc.vector.memset(power[:, :, 0:P], 0.0).then_inc(s_zero, 1)
                    dve.wait_ge(s_sig, 1)
                    nc.vector.tensor_tensor(sg_t[:, :, :], c_t[:, :, :], sg_t[:, :, :], ALU.mult).then_inc(s_silu, 1)
                    n = [0]

                    def link(ins):
                        n[0] += 1
                        ins.then_inc(s_dv, 1)
                        dve.wait_ge(s_dv, n[0])
                    dve.wait_ge(s_modv, 2)
                    dve.wait_ge(s_par, 8 * 16)
                    gates = [(ga0[:, :], sign[0:B, 0:D]), (rowv[:, 4, :], sign[0:B, D:2 * D]),
                             (mod_t[:, GB0, :], sign[:, 2 * D:2 * D + B]), (mod_t[:, GA1, :], sign[:, 2 * D + B:2 * D + 2 * B])]
                    for g, sg in gates:
                        last = nc.vector.tensor_scalar(sg, g, 0.0, 2.0, ALU.is_ge, ALU.mult)
                    link(last)
                    for g, sg in gates:
                        nc.vector.tensor_scalar(sg, sg, -1.0, None, ALU.add)
                        last = nc.vector.scalar_tensor_tensor(g, g, -1.0, g, ALU.mult, ALU.max)
                    link(last)
                    for g, sg in gates:
                        last = nc.vector.tensor_scalar(g, g, 0.25, None, ALU.max)
                    link(last)
                    for g, sg in gates:
                        last = nc.vector.tensor_tensor(g, g, sg, ALU.mult)
                    link(last)
                    nc.vector.tensor_scalar(mod_t[:, GA_BO, :], mod_t[:, GA1, :], bo[:, :], None, ALU.mult)
                    nc.vector.tensor_tensor(rowv[:, 0, :], ga0[:, :], vecs[:, 0, :], ALU.mult)
                    nc.vector.tensor_tensor(rowv[:, 1, :], ga0[:, :], vecs[:, 1, :], ALU.mult).then_inc(s_rows, 1)
                    nc.vector.tensor_tensor(cbd[:, :, :], ccol[:, :].unsqueeze(2).to_broadcast([P, G, R]),
                                            k("group_of").unsqueeze(1).to_broadcast([P, G, R]), ALU.mult)
                    nc.vector.tensor_copy(power_t[:, :, P:P + 1], bcol[:, :].unsqueeze(2))
                    nc.vector.tensor_copy(power[:, :, P:P + 1], ccol[:, :].unsqueeze(2)).then_inc(s_seed, 1)
                    dve.wait_ge(s_zero_t, 2)
                    dve.wait_ge(s_a, 2 * R * 16)
                    nc.vector.tensor_copy(a1t[:, :, :], power_t[:, :, 0:P]).then_inc(s_a1, 1)
                    dve.wait_ge(s_a1, 1)
                    for lv in range(LEVELS):
                        m = 1 << lv
                        for q in range(4):
                            dve.wait_ge(s_sqt, 4 * lv + q + 1)
                            gs, b0 = slice(4 * q, 4 * q + 4), 4 * (q % 2) + 2
                            src = ps[:, b0:b0 + 2, :].rearrange("p b (g n) -> p b g n", g=2)
                            if lv < LEVELS - 1:
                                nc.vector.tensor_copy(power_t[:, gs, 0:P].rearrange("p (b g) n -> p b g n", b=2), src[:, :, :, 0:P])
                            nc.vector.tensor_copy(power_t[:, gs, P + m:P + 2 * m].rearrange("p (b g) n -> p b g n", b=2),
                                                  src[:, :, :, P:P + m]).then_inc(s_sqtc, 1)
                    for q in range(4):
                        dve.wait_ge(s_fin, q + 1)
                        nc.vector.tensor_copy(states_of[:, 4 * q:4 * q + 4, TO_OUT, :],
                                              ps[:, q, :].rearrange("p (g m) -> p g m", m=P)).then_inc(s_fint, 1)
                    dve.wait_ge(s_fin, 12)
                    link(nc.vector.tensor_copy(taps[:, :, P:2 * P].rearrange("r (k g) m -> r k g m", k=4),
                                               ps[0:R, 4:8, :].rearrange("r k (g m) -> r k g m", m=P)))
                    nc.vector.tensor_tensor(taps[:, :, P:P + 1], taps[:, :, P:P + 1], dcol[:, :].unsqueeze(2), ALU.add).then_inc(s_tap, 1)
                    dve.wait_ge(s_tap, 1)
                    nc.vector.tensor_scalar(taps[:, :, P:P + 1], taps[:, :, P:P + 1], 1.0, None, ALU.add).then_inc(s_tap, 1)

                @block.scalar
                def _(act):
                    act.wait_ge(s_zero_t, 1)
                    with nc.allow_non_contiguous_dma(reason="small state matrices"):
                        for r in range(R):
                            d0 = slice(16 * r, 16 * r + 16)
                            act.dma_start(power_t[d0, :, d0], a["A_t"][r]).then_inc(s_a, 16)
                    act.wait_ge(s_c, 32)
                    nc.scalar.activation(sg_t[:, :, :], c_t[:, :, :], ACT.Sigmoid).then_inc(s_sig, 1)
                    act.wait_ge(s_modT, 1)
                    for j in range(8):
                        last = nc.scalar.activation(mod_t[:, j, :], ps[:, 4, 16 * j:16 * j + B], ACT.Copy,
                                                    bias=float(j in (CA0, CB0, CA1)))
                    last.then_inc(s_modv, 1)
                    act.wait_ge(s_mod, 2)
                    nc.scalar.activation(ga0[:, :], ps[0:B, 0, 0:D], ACT.Copy)
                    nc.scalar.activation(rowv[:, 3, :], ps[0:B, 1, 0:D], ACT.Copy)
                    nc.scalar.activation(rowv[:, 2, :], ps[0:B, 1, D:2 * D], ACT.Copy, bias=1.0)
                    nc.scalar.activation(rowv[:, 4, :], ps[0:B, 1, 2 * D:3 * D], ACT.Copy).then_inc(s_modv, 1)
                    for lv in range(LEVELS):
                        m = 1 << lv
                        for q in range(4):
                            act.wait_ge(s_sqt, 4 * lv + q + 1)
                            gs, b0 = slice(4 * q, 4 * q + 4), 4 * (q % 2)
                            src = ps[:, b0:b0 + 2, :].rearrange("p b (g n) -> p b g n", g=2)
                            dst = states_of[:, gs, CARRY, :] if lv == LEVELS - 1 else power[:, gs, 0:P]
                            nc.scalar.activation(dst.rearrange("p (b g) n -> p b g n", b=2), src[:, :, :, 0:P], ACT.Copy)
                            nc.scalar.activation(power[:, gs, P + m:P + 2 * m].rearrange("p (b g) n -> p b g n", b=2),
                                                 src[:, :, :, P:P + m], ACT.Copy).then_inc(s_sqc, 1)
                    for q in range(4):
                        act.wait_ge(s_fin, 5 + q)
                        nc.scalar.activation(states_of[:, 4 * q:4 * q + 4, TO_STATE, :],
                                             ps[:, 4 + q, :].rearrange("p (g m) -> p g m", m=P), ACT.Copy).then_inc(s_sqc, 1)

                @block.tensor
                def _(pe):
                    pe.wait_ge(s_silu, 1)
                    for j, (l, part) in enumerate(((0, 0), (0, 1), (0, 3), (0, 4), (0, 5), (1, 0), (1, 1), (1, 2))):
                        last = nc.tensor.matmul(ps[:, 4, 16 * j:16 * j + B], wmod[:, l, part * D:(part + 1) * D],
                                                sg_t[:, l, :], start=True, stop=True)
                    last.then_inc(s_modT, 1)
                    nc.tensor.matmul(ps[0:B, 0, 0:D], sg_t[:, 0, :], wmod[:, 0, 2 * D:3 * D], start=True, stop=True).then_inc(s_mod, 1)
                    nc.tensor.matmul(ps[0:B, 1, 0:3 * D], sg_t[:, 1, :], wmod[:, 1, 3 * D:6 * D], start=True, stop=True).then_inc(s_mod, 1)
                    pe.wait_ge(s_con, 16)
                    pe.wait_ge(s_seed, 1)
                    pe.wait_ge(s_modv, 2)
                    pe.wait_ge(s_a1, 1)
                    for lv in range(LEVELS):
                        m = 1 << lv
                        for q in range(4):
                            done = 4 * lv + q - 1
                            if done > 0:
                                pe.wait_ge(s_sqc, done)
                                pe.wait_ge(s_sqtc, done)
                            for g in range(4 * q, 4 * q + 4):
                                bank, at = 4 * (q % 2) + (g % 4) // 2, (g % 2) * 256
                                nc.tensor.matmul(ps[:, bank, at:at + P + m], power_t[:, g, 0:P], power[:, g, 0:P + m], start=True, stop=True)
                            for g in range(4 * q, 4 * q + 4):
                                bank, at = 4 * (q % 2) + 2 + (g % 4) // 2, (g % 2) * 256
                                lo = 0 if lv < LEVELS - 1 else P
                                last = nc.tensor.matmul(ps[:, bank, at + lo:at + P + m], power[:, g, 0:P], power_t[:, g, lo:P + m], start=True, stop=True)
                            last.then_inc(s_sqt, 1)
                    pe.wait_ge(s_sqtc, 4 * LEVELS)
                    pe.wait_ge(s_sqc, 4 * LEVELS)
                    for g in range(G):
                        last = nc.tensor.matmul(ps[:, g // 4, (g % 4) * P:(g % 4 + 1) * P], a1t[:, g, :], wout[:, g, :],
                                                start=True, stop=True)
                        if g % 4 == 3:
                            last.then_inc(s_fin, 1)
                    for g in range(G):
                        last = nc.tensor.transpose(ps[:, 4 + g // 4, (g % 4) * P:(g % 4 + 1) * P], vin[:, g, :], ident)
                        if g % 4 == 3:
                            last.then_inc(s_fin, 1)
                    for q in range(4):
                        pe.wait_ge(s_sqc, 4 * LEVELS + q + 1)
                        for g in range(4 * q, 4 * q + 4):
                            last = nc.tensor.matmul(ps[0:R, 4 + q, (g % 4) * P:(g % 4 + 1) * P], cbd[:, g, :], vin[:, g, :],
                                                    start=True, stop=True)
                        last.then_inc(s_fin, 1)

        with ExitStack() as sc:
            st = sb("st", [P, U, C, 6], scope=sc)
            mv = sb("mv", [P, U, C, 2], scope=sc)
            rstd = sb("rstd", [P, U * C], scope=sc)
            nrm = [sb(f"nrm{u}", [P, C, D], scope=sc) for u in range(U)]
            h_t = [sb(f"h_t{u}", [P, C * P], scope=sc) for u in range(U)]
            sig = [sb(f"sig{u}", [P, C * P], scope=sc) for u in range(U)]
            xr_t = [sb(f"xr_t{u}", [P, C * P], scope=sc) for u in range(U)]
            s_st = sem("p1_stats")
            s_mv = sem("p1_mean_var")
            s_ve = sem("p1_var_eps")
            s_rs = sem("p1_rstd")
            s_n = sem("p1_normed")
            s_nt = sem("p1_transposed")
            s_h = sem("p1_modulated")
            s_gm = sem("p1_gate_product")
            s_gs = sem("p1_gate")
            s_xr = sem("p1_gated")
            s_xt = sem("p1_back")
            s_w = sem("p1_written")
            with nc.Block() as block:
                @block.vector
                def _(dve):
                    def number(i, per, k):
                        return i * per + k if isinstance(i, int) else dve.snap(i * per + k)

                    def tile_of(i, t):
                        return x_tok[:, i * U * C + t, :] if isinstance(i, int) else x_tok[:, bass.ds(i * (U * C) + t, 1), :].squeeze(1)

                    def statistics(i, more=True):
                        for u in range(U):
                            for c in range(C):
                                last = nc.vector.bn_stats(st[:, u, c, :], tile_of(i, u * C + c))
                        last.then_inc(s_st, 1)
                        if more:
                            dve.wait_ge(s_n, number(i, U, 0))
                        hold(dve, s_st, number(i, 1, 1))
                        for u in range(U):
                            for c in range(C):
                                last = nc.vector.bn_aggr(mv[:, u, c, :], st[:, u, c, :])
                        last.then_inc(s_mv, 1)

                    def norm(i):
                        dve.wait_ge(s_rs, number(i, 1, 1))
                        for u in range(U):
                            for c in range(C):
                                last = nc.vector.tensor_scalar(nrm[u][:, c, :], tile_of(i, u * C + c), mv[:, u, c, 0:1],
                                                               rstd[:, u * C + c:u * C + c + 1], ALU.subtract, ALU.mult)
                            last.then_inc(s_n, 1)

                    def keep(i):
                        for u in range(U):
                            dve.wait_ge(s_gs, number(i, U, u + 1))
                            nc.vector.tensor_tensor(xr_t[u][:, :].rearrange("p (c t) -> p c t", c=C)[:, :, ::-1],
                                                    h_t[u][:, :].rearrange("p (c t) -> p c t", c=C),
                                                    sig[u][:, :].rearrange("p (c t) -> p c t", c=C), ALU.mult).then_inc(s_xr, 1)
                        for u in range(U):
                            dve.wait_ge(s_xt, number(i, U, u + 1))
                            dst = xg[:, :, (i * U + u) * C:(i * U + u + 1) * C] if isinstance(i, int) else xg[:, :, bass.ds((i * U + u) * C, C)]
                            nc.vector.tensor_copy(dst.rearrange("p d c -> p c d"), ps[:, u, :].rearrange("p (c d) -> p c d", c=C)).then_inc(s_w, 1)
                    statistics(0, more=False)
                    with dve.Fori(0, NI - 1) as i:
                        norm(i)
                        statistics(i + 1)
                        keep(i)
                    norm(NI - 1)
                    keep(NI - 1)

                @block.gpsimd
                def _(pool):
                    with pool.Fori(0, NI) as i:
                        it = pool.snap(i + 1)
                        hold(pool, s_mv, it)
                        nc.gpsimd.tensor_scalar(rstd[:, :], mv[:, :, :, 1].rearrange("p u c -> p (u c)"), EPS, None, ALU.add).then_inc(s_ve, 1)
                        pool.wait_ge(s_ve, it)
                        nc.gpsimd.tensor_tensor(rstd[:, :], rstd[:, :], k("minus_half"), ALU.pow).then_inc(s_rs, 1)

                @block.scalar
                def _(act):
                    with act.Fori(0, NI) as i:
                        n = [act.snap(i * U + u + 1) for u in range(U)]
                        for u in range(U):
                            act.wait_ge(s_nt, n[u])
                            b = i * U + u
                            nc.scalar.activation(h_t[u][:, :], ps[:, u, :], ACT.Identity,
                                                 bias=mod_t[:, SA0, bass.ds(b, 1)], scale=mod_t[:, CA0, bass.ds(b, 1)]).then_inc(s_h, 1)
                        for u in range(U):
                            act.wait_ge(s_gm, n[u])
                            nc.scalar.activation(sig[u][:, :], ps[:, 4 + u, :], ACT.Sigmoid, bias=bg[:, :]).then_inc(s_gs, 1)

                @block.tensor
                def _(pe):
                    with pe.Fori(0, NI) as i:
                        n = [pe.snap(i * U + u + 1) for u in range(U)]
                        for u in range(U):
                            pe.wait_ge(s_n, n[u])
                            for c in range(C):
                                last = nc.tensor.transpose(ps[:, u, c * P:(c + 1) * P], nrm[u][:, c, :], ident)
                            last.then_inc(s_nt, 1)
                        for u in range(U):
                            pe.wait_ge(s_h, n[u])
                            nc.tensor.matmul(ps[:, 4 + u, :], wg[:, :], h_t[u][:, :], start=True, stop=True).then_inc(s_gm, 1)
                        for u in range(U):
                            pe.wait_ge(s_xr, n[u])
                            for c in range(C):
                                last = nc.tensor.transpose(ps[:, u, c * P:(c + 1) * P], xr_t[u][:, c * P:(c + 1) * P], ident)
                            last.then_inc(s_xt, 1)

        with ExitStack() as sc:
            TS = B * C
            toep = [sb(f"toep{u}", [P, R, P], scope=sc) for u in range(U)]
            mats = [sb(f"mats{u}", [P, 3, P], scope=sc) for u in range(U)]
            ends = [sb(f"ends{u}", [P, TS], scope=sc) for u in range(U)]
            endm = [sb(f"endm{u}", [P, R, TS], scope=sc) for u in range(U)]
            carry = [sb(f"carry{u}", [P, R, TS], scope=sc) for u in range(U)]
            s_toep = [sem(f"p2_toep{u}") for u in range(U)]
            s_m = sem("p2_matrices")
            s_mo = sem("p2_out_matrix")
            s_e = sem("p2_end_products")
            s_em = sem("p2_ends_masked")
            s_er = sem("p2_ends")
            s_c1 = [sem(f"p2_carry_product{j}") for j in range(2)]
            s_c2 = [sem(f"p2_carried{j}") for j in range(2)]
            s_cb = sem("p2_carry_spread")
            s_y = sem("p2_outputs")
            s_yc = sem("p2_outputs_kept")
            s_z = sem("p2_cleared")

            def by_chunk(ap, c):
                return ap.rearrange("p (b c) -> p b c", c=C)[:, :, c]

            s2 = dict(matrices=s_m, out_matrix=s_mo, ends_ps=s_e, masked=s_em, ends=s_er, carry_ps0=s_c1[0], carry_ps1=s_c1[1],
                      carried0=s_c2[0], carried1=s_c2[1], spread=s_cb, out_ps=s_y, kept=s_yc)

            class Group:
                def __init__(self, eng, i):
                    self.eng, self.i, self.made = eng, i, {}

                def value(self, per, k):
                    if isinstance(self.i, int):
                        return self.i * per + k
                    if (per, k) not in self.made:
                        self.made[per, k] = self.eng.snap(self.i * per + k)
                    return self.made[per, k]

                def exists(self, v):
                    return not isinstance(self.i, int) or 0 <= self.i * U + v < G

                def done(self, name, v):
                    if self.exists(v):
                        self.eng.wait_ge(s2[name], self.value(U, v + 1))

                def channels(self, v, first=0, many=R):
                    at = (self.i * U + v) * R + first
                    return xg[:, at:at + many, :] if isinstance(self.i, int) else xg[:, bass.ds(at, many), :]

            def groups(eng, body, back=0):
                body(Group(eng, 0), range(U))
                with eng.Fori(1, G // U - 1) as i:
                    body(Group(eng, i), range(U))
                body(Group(eng, G // U - 1), range(U))
                body(Group(eng, G // U), range(back))

            with nc.Block() as block:
                @block.sync
                def _(sp):
                    def body(g, steps):
                        for v in steps:
                            g.done("out_ps", v - U)
                            src = bass.AP(taps_dram, (g.i * U + v) * (R * 2 * P) + 1, [[1, P], [2 * P, R], [1, P]])
                            sp.dma_start(toep[v][:, :, :], src).then_inc(s_toep[v], 16)
                    groups(sp, body)
                    for u in range(U):
                        sp.wait_ge(s_toep[u], 16 * (G // U))

                @block.scalar
                def _(act):
                    def body(g, steps):
                        for v in steps:
                            at = g.i * U + v
                            src = states_of[:, at:at + 1, :, :] if isinstance(g.i, int) else states_of[:, bass.ds(at, 1), :, :]
                            g.done("carry_ps1", v - U)
                            nc.scalar.activation(mats[v][:, 0:TO_OUT, :].unsqueeze(1), src[:, :, 0:TO_OUT, :], ACT.Copy).then_inc(s_m, 1)
                            g.done("out_ps", v - U)
                            nc.scalar.activation(mats[v][:, TO_OUT:, :].unsqueeze(1), src[:, :, TO_OUT:, :], ACT.Copy).then_inc(s_mo, 1)
                    groups(act, body)

                @block.vector
                def _(dve):
                    for u in range(U):
                        last = nc.vector.memset(carry[u][:, :, :], 0.0)
                    last.then_inc(s_z, 1)

                    def body(g, steps):
                        for v in steps:
                            if g.exists(v - 4):
                                g.done("out_ps", v - 4)
                                nc.vector.tensor_copy(g.channels(v - 4), ps[:, 4 + v % U, 0:R * TS].rearrange("p (r t) -> p r t", r=R)).then_inc(s_yc, 1)
                            if g.exists(v):
                                g.done("ends_ps", v)
                                nc.vector.tensor_tensor(endm[v][:, :, :], ps[:, v, 0:R * TS].rearrange("p (r t) -> p r t", r=R),
                                                        k("group_of").unsqueeze(2).to_broadcast([P, R, TS]), ALU.mult).then_inc(s_em, 1)
                            for j in range(2):
                                u = (v - 1 - j) % U
                                if g.exists(v - 1 - j):
                                    g.done(f"carry_ps{j}", v - 1 - j)
                                    nc.vector.tensor_tensor(by_chunk(ends[u][:, :], j + 1), by_chunk(ends[u][:, :], j + 1), ps[:, u, j * B:(j + 1) * B],
                                                            ALU.add).then_inc(s_c2[j], 1)
                            if g.exists(v):
                                g.done("masked", v)
                                nc.vector.tensor_reduce(ends[v][:, :], endm[v][:, :, :].rearrange("p r t -> p t r"), AX.X, ALU.add).then_inc(s_er, 1)
                            if g.exists(v - 2):
                                u = (v - 2) % U
                                g.done("carried1", v - 2)
                                for c in range(1, C):
                                    src = by_chunk(ends[u][:, :], c - 1)
                                    last = nc.vector.tensor_tensor(
                                        carry[u][:, :, :].rearrange("p r (b c) -> p r b c", c=C)[:, :, :, c],
                                        src.unsqueeze(1).to_broadcast([P, R, B]),
                                        k("group_of").unsqueeze(2).to_broadcast([P, R, B]), ALU.mult)
                                last.then_inc(s_cb, 1)
                    groups(dve, body, back=4)

                @block.tensor
                def _(pe):
                    pe.wait_ge(s_z, 1)

                    def body(g, steps):
                        for v in steps:
                            if g.exists(v):
                                g.done("carried1", v - 4)
                                g.done("matrices", v)
                                nc.tensor.matmul(ps[:, v, 0:R * TS], mats[v][:, TO_STATE, :], g.channels(v), start=True, stop=True).then_inc(s_e, 1)
                            for j in range(2):
                                u = (v - 1 - j) % U
                                if g.exists(v - 1 - j):
                                    g.done("carried0" if j else "ends", v - 1 - j)
                                    nc.tensor.matmul(ps[:, u, j * B:(j + 1) * B], mats[u][:, CARRY, :], by_chunk(ends[u][:, :], j),
                                                     start=True, stop=True).then_inc(s_c1[j], 1)
                            if g.exists(v - 3):
                                u = (v - 3) % U
                                g.done("spread", v - 3)
                                g.done("out_matrix", v - 3)
                                pe.wait_ge(s_toep[u], g.value(16, 16 * ((v - 3) // U) + 16))
                                nc.tensor.matmul(ps[:, 4 + u, 0:R * TS], mats[u][:, TO_OUT, :], carry[u][:, :, :], start=True, stop=False)
                                for r in range(R):
                                    last = nc.tensor.matmul(ps[:, 4 + u, r * TS:(r + 1) * TS], toep[u][:, r, :], g.channels(v - 3, r, 1),
                                                            start=False, stop=(r == R - 1))
                                last.then_inc(s_y, 1)
                    groups(pe, body, back=3)
        ssm.close()
        end_phase()

        mean_x = sb("mean_x", [P, TILES])
        rstd_x = sb("rstd_x", [P, TILES])
        NT = U * C
        with ExitStack() as sc:
            st = sb("st", [P, 2, NT, 6], scope=sc)
            mv = sb("mv", [P, NT, 2], scope=sc)
            mv2 = sb("mv2", [P, NT, 2], scope=sc)
            var_eps = sb("var_eps", [P, NT], scope=sc)
            rstd = sb("rstd", [P, NT], scope=sc)
            shift = sb("shift", [P, NT], scope=sc)
            nrm = [sb(f"nrm{u}", [P, C, D], scope=sc) for u in range(U)]
            rows = [sb(f"rows{u}", [P, 2, D], scope=sc) for u in range(U)]
            names = ("y_stats", "y_mv", "y_ve", "y_rs", "shift", "normed", "gamma", "beta", "added", "x_stats", "x_mv", "x_ve",
                     "x_rs")
            s = {nm: sem(f"join_{nm}") for nm in names}
            s_rows = [sem(f"join_rows{u}") for u in range(U)]

            def value(eng, i, per, k):
                return i * per + k if isinstance(i, int) else eng.snap(i * per + k)

            def tiles(ap, i, many):
                return ap[:, i * NT:i * NT + many] if isinstance(i, int) else ap[:, bass.ds(i * NT, many)]

            def tile_of(ap, i, t):
                return ap[:, i * NT + t] if isinstance(i, int) else ap[:, bass.ds(i * NT + t, 1)].squeeze(1)

            def seq_of(i, u):
                return x_tok[:, (i * U + u) * C:(i * U + u + 1) * C, :] if isinstance(i, int) else x_tok[:, bass.ds((i * U + u) * C, C), :]

            with nc.Block() as block:
                @block.sync
                def _(sp):
                    def load(i, u):
                        src = rows_dram[i * U + u:i * U + u + 1, 0:2 * D] if isinstance(i, int) else rows_dram[bass.ds(i * U + u, 1), 0:2 * D]
                        sp.dma_start(rows[u][:, :, :], src.rearrange("o (j d) -> (o j) d", d=D).partition_broadcast(P)).then_inc(s_rows[u], 16)
                    for u in range(U):
                        load(0, u)
                    with sp.Fori(1, NI) as i:
                        for u in range(U):
                            sp.wait_ge(s["beta"], value(sp, i, U, u + 1 - U))
                            sp.wait_ge(s["gamma"], value(sp, i, U, u + 1 - U))
                            load(i, u)
                    for u in range(U):
                        sp.wait_ge(s_rows[u], 16 * NI)

                @block.gpsimd
                def _(pool):
                    def body(i):
                        hold(pool, s["y_mv"], value(pool, i, 1, 1))
                        nc.gpsimd.tensor_scalar(rstd[:, :], mv[:, :, 1], EPS, None, ALU.add).then_inc(s["y_ve"], 1)
                        pool.wait_ge(s["y_ve"], value(pool, i, 1, 1))
                        nc.gpsimd.tensor_tensor(rstd[:, :], rstd[:, :], k("minus_half"), ALU.pow).then_inc(s["y_rs"], 1)
                        for u in range(U):
                            hold(pool, s_rows[u], value(pool, i, 16, 16))
                            nc.gpsimd.tensor_tensor(seq_of(i, u), seq_of(i, u), rows[u][:, 1:2, :].to_broadcast([P, C, D]), ALU.add).then_inc(s["beta"], 1)

                    def finish(i):
                        hold(pool, s["x_ve"], value(pool, i, 1, 1))
                        nc.gpsimd.tensor_tensor(tiles(rstd_x, i, NT), var_eps[:, :], k("minus_half"), ALU.pow).then_inc(s["x_rs"], 1)
                    body(0)
                    with pool.Fori(1, NI) as i:
                        body(i)
                        finish(i - 1)
                    finish(NI - 1)

                @block.scalar
                def _(act):
                    def body(i, first=False):
                        for u in range(U):
                            if not first:
                                act.wait_ge(s["added"], value(act, i, U, u + 1 - U))
                            hold(act, s["shift"], value(act, i, 1, 1))
                            for c in range(C):
                                t = u * C + c
                                last = nc.scalar.activation(nrm[u][:, c, :], xg[:, :, i * NT + t] if first else xg[:, :, bass.ds(i * NT + t, 1)].squeeze(2),
                                                            ACT.Identity, bias=shift[:, t:t + 1], scale=rstd[:, t:t + 1])
                            last.then_inc(s["normed"], 1)
                    body(0, first=True)
                    with act.Fori(1, NI) as i:
                        body(i)

                @block.vector
                def _(dve):
                    def stats_y(i):
                        for t in range(NT):
                            src = xg[:, :, i * NT + t] if isinstance(i, int) else xg[:, :, bass.ds(i * NT + t, 1)].squeeze(2)
                            last = nc.vector.bn_stats(st[:, 0, t, :], src)
                        last.then_inc(s["y_stats"], 1)
                        if not (isinstance(i, int) and i == 0):
                            dve.wait_ge(s["normed"], value(dve, i, U, 0))
                        hold(dve, s["y_stats"], value(dve, i, 1, 1))
                        for t in range(NT):
                            last = nc.vector.bn_aggr(mv[:, t, :], st[:, 0, t, :])
                        last.then_inc(s["y_mv"], 1)

                    def shift_y(i):
                        dve.wait_ge(s["y_rs"], value(dve, i, 1, 1))
                        nc.vector.scalar_tensor_tensor(shift[:, :], mv[:, :, 0], -1.0, rstd[:, :], ALU.mult, ALU.mult).then_inc(s["shift"], 1)

                    def join(i):
                        for u in range(U):
                            dve.wait_ge(s["normed"], value(dve, i, U, u + 1))
                            dve.wait_ge(s_rows[u], value(dve, i, 16, 16))
                            nc.vector.tensor_tensor(nrm[u][:, :, :], nrm[u][:, :, :], rows[u][:, 0:1, :].to_broadcast([P, C, D]), ALU.mult).then_inc(s["gamma"], 1)
                        for u in range(U):
                            dve.wait_ge(s["gamma"], value(dve, i, U, u + 1))
                            dve.wait_ge(s["beta"], value(dve, i, U, u + 1))
                            nc.vector.tensor_tensor(seq_of(i, u), seq_of(i, u), nrm[u][:, :, :], ALU.add).then_inc(s["added"], 1)

                    def stats_x(i, more=True):
                        for u in range(U):
                            hold(dve, s["added"], value(dve, i, U, u + 1))
                            for c in range(C):
                                last = nc.vector.bn_stats(st[:, 1, u * C + c, :], tile_of(x_tok, i, u * C + c))
                        last.then_inc(s["x_stats"], 1)
                        hold(dve, s["x_stats"], value(dve, i, 1, 1))
                        for t in range(NT):
                            last = nc.vector.bn_aggr(mv2[:, t, :], st[:, 1, t, :])
                        last.then_inc(s["x_mv"], 1)
                        dve.wait_ge(s["x_mv"], value(dve, i, 1, 1))
                        nc.vector.tensor_copy(tiles(mean_x, i, NT), mv2[:, :, 0])
                        if more:
                            dve.wait_ge(s["x_rs"], value(dve, i, 1, 0))
                        nc.vector.tensor_scalar(var_eps[:, :], mv2[:, :, 1], EPS, None, ALU.add).then_inc(s["x_ve"], 1)
                    stats_y(0)
                    shift_y(0)
                    stats_y(1)
                    join(0)
                    shift_y(1)
                    stats_x(0, more=False)
                    with dve.Fori(2, NI) as i:
                        stats_y(i)
                        join(i - 1)
                        shift_y(i)
                        stats_x(i - 1)
                    join(NI - 1)
                    stats_x(NI - 1)

        end_phase()

        with ExitStack() as sc:
            W = 2
            NW = B // W
            ew0 = sb("ew0", [P, E, D], scope=sc)
            eb0 = sb("eb0", [E, D], scope=sc)
            gw0 = sb("gw0", [P, E], scope=sc)
            gb0 = sb("gb0", [P, 1, E], scope=sc)
            pick = sb("pick", [E, E, P], BF16, scope=sc)
            nrm = [sb(f"nrm{w}", [P, C, D], scope=sc) for w in range(W)]
            f_t = [sb(f"f_t{w}", [P, C * P], scope=sc) for w in range(W)]
            hot_t = [sb(f"hot_t{w}", [E, C * P], scope=sc) for w in range(W)]
            hot_b = [sb(f"hot_b{w}", [E, C * P], BF16, scope=sc) for w in range(W)]
            moe_t = [sb(f"moe_t{w}", [P, C * P], scope=sc) for w in range(W)]
            masked = [sb(f"masked{m}", [P, C * P], scope=sc) for m in range(4)]
            logit = sb("logit", [P, C, E], scope=sc)
            top = sb("top", [P, C, 8], scope=sc)
            idx = sb("idx", [P, C, 8], U32, scope=sc)
            idf = sb("idf", [P, C, 1], scope=sc)
            hot = sb("hot", [P, C, E], scope=sc)
            st = sb("st", [P, C, 6], scope=sc)
            mv = sb("mv", [P, C, 2], scope=sc)
            var_eps = sb("var_eps", [P, C], scope=sc)
            SPREAD = (2, 3, 6, 7)
            names = ("weights", "pick", "normed", "turned", "feat", "lg_ps", "lg", "max", "idx", "idf", "hot", "hot_ps",
                     "hot_t", "hot_b", "spread", "masked", "product", "moe_t", "moe_ps", "added", "st", "mv", "ve", "rs")
            s = {nm: sem(f"moe_{nm}") for nm in names}

            class Seq:
                def __init__(self, eng, i):
                    self.eng, self.i, self.made = eng, i, {}

                def value(self, per, k):
                    if isinstance(self.i, int):
                        return self.i * per + k
                    if (per, k) not in self.made:
                        self.made[per, k] = self.eng.snap(self.i * per + k)
                    return self.made[per, k]

                def exists(self, w):
                    return not isinstance(self.i, int) or 0 <= self.i * W + w < B

                def done(self, name, w, alone=False):
                    if self.exists(w):
                        (hold if alone else wait)(self.eng, s[name], self.value(W, w + 1))

                def expert(self, name, w, e):
                    w, e = w + e // E, e % E
                    if self.exists(w):
                        self.eng.wait_ge(s[name], self.value(W * E, w * E + e + 1))

                def tiles(self, ap, w, first=0, many=C):
                    at = (self.i * W + w) * C + first
                    return ap[:, at:at + many] if isinstance(self.i, int) else ap[:, bass.ds(at, many)]

                def modulation(self, which, w):
                    b = self.i * W + w
                    return mod_t[:, which, b:b + 1] if isinstance(self.i, int) else mod_t[:, which, bass.ds(b, 1)]

            def sequences(eng, body, back=0):
                body(Seq(eng, 0), range(W))
                with eng.Fori(1, NW - 1) as i:
                    body(Seq(eng, i), range(W))
                body(Seq(eng, NW - 1), range(W))
                body(Seq(eng, NW), range(back))

            with nc.Block() as block:
                @block.sync
                def _(sp):
                    sp.dma_start(gw0[:, :], a["gw0"]).then_inc(s["weights"], 16)
                    sp.dma_start(gb0[:, 0, :], a["gb0"].partition_broadcast(P)).then_inc(s["weights"], 16)
                    sp.dma_start(eb0[:, :], a["eb0"]).then_inc(s["weights"], 16)
                    sp.dma_start(ew0[:, :, :], a["ew0"]).then_inc(s["weights"], 16)

                @block.gpsimd
                def _(pool):
                    def body(q, steps):
                        for w in steps:
                            if q.exists(w):
                                q.done("ve", w, alone=True)
                                nc.gpsimd.tensor_tensor(q.tiles(rstd_x, w), var_eps[:, :], k("minus_half")[:, 0:C], ALU.pow).then_inc(s["rs"], 1)
                    sequences(pool, body)

                @block.scalar
                def _(act):
                    def feat(q, w):
                        if q.exists(w):
                            q.done("turned", w, alone=True)
                            nc.scalar.activation(f_t[w % W][:, :], ps[:, 4, :], ACT.Identity, bias=q.modulation(SB0, w),
                                                 scale=q.modulation(CB0, w)).then_inc(s["feat"], 1)

                    def hot_half(q, w):
                        if q.exists(w):
                            q.done("hot_t", w)
                            nc.scalar.activation(hot_b[w % W][:, :], hot_t[w % W][:, :], ACT.Copy).then_inc(s["hot_b"], 1)

                    def body(q, steps):
                        for w in steps:
                            if isinstance(q.i, int) and q.i == 0 and w == 0:
                                feat(q, 0)
                                hot_half(q, 0)
                            if q.exists(w - 1):
                                hold(act, s["product"], q.value(W * E, (w - 1) * E + E))
                                nc.scalar.activation(moe_t[(w - 1) % W][:, :], ps[:, (w - 1) % W, :], ACT.Copy,
                                                     scale=q.modulation(GB0, w - 1)).then_inc(s["moe_t"], 1)
                            feat(q, w + 1)
                            hot_half(q, w + 1)
                    sequences(act, body, back=1)

                @block.vector
                def _(dve):
                    nc.vector.tensor_copy(pick[:, :, :], k("ident", E)[:, 0:E].unsqueeze(2).to_broadcast([E, E, P])).then_inc(s["pick"], 1)

                    def norm(q, w):
                        if q.exists(w):
                            q.done("turned", w - W)
                            for c in range(C):
                                last = nc.vector.tensor_scalar(nrm[w % W][:, c, :], q.tiles(x_tok, w, c, 1).squeeze(1), q.tiles(mean_x, w, c, 1),
                                                               q.tiles(rstd_x, w, c, 1), ALU.subtract, ALU.mult)
                            last.then_inc(s["normed"], 1)

                    def best(q, w):
                        if q.exists(w):
                            q.done("lg_ps", w)
                            nc.vector.tensor_tensor(logit[:, :, :], ps[:, 5, 0:C * E].rearrange("p (t e) -> p t e", e=E),
                                                    gb0[:, :, :].to_broadcast([P, C, E]), ALU.add).then_inc(s["lg"], 1)
                            q.done("lg", w, alone=True)
                            for t in range(C):
                                last = nc.vector.max(top[:, t, :], logit[:, t, :])
                            last.then_inc(s["max"], 1)
                            q.done("max", w, alone=True)
                            for t in range(C):
                                last = nc.vector.max_index(idx[:, t, :], top[:, t, :], logit[:, t, :])
                            last.then_inc(s["idx"], 1)
                            q.done("idx", w)
                            nc.vector.tensor_copy(idf[:, :, :], idx[:, :, 0:1]).then_inc(s["idf"], 1)
                            q.done("idf", w)
                            nc.vector.tensor_tensor(hot[:, :, :], k("iota").unsqueeze(1).to_broadcast([P, C, E]),
                                                    idf[:, :, :].to_broadcast([P, C, E]), ALU.is_equal).then_inc(s["hot"], 1)

                    def hot_rows(q, w):
                        if q.exists(w):
                            q.done("hot_ps", w)
                            nc.vector.tensor_copy(hot_t[w % W][:, :], ps[0:E, 5, :]).then_inc(s["hot_t"], 1)

                    def join(q, w):
                        if q.exists(w):
                            q.done("moe_ps", w)
                            nc.vector.tensor_tensor(q.tiles(x_tok, w), q.tiles(x_tok, w), ps[:, 4, :].rearrange("p (c d) -> p c d", c=C), ALU.add).then_inc(s["added"], 1)

                    def statistics(q, w):
                        if q.exists(w):
                            q.done("added", w, alone=True)
                            for c in range(C):
                                last = nc.vector.bn_stats(st[:, c, :], q.tiles(x_tok, w, c, 1).squeeze(1))
                            last.then_inc(s["st"], 1)
                            q.done("st", w, alone=True)
                            for c in range(C):
                                last = nc.vector.bn_aggr(mv[:, c, :], st[:, c, :])
                            last.then_inc(s["mv"], 1)
                            q.done("mv", w)
                            nc.vector.tensor_copy(q.tiles(mean_x, w), mv[:, :, 0])
                            nc.vector.tensor_scalar(var_eps[:, :], mv[:, :, 1], EPS, None, ALU.add).then_inc(s["ve"], 1)

                    def body(q, steps):
                        for w in steps:
                            if isinstance(q.i, int) and q.i == 0 and w == 0:
                                norm(q, 0)
                                dve.wait_ge(s["weights"], 4 * 16)
                                best(q, 0)
                                hot_rows(q, 0)
                                norm(q, 1)
                            for e in range(E):
                                if q.exists(w):
                                    q.expert("product", w, e - 4)
                                    q.expert("spread", w, e)
                                    nc.vector.tensor_tensor(masked[e % 4][:, :], f_t[w][:, :], ps[:, SPREAD[e % 4], :], ALU.mult).then_inc(s["masked"], 1)
                                if e == 3:
                                    statistics(q, w - 2)
                                if e == 5:
                                    best(q, w + 1)
                                if e == 6:
                                    join(q, w - 1)
                                if e == 7:
                                    q.done("rs", w - 2)
                                    norm(q, w + 2)
                            hot_rows(q, w + 1)
                    sequences(dve, body, back=2)

                @block.tensor
                def _(pe):
                    def turn(q, w):
                        if q.exists(w):
                            q.done("added", w - 3)
                            q.done("normed", w)
                            for c in range(C):
                                last = nc.tensor.transpose(ps[:, 4, c * P:(c + 1) * P], nrm[w % W][:, c, :], ident)
                            last.then_inc(s["turned"], 1)

                    def logits(q, w):
                        if q.exists(w):
                            q.done("hot_t", w - 1)
                            q.done("feat", w)
                            for c in range(C):
                                last = nc.tensor.matmul(ps[:, 5, c * E:(c + 1) * E], f_t[w % W][:, c * P:(c + 1) * P], gw0[:, :], start=True, stop=True)
                            last.then_inc(s["lg_ps"], 1)

                    def turn_hot(q, w):
                        if q.exists(w):
                            q.done("hot", w)
                            for c in range(C):
                                last = nc.tensor.transpose(ps[0:E, 5, c * P:(c + 1) * P], hot[:, c, :], ident)
                            last.then_inc(s["hot_ps"], 1)

                    def turn_back(q, w):
                        if q.exists(w):
                            q.done("feat", w + 2)
                            q.done("moe_t", w)
                            for c in range(C):
                                last = nc.tensor.transpose(ps[:, 4, c * P:(c + 1) * P], moe_t[w % W][:, c * P:(c + 1) * P], ident)
                            last.then_inc(s["moe_ps"], 1)

                    def spread(q, w, e):
                        w, e = w + e // E, e % E
                        if not q.exists(w):
                            return
                        if e == 0:
                            q.done("hot_b", w)
                        q.expert("masked", w, e - 4)
                        nc.tensor.matmul(ps[:, SPREAD[e % 4], :], pick[:, e, :], hot_b[w % W][:, :], start=True, stop=True).then_inc(s["spread"], 1)

                    def body(q, steps):
                        for w in steps:
                            if isinstance(q.i, int) and q.i == 0 and w == 0:
                                turn(q, 0)
                                pe.wait_ge(s["weights"], 4 * 16)
                                pe.wait_ge(s["pick"], 1)
                                logits(q, 0)
                                turn_hot(q, 0)
                                for e in range(4):
                                    spread(q, 0, e)
                            if q.exists(w):
                                q.done("moe_t", w - W)
                                nc.tensor.matmul(ps[:, w, :], eb0[:, :], hot_t[w][:, :], start=True, stop=False)
                            for e in range(E):
                                if q.exists(w):
                                    q.expert("masked", w, e)
                                    nc.tensor.matmul(ps[:, w, :], ew0[:, e, :], masked[e % 4][:, :], start=False, stop=(e == E - 1)).then_inc(
                                        s["product"], 1)
                                    if e < E - 4:
                                        spread(q, w, e + 4)
                                if e == 0:
                                    turn(q, w + 1)
                                if e == 2:
                                    logits(q, w + 1)
                                if e == 3:
                                    turn_back(q, w - 1)
                                if e == 5:
                                    turn_hot(q, w + 1)
                                if e == 7:
                                    for f in range(4):
                                        spread(q, w + 1, f)
                    sequences(pe, body, back=1)

        end_phase()

        QK = 2 * D
        VE = HD + 1
        PAY = D + 4
        CAP = B * C * P + P
        rows_of = nc.dram_tensor("rows_of", [E * CAP, PAY], F32).ap()
        room = xg[:, :, :].rearrange("p d t -> p (d t)") if D * TILES >= 2 * E * I2 else sb("room", [P, 2 * E * I2])
        w1, b1 = room[:, 0:E * I2], room[:, E * I2:2 * E * I2]
        V = 8
        GT = 4
        BT = -(-(2 * TILES + E - 1) // V) * V
        NP = BT // V
        I1 = I2 // 2
        parts = nc.dram_tensor("parts", [(2 * TILES + BT) * P, D], F32).ap()
        number = sb("number", [P, BT])
        cnt = sb("cnt", [P, E])
        cnti = sb("cnti", [P, E], I32)
        nti = sb("nti", [P, E], I32)
        ntile = sb("ntile", [P, E])
        upto = sb("upto_e", [P, E])
        first = sb("first", [P, E])
        step = sb("step", [P, E])
        last_tile = sb("last_tile", [P, 1])
        surplus = sb("surplus", [P, BT])
        beside = sb("beside", [P, BT])
        expert = sb("expert", [P, BT])
        row = sb("row", [P, BT])
        meta = sb("meta", [P, BT], I32)
        digits = sb("digits", [P, NP, V])
        packf = sb("packf", [P, NP])
        packs = sb("packs", [P, NP], I32)
        base = sb("base", [P, E])
        far = sb("far", [P, PAY])
        with ExitStack() as sc:
            wqkv = sb("wqkv", [P, 3 * D], scope=sc)
            wo = sb("wo", [P, D], scope=sc)
            gw = sb("gw", [P, 2, E], scope=sc)
            gb = sb("gb", [P, 2, E], scope=sc)
            bqkv = sb("bqkv", [P, 3 * D], scope=sc)
            scale_ms = sb("scale_ms", [P, D], scope=sc)
            rows = [sb(f"rows{u}", [P, 3, D], scope=sc) for u in range(U)]
            st = sb("st", [P, NT, 6], scope=sc)
            mv = sb("mv", [P, NT, 2], scope=sc)
            rstd = sb("rstd", [P, NT], scope=sc)
            nrm = [sb(f"nrm{u}", [P, C, D], scope=sc) for u in range(U)]
            f_t = [sb(f"f_t{u}", [P, C * P], scope=sc) for u in range(U)]
            qk = [sb(f"qk{u}", [P, C, QK], scope=sc) for u in range(U)]
            ex_room = [sb(f"ex{u}", [P, C * QK], scope=sc) for u in range(U)]
            lg_room = [sb(f"lg{u}", [P, C * QK], scope=sc) for u in range(U)]
            ex = [r[:, :].rearrange("p (c d) -> p c d", c=C) for r in ex_room]
            lg = [r[:, :].rearrange("p (c d) -> p c d", c=C) for r in lg_room]
            q_t = [r[:, 0:C * P] for r in ex_room]
            pay = [sb(f"pay{u}", [P, C, PAY], scope=sc) for u in range(U)]
            red = [r[:, 0:C * VE * H].rearrange("p (c e h) -> p c e h", c=C, e=VE) for r in lg_room]
            v1 = [sb(f"v1{u}", [P, C, VE, H], scope=sc) for u in range(U)]
            kv = [sb(f"kv{j}", [P, HD, D], scope=sc) for j in range(2)]
            qc = [sb(f"qc{j}", [P, VE * D], scope=sc) for j in range(2)]
            ds = [sb(f"ds{u}", [P, VE, H], scope=sc) for u in range(U)]
            skv = [sb(f"skv{u}", [P, VE, H], scope=sc) for u in range(U)]
            rden = sb("rden", [P, NT, H], scope=sc)
            masked = [sb(f"masked{u}", [P, C * P], scope=sc) for u in range(U)]
            logit = sb("logit", [P, NT, E], scope=sc)
            top = sb("top", [P, NT, 8], scope=sc)
            idx = sb("idx", [P, NT, 8], U32, scope=sc)
            idf = sb("idf", [P, 2, NT], scope=sc)
            hot = sb("hot", [P, 2, NT, E], scope=sc)
            both = sb("both", [P, NT, E], scope=sc)
            place = sb("place", [P, NT], scope=sc)
            wts = sb("wts", [P, 4, NT], scope=sc)
            tot = sb("tot", [P, E, NT], scope=sc)
            run = sb("run", [P, E, NT], scope=sc)
            rank = sb("rank", [P, NT, E], scope=sc)
            sel = sb("sel", [P, NT, E], scope=sc)
            pos = sb("pos", [P, 2, NT], scope=sc)
            posu = sb("posu", [P, 2, NT], U32, scope=sc)

            names = ("weights", "init", "sent", "st", "mv", "ve", "rs", "normed", "turned", "feat", "lg_ps", "lg", "max",
                     "idx", "idf", "hot", "qkv_ps", "qkv", "v", "abs", "exp", "ln", "relu", "u1", "cor", "cor_last", "qk",
                     "q_ps", "q_t", "kv", "tri", "qc", "red", "ds_ps", "ds", "skv", "so_ps", "state_in", "rden", "att",
                     "att_ps", "att_t", "wo", "wo_t", "wo_ps", "x3", "cb", "h4", "sq", "sm", "r4", "pay", "pay_ps", "pay_t",
                     "gx", "x4", "ed", "ee", "e1", "p1", "both", "rank_ps", "tot", "run", "excl", "r1", "r2", "sel", "pos",
                     "posu", "extra", "base", "scat", "place", "place2", "pads", "experts", "plan", "padrow")
            s = {nm: sem(f"p3_{nm}") for nm in names}
            s_rows = [sem(f"p3_rows{u}") for u in range(U)]
            counts = sb("counts", [P, E], I32, scope=sc)
            ge, gst = (q[:, 0:BT * E].rearrange("p (b e) -> p b e", e=E) for q in qc)
            sent = sb("sent", [P, 1], scope=sc)

            class At:
                def __init__(self, eng, i):
                    self.eng, self.i, self.made = eng, i, {}

                def __call__(self, per, k):
                    if isinstance(self.i, int):
                        return self.i * per + k
                    if (per, k) not in self.made:
                        self.made[per, k] = self.eng.snap(self.i * per + k)
                    return self.made[per, k]

            def col(ap, i, u):
                return ap[:, bass.ds(i * U + u, 1)]

            def tile(i, u, c):
                return x_tok[:, bass.ds((i * U + u) * C + c, 1), :].squeeze(1)

            def seq(i, u):
                if isinstance(i, int):
                    return x_tok[:, (i * U + u) * C:(i * U + u + 1) * C, :]
                return x_tok[:, bass.ds((i * U + u) * C, C), :]

            with nc.Block() as block:
                @block.sync
                def _(sp):
                    sp.dma_start(wqkv[:, :], a["Wqkv_t"]).then_inc(s["weights"], 16)
                    sp.dma_start(wo[:, :], a["Wo_t"]).then_inc(s["weights"], 16)
                    for l in range(2):
                        sp.dma_start(gw[:, l, :], a[f"gw{l}"]).then_inc(s["weights"], 16)
                        sp.dma_start(gb[:, l, :], a[f"gb{l}"].partition_broadcast(P)).then_inc(s["weights"], 16)
                    sp.dma_start(bqkv[:, :], a["bqkv"].partition_broadcast(P)).then_inc(s["weights"], 16)
                    sp.dma_start(scale_ms[:, :], a["ns"].partition_broadcast(P)).then_inc(s["weights"], 16)
                    def load(src, u):
                        sp.dma_start(rows[u][:, :, :], src.rearrange("o (j d) -> (o j) d", d=D).partition_broadcast(P)).then_inc(s_rows[u], 16)
                    for u in range(U):
                        load(rows_dram[u:u + 1, 2 * D:5 * D], u)
                    sp.dma_start(w1, a["w1"].rearrange("p e i -> p (e i)")).then_inc(s["experts"], 16)
                    sp.dma_start(b1, a["b1"].rearrange("e i -> (e i)").partition_broadcast(P)).then_inc(s["experts"], 16)
                    sp.dma_start(number[:, :], a["numbers"].partition_broadcast(P)).then_inc(s["experts"], 16)
                    with sp.Fori(1, NI) as i:
                        for u in range(U):
                            sp.wait_ge(s["gx"], sp.snap(i * U + (u + 1 - U)))
                            load(rows_dram[bass.ds(i * U + u, 1), 2 * D:5 * D], u)
                    for u in range(U):
                        sp.wait_ge(s_rows[u], 16 * NI)
                    sp.wait_ge(s["place"], 1)
                    for e in range(E):
                        row = sp.value_load(counts[0:1, e:e + 1], min_val=e * CAP, max_val=(e + 1) * CAP - P)
                        sp.dma_start(rows_of[bass.ds(row, P), :], far[:, :]).then_inc(s["pads"], 16)
                    sp.wait_ge(s["pads"], 16 * E)
                    sp.wait_ge(s["experts"], 3 * 16)

                @block.gpsimd
                def _(pool):
                    def scatter(first, last):
                        for n in range(first, last):
                            t, slot = n // 2, n % 2
                            nc.gpsimd.indirect_dma_start(
                                rows_of, bass.IndirectOffsetOnAxis(ap=posu[:, slot, t:t + 1], axis=0),
                                pay[t // C][:, t % C, :], None).then_inc(s["scat"], 16)

                    def body(i):
                        at = At(pool, i)
                        more = not isinstance(i, int)
                        EARLY = NT + 4
                        if more:
                            pool.wait_ge(s["posu"], at(1, 0))
                            hold(pool, s["extra"], at(1, 0))
                            scatter(0, EARLY)

                        def rsqrt(nth):
                            for half in range(2):
                                ts = slice(half * NT // 2, (half + 1) * NT // 2)
                                hold(pool, s["mv"], at(2, 2 * nth + half + 1))
                                nc.gpsimd.tensor_scalar(rstd[:, ts], mv[:, ts, 1], EPS, None, ALU.add).then_inc(s["ve"], 1)
                                pool.wait_ge(s["ve"], at(2, 2 * nth + half + 1))
                                nc.gpsimd.tensor_tensor(rstd[:, ts], rstd[:, ts], k("minus_half")[:, ts], ALU.pow).then_inc(s["rs"], 1)

                        def lost(u):
                            pool.wait_ge(s["u1"], at(U, u + 1))
                            nc.gpsimd.tensor_tensor(lg[u][:, :, :], ex[u][:, :, :], lg[u][:, :, :], ALU.subtract).then_inc(s["cor"], 1)
                        lost(0)
                        lost(1)
                        lost(2)
                        for c in range(C):
                            for u in range(U):
                                j = (c * U + u) % 2
                                t = c * U + u
                                if t >= 2:
                                    pool.wait_ge(s["tri"], at(NT, t - 1))
                                if c == 0:
                                    pool.wait_ge(s["qk"], at(U, u + 1))
                                k_in = qk[u][:, c, D:QK].rearrange("p (h d) -> p h d", h=H).unsqueeze(1).to_broadcast([P, HD, H, HD])
                                v_in = v1[u][:, c, 0:HD, :].unsqueeze(3).to_broadcast([P, HD, H, HD])
                                nc.gpsimd.tensor_tensor(kv[j][:, :, :].rearrange("p e (h d) -> p e h d", h=H), k_in, v_in, ALU.mult).then_inc(s["kv"], 1)
                                if more and EARLY + t < 2 * NT:
                                    scatter(EARLY + t, EARLY + t + 1)
                        if more:
                            hold(pool, s["scat"], at(16 * 2 * NT, 0))
                            nc.gpsimd.tensor_tensor(sent[:, :], k("ones")[:, 0:1], k("ones")[:, 0:1], ALU.mult).then_inc(s["sent"], 1)
                        rsqrt(0)
                        for half in range(2):
                            ts = slice(half * NT // 2, (half + 1) * NT // 2)
                            hold(pool, s["sq"], at(2, half + 1))
                            nc.gpsimd.tensor_scalar(rstd[:, ts], rstd[:, ts], 1.0 / D, EPS, ALU.mult, ALU.add).then_inc(s["sm"], 1)
                            pool.wait_ge(s["sm"], at(2, half + 1))
                            nc.gpsimd.tensor_tensor(rstd[:, ts], rstd[:, ts], k("minus_half")[:, ts], ALU.pow).then_inc(s["r4"], 1)
                        for u in range(U):
                            hold(pool, s["gx"], at(U, u + 1))
                            nc.gpsimd.tensor_tensor(seq(i, u), seq(i, u), masked[u][:, :].rearrange("p (c d) -> p c d", c=C), ALU.add).then_inc(s["x4"], 1)
                    body(0)
                    with pool.Fori(1, NI) as i:
                        body(i)
                    pool.wait_ge(s["posu"], NI)
                    pool.wait_ge(s["extra"], NI)
                    scatter(0, 2 * NT)
                    pool.wait_ge(s["scat"], 16 * 2 * NT * NI)

                @block.scalar
                def _(act):
                    with act.Fori(0, NI) as i:
                        at = At(act, i)

                        def feat(nth, bias, scale):
                            for u in range(U):
                                act.wait_ge(s["turned"], at(U, nth * U + u + 1))
                                nc.scalar.activation(f_t[u][:, :], ps[:, u, :], ACT.Identity, bias=col(mod_t[:, bias, :], i, u),
                                                     scale=col(mod_t[:, scale, :], i, u)).then_inc(s["feat"], 1)
                        feat(0, SA1, CA1)
                        for u in range(U):
                            act.wait_ge(s["qkv"], at(U, u + 1))
                            nc.scalar.activation(ex[u][:, :, :], qk[u][:, :, :], ACT.Abs).then_inc(s["abs"], 1)
                            act.wait_ge(s["abs"], at(U, u + 1))
                            nc.scalar.activation(ex[u][:, :, :], ex[u][:, :, :], ACT.Exp, scale=-1.0).then_inc(s["exp"], 1)
                        for u in range(U):
                            act.wait_ge(s["exp"], at(U, u + 1))
                            nc.scalar.activation(lg[u][:, :, :], ex[u][:, :, :], ACT.Ln, bias=1.0).then_inc(s["ln"], 1)
                        for u in range(U):
                            act.wait_ge(s["q_ps"], at(U, u + 1))
                            nc.scalar.activation(q_t[u][:, :], ps[:, u, :], ACT.Copy).then_inc(s["q_t"], 1)
                        for u in range(U):
                            act.wait_ge(s["att_ps"], at(U, u + 1))
                            nc.scalar.activation(f_t[u][:, :], ps[:, u, :], ACT.Copy).then_inc(s["att_t"], 1)
                        for u in range(U):
                            act.wait_ge(s["wo"], at(U, u + 1))
                            nc.scalar.activation(masked[u][:, :], ps[:, 4 + u, :], ACT.Identity, bias=col(mod_t[:, GA_BO, :], i, u),
                                                 scale=col(mod_t[:, GA1, :], i, u)).then_inc(s["wo_t"], 1)
                        for u in range(U):
                            act.wait_ge(s["h4"], at(U, u + 1))
                            for c in range(C):
                                last = nc.scalar.activation(masked[u][:, c * P:(c + 1) * P], nrm[u][:, c, :], ACT.Square,
                                                            accum_out=rstd[:, u * C + c:u * C + c + 1])
                            if u % 2:
                                last.then_inc(s["sq"], 1)
                        for u in range(U):
                            act.wait_ge(s["pay_ps"], at(U, u + 1))
                            nc.scalar.activation(f_t[u][:, :], ps[:, u, :], ACT.Copy).then_inc(s["pay_t"], 1)
                        act.wait_ge(s["ed"], at(1, 1))
                        nc.scalar.activation(wts[:, 1, :], wts[:, 0, :], ACT.Exp).then_inc(s["ee"], 1)

                @block.vector
                def _(dve):
                    dve.wait_ge(s["weights"], 8 * 16)
                    for u in range(U):
                        nc.vector.memset(v1[u][:, :, HD:VE, :], 1.0)
                    nc.vector.memset(far[:, :], 0.0).then_inc(s["padrow"], 1)
                    dve.wait_ge(s["padrow"], 1)
                    nc.vector.memset(far[:, D:D + 1], NOWHERE)
                    nc.vector.memset(far[:, D + 1:D + 2], -1.0).then_inc(s["padrow"], 1)
                    nc.vector.tensor_scalar(base[:, :], k("iota"), float(CAP), None, ALU.mult)
                    nc.vector.tensor_copy(place[:, :], k("token")).then_inc(s["init"], 1)
                    nc.vector.memset(ds[0][:, :, :], 0.0).then_inc(s["sent"], 1)
                    with dve.Fori(0, NI) as i:
                        at = At(dve, i)

                        def stats(nth, tiles, ready):
                            for half in range(2):
                                for u in range(half * U // 2, (half + 1) * U // 2):
                                    ready(u)
                                    for c in range(C):
                                        last = nc.vector.bn_stats(st[:, u * C + c, :], tiles(u, c))
                                last.then_inc(s["st"], 1)
                                hold(dve, s["st"], at(2, 2 * nth + half + 1))
                                for t in range(half * NT // 2, (half + 1) * NT // 2):
                                    last = nc.vector.bn_aggr(mv[:, t, :], st[:, t, :])
                                last.then_inc(s["mv"], 1)
                            for u in range(U):
                                if u % 2 == 0:
                                    dve.wait_ge(s["rs"], at(2, 2 * nth + u // 2 + 1))
                                for c in range(C):
                                    t = u * C + c
                                    last = nc.vector.tensor_scalar(nrm[u][:, c, :], tiles(u, c), mv[:, t, 0:1], rstd[:, t:t + 1],
                                                                   ALU.subtract, ALU.mult)
                                last.then_inc(s["normed"], 1)

                        for u in range(U):
                            for c in range(C):
                                tt = (i * U + u) * C + c
                                last = nc.vector.tensor_scalar(nrm[u][:, c, :], tile(i, u, c), mean_x[:, bass.ds(tt, 1)], rstd_x[:, bass.ds(tt, 1)],
                                                               ALU.subtract, ALU.mult)
                            last.then_inc(s["normed"], 1)

                        def best(nth, bias):
                            dve.wait_ge(s["lg_ps"], at(1, 1))
                            nc.vector.tensor_tensor(logit[:, :, :], ps[:, 4, 0:NT * E].rearrange("p (t e) -> p t e", e=E),
                                                    bias.to_broadcast([P, NT, E]), ALU.add).then_inc(s["lg"], 1)
                            hold(dve, s["lg"], at(1, 1))
                            for t in range(NT):
                                last = nc.vector.max(top[:, t, :], logit[:, t, :])
                            last.then_inc(s["max"], 1)
                            hold(dve, s["max"], at(1, 1))
                            for t in range(NT):
                                last = nc.vector.max_index(idx[:, t, :], top[:, t, :], logit[:, t, :])
                            last.then_inc(s["idx"], 1)
                            dve.wait_ge(s["idx"], at(1, 1))
                            nc.vector.tensor_copy(idf[:, :, :], idx[:, :, 0:2].rearrange("p t j -> p j t")).then_inc(s["idf"], 1)
                            dve.wait_ge(s["idf"], at(1, 1))
                            for j in range(1 + nth):
                                last = nc.vector.tensor_tensor(hot[:, j, :, :], k("iota").unsqueeze(1).to_broadcast([P, NT, E]),
                                                               idf[:, j, :].unsqueeze(2).to_broadcast([P, NT, E]), ALU.is_equal)
                            last.then_inc(s["hot"], 1)

                        for u in range(U):
                            dve.wait_ge(s["qkv_ps"], at(U, u + 1))
                            bank = 4 * (u % 2)
                            nc.vector.tensor_tensor(qk[u][:, :, :], ps[:, bank:bank + C, 0:QK],
                                                    bqkv[:, 0:QK].unsqueeze(1).to_broadcast([P, C, QK]), ALU.add).then_inc(s["qkv"], 1)
                            for c in range(C):
                                last = nc.vector.tensor_tensor(v1[u][:, c, 0:HD, :].rearrange("p e h -> p h e"),
                                                        ps[:, bank + c, QK:3 * D].rearrange("p (h e) -> p h e", h=H),
                                                        bqkv[:, QK:3 * D].rearrange("p (h e) -> p h e", h=H), ALU.add)
                            last.then_inc(s["v"], 1)
                        for u in range(U):
                            dve.wait_ge(s["ln"], at(U, u + 1))
                            nc.vector.scalar_tensor_tensor(qk[u][:, :, :], qk[u][:, :, :], 0.0, lg[u][:, :, :], ALU.max, ALU.add).then_inc(s["relu"], 1)
                            dve.wait_ge(s["relu"], at(U, u + 1))
                            nc.vector.tensor_scalar(lg[u][:, :, :], ex[u][:, :, :], 1.0, -1.0, ALU.add, ALU.add).then_inc(s["u1"], 1)
                        for u in range(U):
                            if u == 0:
                                dve.wait_ge(s["u1"], at(U, U))
                                nc.vector.tensor_tensor(lg[U - 1][:, :, :], ex[U - 1][:, :, :], lg[U - 1][:, :, :], ALU.subtract).then_inc(s["cor_last"], 1)
                            if u < U - 1:
                                dve.wait_ge(s["cor"], at(U - 1, u + 1))
                            else:
                                dve.wait_ge(s["cor_last"], at(1, 1))
                            nc.vector.tensor_tensor(qk[u][:, :, :], qk[u][:, :, :], lg[u][:, :, :], ALU.add).then_inc(s["qk"], 1)
                        for c in range(C):
                            for u in range(U):
                                t = c * U + u
                                j = t % 2
                                dve.wait_ge(s["tri"], at(NT, t + 1))
                                q_in = qk[u][:, c, 0:D].unsqueeze(1).to_broadcast([P, VE, D])
                                nc.vector.tensor_tensor(qc[j][:, :].rearrange("p (e d) -> p e d", d=D),
                                                        ps3(j)[:, 0:VE * D].rearrange("p (e d) -> p e d", d=D), q_in, ALU.mult).then_inc(s["qc"], 1)
                                dve.wait_ge(s["qc"], at(NT, t + 1))
                                nc.vector.tensor_reduce(red[u][:, c, :, :].rearrange("p e h -> p (e h)"),
                                                        qc[j][:, :].rearrange("p (g d) -> p g d", d=HD), AX.X, ALU.add).then_inc(s["red"], 1)
                                if c < C - 1:
                                    dve.wait_ge(s["ds_ps"], at((C - 1) * U, t + 1))
                                    mask = k("head_of").unsqueeze(1).to_broadcast([P, VE, H])
                                    dst = skv[u] if c == 0 else ds[u]
                                    nc.vector.tensor_tensor(dst[:, :, :], ps[:, 6, 0:VE * H].rearrange("p (e h) -> p e h", h=H), mask, ALU.mult).then_inc(s["ds"], 1)
                                if c:
                                    dve.wait_ge(s["so_ps"], at((C - 1) * U, t - U + 1))
                                    dve.wait_ge(s["red"], at(NT, t + 1))
                                    nc.vector.tensor_tensor(red[u][:, c, :, :].rearrange("p e h -> p (e h)"), red[u][:, c, :, :].rearrange("p e h -> p (e h)"),
                                                            ps[:, 7, 0:VE * H], ALU.add).then_inc(s["state_in"], 1)
                                if 0 < c < C - 1:
                                    dve.wait_ge(s["ds"], at((C - 1) * U, t + 1))
                                    nc.vector.tensor_tensor(skv[u][:, :, :], skv[u][:, :, :], ds[u][:, :, :], ALU.add).then_inc(s["skv"], 1)
                        for u in range(U):
                            dve.wait_ge(s["red"], at(NT, NT))
                            dve.wait_ge(s["state_in"], at((C - 1) * U, (C - 1) * U))
                            nc.vector.reciprocal(rden[:, u * C:(u + 1) * C, :], red[u][:, :, HD, :]).then_inc(s["rden"], 1)
                        for u in range(U):
                            dve.wait_ge(s["rden"], at(U, u + 1))
                            for c in range(C):
                                last = nc.vector.tensor_tensor(nrm[u][:, c, :].rearrange("p (h e) -> p h e", h=H),
                                                        red[u][:, c, 0:HD, :].rearrange("p e h -> p h e"),
                                                        rden[:, u * C + c, :].unsqueeze(2).to_broadcast([P, H, HD]), ALU.mult)
                            last.then_inc(s["att"], 1)
                        for u in range(U):
                            dve.wait_ge(s["wo_ps"], at(U, u + 1))
                            nc.vector.tensor_tensor(seq(i, u), seq(i, u), ps[:, u, :].rearrange("p (c d) -> p c d", c=C), ALU.add).then_inc(s["x3"], 1)
                        stats(0, lambda u, c: tile(i, u, c), lambda u: hold(dve, s["x3"], at(U, u + 1)))
                        for half in range(2):
                            us = range(half * U // 2, (half + 1) * U // 2)
                            for u in us:
                                dve.wait_ge(s_rows[u], at(16, 16))
                                dve.wait_ge(s["normed"], at(2 * U, U + u + 1))
                                nc.vector.tensor_tensor(nrm[u][:, :, :], nrm[u][:, :, :], rows[u][:, 0:1, :].to_broadcast([P, C, D]), ALU.mult).then_inc(s["cb"], 1)
                            for u in us:
                                dve.wait_ge(s["cb"], at(U, u + 1))
                                nc.vector.tensor_tensor(nrm[u][:, :, :], nrm[u][:, :, :], rows[u][:, 1:2, :].to_broadcast([P, C, D]), ALU.add).then_inc(s["h4"], 1)
                        dve.wait_ge(s["h4"], at(U, U))
                        dve.wait_ge(s["sent"], at(1, 1))
                        for u in range(U):
                            if u % 2 == 0:
                                dve.wait_ge(s["r4"], at(2, u // 2 + 1))
                            for c in range(C):
                                last = nc.vector.scalar_tensor_tensor(pay[u][:, c, 0:D], nrm[u][:, c, :], rstd[:, u * C + c:u * C + c + 1],
                                                                      scale_ms[:, :], ALU.mult, ALU.mult)
                            last.then_inc(s["pay"], 1)
                        for u in range(U):
                            nc.vector.tensor_tensor(masked[u][:, :].rearrange("p (c d) -> p c d", c=C), nrm[u][:, :, :],
                                                    rows[u][:, 2:3, :].to_broadcast([P, C, D]), ALU.mult).then_inc(s["gx"], 1)
                        best(1, gb[:, 1:2, :])
                        nc.vector.tensor_tensor(wts[:, 0, :], top[:, :, 1], top[:, :, 0], ALU.subtract).then_inc(s["ed"], 1)
                        dve.wait_ge(s["hot"], at(1, 1))
                        nc.vector.tensor_tensor(both[:, :, :], hot[:, 0, :, :], hot[:, 1, :, :], ALU.add).then_inc(s["both"], 1)
                        dve.wait_ge(s["ee"], at(1, 1))
                        nc.vector.tensor_scalar(wts[:, 2, :], wts[:, 1, :], 1.0, None, ALU.add).then_inc(s["e1"], 1)
                        dve.wait_ge(s["e1"], at(1, 1))
                        nc.vector.reciprocal(wts[:, 3, :], wts[:, 2, :]).then_inc(s["p1"], 1)
                        dve.wait_ge(s["rank_ps"], at(1, 1))
                        nc.vector.tensor_copy(tot[:, :, :], ps[:, 6, 0:NT * E].rearrange("p (t e) -> p e t", e=E)).then_inc(s["tot"], 1)
                        dve.wait_ge(s["p1"], at(1, 1))
                        for u in range(U):
                            ts = slice(u * C, (u + 1) * C)
                            nc.vector.tensor_copy(pay[u][:, :, D:D + 1], place[:, ts].unsqueeze(2))
                            nc.vector.tensor_copy(pay[u][:, :, D + 1:D + 2], idf[:, 1, ts].unsqueeze(2))
                            nc.vector.tensor_copy(pay[u][:, :, D + 2:D + 3], wts[:, 3, ts].unsqueeze(2))
                            last = nc.vector.scalar_tensor_tensor(pay[u][:, :, D + 3:D + 4], wts[:, 1, ts].unsqueeze(2), -1.0,
                                                                  wts[:, 3, ts].unsqueeze(2), ALU.add, ALU.mult)
                        last.then_inc(s["extra"], 1)
                        dve.wait_ge(s["tot"], at(1, 1))
                        nc.vector.tensor_tensor_scan(run[:, :, :].rearrange("p e t -> p (e t)"), k("restart"),
                                                     tot[:, :, :].rearrange("p e t -> p (e t)"), 0.0, ALU.mult, ALU.add).then_inc(s["run"], 1)
                        dve.wait_ge(s["run"], at(1, 1))
                        nc.vector.tensor_tensor(tot[:, :, :], run[:, :, :], tot[:, :, :], ALU.subtract).then_inc(s["excl"], 1)
                        dve.wait_ge(s["excl"], at(1, 1))
                        nc.vector.tensor_tensor(rank[:, :, :], ps[:, 5, 0:NT * E].rearrange("p (t e) -> p t e", e=E),
                                                tot[:, :, :].rearrange("p e t -> p t e"), ALU.add).then_inc(s["r1"], 1)
                        dve.wait_ge(s["r1"], at(1, 1))
                        nc.vector.tensor_tensor(rank[:, :, :], rank[:, :, :], base[:, :].unsqueeze(1).to_broadcast([P, NT, E]), ALU.add).then_inc(s["r2"], 1)
                        dve.wait_ge(s["r2"], at(1, 1))
                        nc.vector.tensor_tensor(base[:, :], base[:, :], run[:, :, NT - 1], ALU.add).then_inc(s["base"], 1)
                        for j in range(2):
                            nc.vector.tensor_tensor(sel[:, :, :], rank[:, :, :], hot[:, j, :, :], ALU.mult).then_inc(s["sel"], 1)
                            dve.wait_ge(s["sel"], at(2, j + 1))
                            nc.vector.tensor_reduce(pos[:, j, :], sel[:, :, :], AX.X, ALU.add).then_inc(s["pos"], 1)
                            dve.wait_ge(s["pos"], at(2, j + 1))
                        nc.vector.tensor_copy(posu[:, :, :], pos[:, :, :]).then_inc(s["posu"], 1)
                        nc.vector.tensor_scalar(place[:, :], place[:, :], float(NT * P), None, ALU.add).then_inc(s["place2"], 1)
                        dve.wait_ge(s["place2"], at(1, 1))
                        dve.wait_ge(s["base"], at(1, 1))
                        dve.wait_ge(s["x4"], at(U, U))
                        nc.vector.memset(ds[0][0:1, 0, 0:1], 0.0)
                    nc.vector.tensor_copy(counts[:, :], base[:, :]).then_inc(s["place"], 1)
                    c = [0]

                    def link(ins):
                        c[0] += 1
                        ins.then_inc(s["plan"], 1)
                        dve.wait_ge(s["plan"], c[0])
                    link(nc.vector.scalar_tensor_tensor(cnt[:, :], k("iota"), float(-CAP), base[:, :], ALU.mult, ALU.add))
                    link(nc.vector.tensor_scalar(cnt[:, :], cnt[:, :], float(P - 1), None, ALU.add))
                    link(nc.vector.tensor_copy(cnti[:, :], cnt[:, :]))
                    link(nc.vector.tensor_scalar(nti[:, :], cnti[:, :], 7, None, ALU.arith_shift_right))
                    link(nc.vector.tensor_copy(ntile[:, :], nti[:, :]))
                    link(nc.vector.tensor_tensor_scan(upto[:, :], k("ones")[:, 0:E], ntile[:, :], 0.0, ALU.mult, ALU.add))
                    nc.vector.tensor_scalar(last_tile[:, :], upto[:, E - 1:E], -1.0, None, ALU.add)
                    nc.vector.tensor_copy(step[:, 1:E], ntile[:, 0:E - 1])
                    nc.vector.memset(step[:, 0:1], 0.0)
                    link(nc.vector.tensor_tensor(first[:, :], upto[:, :], ntile[:, :], ALU.subtract))
                    dve.wait_ge(s["experts"], 3 * 16)
                    nc.vector.tensor_scalar(surplus[:, :], number[:, :], last_tile[:, :], NOWHERE, ALU.is_gt, ALU.mult)
                    link(nc.vector.tensor_scalar(beside[:, :], number[:, :], float(P), k("token")[:, 0:1], ALU.mult, ALU.add))
                    link(nc.vector.tensor_scalar(beside[:, :], beside[:, :], float(2 * TILES * P), None, ALU.add))
                    link(nc.vector.tensor_scalar(number[:, :], number[:, :], last_tile[:, :], None, ALU.min))
                    link(nc.vector.tensor_tensor(ge, number[:, :].unsqueeze(2).to_broadcast([P, BT, E]),
                                                 first[:, :].unsqueeze(1).to_broadcast([P, BT, E]), ALU.is_ge))
                    link(nc.vector.tensor_tensor(gst, ge, step[:, :].unsqueeze(1).to_broadcast([P, BT, E]), ALU.mult))
                    nc.vector.tensor_reduce(expert[:, :], ge, AX.X, ALU.add)
                    link(nc.vector.tensor_reduce(row[:, :], gst, AX.X, ALU.add))
                    link(nc.vector.tensor_scalar(expert[:, :], expert[:, :], -1.0, None, ALU.add))
                    link(nc.vector.tensor_tensor(row[:, :], number[:, :], row[:, :], ALU.subtract))
                    nc.vector.tensor_tensor(digits[:, :, :], expert[:, :].rearrange("p (i v) -> p i v", v=V),
                                            k("powers").unsqueeze(1).to_broadcast([P, NP, V]), ALU.mult)
                    link(nc.vector.tensor_scalar(row[:, :], row[:, :], float(P), None, ALU.mult))
                    link(nc.vector.scalar_tensor_tensor(row[:, :], expert[:, :], float(CAP), row[:, :], ALU.mult, ALU.add))
                    link(nc.vector.tensor_reduce(packf[:, :], digits[:, :, :], AX.X, ALU.add))
                    nc.vector.tensor_copy(packs[:, :], packf[:, :])
                    nc.vector.tensor_copy(meta[:, :], row[:, :]).then_inc(s["place"], 1)
                    dve.wait_ge(s["plan"], c[0])


                @block.tensor
                def _(pe):
                    pe.wait_ge(s["weights"], 8 * 16)
                    pe.wait_ge(s["init"], 1)
                    with pe.Fori(0, NI) as i:
                        at = At(pe, i)

                        def turn(src, u, bank):
                            for c in range(C):
                                last = nc.tensor.transpose(ps[:, bank, c * P:(c + 1) * P], src[u][:, c * P:(c + 1) * P], ident)
                            return last

                        def turn_tok(src, u, bank):
                            for c in range(C):
                                last = nc.tensor.transpose(ps[:, bank, c * P:(c + 1) * P], src[u][:, c, 0:D], ident)
                            return last

                        def logits(l):
                            for u in range(U):
                                pe.wait_ge(s["pay_t"], at(U, u + 1))
                                for c in range(C):
                                    t = u * C + c
                                    last = nc.tensor.matmul(ps[:, 4, t * E:(t + 1) * E], f_t[u][:, c * P:(c + 1) * P], gw[:, l, :],
                                                            start=True, stop=True)
                            last.then_inc(s["lg_ps"], 1)

                        for u in range(U):
                            pe.wait_ge(s["normed"], at(2 * U, u + 1))
                            turn_tok(nrm, u, u).then_inc(s["turned"], 1)
                        for u in range(U):
                            bank = 4 * (u % 2)
                            pe.wait_ge(s["feat"], at(U, u + 1))
                            if u == 0:
                                pe.wait_ge(s["feat"], at(U, U))
                            if u >= 2:
                                pe.wait_ge(s["v"], at(U, u - 1))
                            for c in range(C):
                                last = nc.tensor.matmul(ps[:, bank + c, 0:3 * D], f_t[u][:, c * P:(c + 1) * P], wqkv[:, :], start=True, stop=True)
                            last.then_inc(s["qkv_ps"], 1)
                        for u in range(U):
                            pe.wait_ge(s["qk"], at(U, u + 1))
                            turn_tok(qk, u, u).then_inc(s["q_ps"], 1)
                        pe.wait_ge(s["q_t"], at(U, U))
                        for c in range(C):
                            for u in range(U):
                                t = c * U + u
                                j = t % 2
                                if t >= 2:
                                    pe.wait_ge(s["qc"], at(NT, t - 1))
                                pe.wait_ge(s["kv"], at(NT, t + 1))
                                for m in range(2):
                                    nc.tensor.matmul(ps[:, 3 * j + m, :], k("upto"), kv[j][:, 4 * m:4 * m + 4, :].rearrange("p e d -> p (e d)"),
                                                     start=True, stop=True)
                                nc.tensor.matmul(ps[:, 3 * j + 2, 0:D], k("upto"), qk[u][:, c, D:QK], start=True, stop=True).then_inc(s["tri"], 1)
                                if c < C - 1:
                                    pe.wait_ge(s["v"], at(U, u + 1))
                                    if t:
                                        pe.wait_ge(s["ds"], at((C - 1) * U, t))
                                    nc.tensor.matmul(ps[:, 6, 0:VE * H], qk[u][:, c, D:QK], v1[u][:, c, :, :].rearrange("p e h -> p (e h)"),
                                                     start=True, stop=True).then_inc(s["ds_ps"], 1)
                                if c:
                                    if c == 1:
                                        pe.wait_ge(s["ds"], at((C - 1) * U, u + 1))
                                    else:
                                        pe.wait_ge(s["skv"], at((C - 2) * U, (c - 2) * U + u + 1))
                                    if t > U:
                                        pe.wait_ge(s["state_in"], at((C - 1) * U, t - U))
                                    nc.tensor.matmul(ps[:, 7, 0:VE * H], q_t[u][:, c * P:(c + 1) * P], skv[u][:, :, :].rearrange("p e h -> p (e h)"),
                                                     start=True, stop=True).then_inc(s["so_ps"], 1)
                        for u in range(U):
                            pe.wait_ge(s["att"], at(U, u + 1))
                            turn_tok(nrm, u, u).then_inc(s["att_ps"], 1)
                        for u in range(U):
                            pe.wait_ge(s["att_t"], at(U, u + 1))
                            nc.tensor.matmul(ps[:, 4 + u, :], wo[:, :], f_t[u][:, :], start=True, stop=True).then_inc(s["wo"], 1)
                        for u in range(U):
                            pe.wait_ge(s["wo_t"], at(U, u + 1))
                            turn(masked, u, u).then_inc(s["wo_ps"], 1)
                        for u in range(U):
                            pe.wait_ge(s["pay"], at(U, u + 1))
                            turn_tok(pay, u, u).then_inc(s["pay_ps"], 1)
                        logits(1)
                        pe.wait_ge(s["both"], at(1, 1))
                        nc.tensor.matmul(ps[:, 5, 0:NT * E], k("before"), both[:, :, :].rearrange("p t e -> p (t e)"), start=True, stop=True)
                        nc.tensor.matmul(ps[:, 6, 0:NT * E], k("ones"), both[:, :, :].rearrange("p t e -> p (t e)"), start=True, stop=True).then_inc(s["rank_ps"], 1)

        end_phase()

        with ExitStack() as sc:
            w2 = sb("w2", [P, E * 2 * D], scope=sc)
            b2 = sb("b2", [P, E * D], scope=sc)
            xt = sb("xt", [P, V, PAY], scope=sc)
            x_t = [sb(f"x_t{v}", [P, P], scope=sc) for v in range(V)]
            hid = [sb(f"hid{v}", [P, I2], scope=sc) for v in range(V)]
            glu = [h[:, 0:I1] for h in hid]
            lin = [h[:, I1:I2] for h in hid]
            act_t = [sb(f"act_t{v}", [P, I1], scope=sc) for v in range(V)]
            sg = [sb(f"sg{v}", [P, I1], scope=sc) for v in range(V)]
            yw = [sb(f"yw{v}", [P, D], scope=sc) for v in range(V)]
            own = sb("own", [P, 4, V], scope=sc)
            dest = sb("dest", [P, V], U32, scope=sc)
            names = ("weights", "x_ps", "x_t", "h_ps", "h", "glu", "lin", "sig", "gs", "a", "a_ps", "a_t", "y_ps", "yw",
                     "second", "own", "dest")
            s = {nm: sem(f"p4_{nm}") for nm in names}
            s_in = [sem(f"p4_rows{v}") for v in range(V)]
            s_out = [sem(f"p4_out{v}") for v in range(V)]

            class Tiles:
                def __init__(self, eng, i):
                    self.eng, self.i, self.made = eng, i, {}

                def value(self, per, k):
                    if isinstance(self.i, int):
                        return self.i * per + k
                    if (per, k) not in self.made:
                        self.made[per, k] = self.eng.snap(self.i * per + k)
                    return self.made[per, k]

                def exists(self, v):
                    return not isinstance(self.i, int) or 0 <= self.i * V + v < BT

                def done(self, name, v, alone=False):
                    if self.exists(v):
                        (hold if alone else wait)(self.eng, s[name], self.value(V, v + 1))

                def landed(self, sems, v, alone=False):
                    if self.exists(v):
                        (hold if alone else wait)(self.eng, sems[v % V], self.value(16, 16 * (v // V) + 16))

                def grouped(self, name, v, per=1, k=1):
                    if self.exists(v):
                        self.eng.wait_ge(s[name], self.value(per * V // GT, per * (v // GT) + k))

                def at(self, v, many=1):
                    return slice(self.i * V + v, self.i * V + v + many) if isinstance(self.i, int) else bass.ds(self.i * V + v, many)

                def row(self, v):
                    return self.eng.value_load(meta[0:1, self.at(v)], min_val=0, max_val=E * CAP - P)

                def experts(self, ahead=0):
                    i = self.i + ahead
                    at = slice(i, i + 1) if isinstance(i, int) else bass.ds(i, 1)
                    packed = self.eng.value_load(packs[0:1, at], min_val=0, max_val=E ** V - 1)
                    return [self.eng.snap((packed >> (3 * v)) & (E - 1), min_val=0, max_val=E - 1) for v in range(V)]

            def passes(eng, body, back=0):
                body(Tiles(eng, 0), range(V))
                with eng.Fori(1, NP - 1) as i:
                    body(Tiles(eng, i), range(V))
                body(Tiles(eng, NP - 1), range(V))
                body(Tiles(eng, NP), range(back))

            with nc.Block() as block:
                @block.sync
                def _(sp):

                    sp.dma_start(w2[:, :], a["w2"].rearrange("p e k d -> p (e k d)")).then_inc(s["weights"], 16)
                    sp.dma_start(b2[:, :], a["b2"].rearrange("e d -> (e d)").partition_broadcast(P)).then_inc(s["weights"], 16)

                    def body(t, steps):
                        for v in steps:
                            at = t.row(v)
                            t.done("x_ps", v - V)
                            t.grouped("dest", v - V)
                            sp.dma_start(xt[:, v, :], rows_of[bass.ds(at, P), :]).then_inc(s_in[v], 16)
                    passes(sp, body)
                    sp.wait_ge(s["weights"], 2 * 16)
                    for v in range(V):
                        sp.wait_ge(s_in[v], 16 * NP)

                @block.gpsimd
                def _(pool):
                    def body(t, steps):
                        for v in steps:
                            if t.exists(v):
                                t.done("sig", v)
                                nc.gpsimd.tensor_tensor(sg[v][:, :], sg[v][:, :], glu[v], ALU.mult).then_inc(s["gs"], 1)
                            if t.exists(v - 6):
                                u = (v - 6) % V
                                t.done("yw", v - 6, alone=True)
                                nc.gpsimd.indirect_dma_start(parts, bass.IndirectOffsetOnAxis(ap=dest[:, u:u + 1], axis=0),
                                                             yw[u][:, :], None).then_inc(s_out[u], 16)
                    passes(pool, body, back=6)
                    for v in range(V):
                        pool.wait_ge(s_out[v], 16 * NP)

                @block.scalar
                def _(act):
                    def turned(t, v):
                        if t.exists(v):
                            t.done("h_ps", v - V)
                            t.done("x_ps", v)
                            nc.scalar.activation(x_t[v % V][:, :], ps[:, 2 + v % 2, 0:P], ACT.Copy).then_inc(s["x_t"], 1)

                    def body(t, steps):
                        for v in steps:
                            if v == 0 and isinstance(t.i, int) and t.i == 0:
                                turned(t, 0)
                            turned(t, v + 1)
                            if t.exists(v):
                                t.done("a", v - V)
                                t.done("glu", v)
                                nc.scalar.activation(sg[v][:, :], glu[v], ACT.Sigmoid, scale=1.702).then_inc(s["sig"], 1)
                            if t.exists(v - 3):
                                t.done("a_ps", v - 3)
                                nc.scalar.activation(act_t[(v - 3) % V][:, :], ps[:, 4 + (v - 3) % 2, 0:I1], ACT.Copy).then_inc(s["a_t"], 1)
                            if t.exists(v - 5):
                                u = (v - 5) % V
                                t.grouped("dest", v - 5)
                                t.done("y_ps", v - 5)
                                nc.scalar.activation(yw[u][:, :], ps[:, 6 + u % 2, 0:D], ACT.Copy, scale=own[:, 2, u:u + 1]).then_inc(s["yw"], 1)
                    passes(act, body, back=5)

                @block.vector
                def _(dve):
                    def weights_and_places(t, v):
                        gs, tiles = slice(v, v + GT), t.at(v, GT)
                        for u in range(v, v + GT):
                            t.landed(s_in, u)
                            t.landed(s_out, u - V)
                        nc.vector.tensor_tensor(own[:, 0, gs], xt[:, gs, D + 1], expert[:, tiles], ALU.is_equal).then_inc(s["second"], 1)
                        t.grouped("second", v)
                        nc.vector.tensor_scalar(own[:, 1, gs], own[:, 0, gs], float(TILES * P), None, ALU.mult)
                        nc.vector.tensor_tensor(own[:, 3, gs], own[:, 0, gs], xt[:, gs, D + 3], ALU.mult).then_inc(s["own"], 1)
                        t.grouped("own", v, 4, 1)
                        nc.vector.tensor_tensor(own[:, 1, gs], own[:, 1, gs], xt[:, gs, D], ALU.add).then_inc(s["own"], 1)
                        t.done("yw", v + GT - 1 - V)
                        nc.vector.tensor_tensor(own[:, 2, gs], own[:, 3, gs], xt[:, gs, D + 2], ALU.add)
                        t.grouped("own", v, 4, 2)
                        nc.vector.tensor_tensor(own[:, 1, gs], own[:, 1, gs], surplus[:, tiles], ALU.max).then_inc(s["own"], 1)
                        t.grouped("own", v, 4, 3)
                        nc.vector.tensor_tensor(own[:, 1, gs], own[:, 1, gs], beside[:, tiles], ALU.min).then_inc(s["own"], 1)
                        t.grouped("own", v, 4, 4)
                        nc.vector.tensor_copy(dest[:, gs], own[:, 1, gs]).then_inc(s["dest"], 1)

                    def body(t, steps):
                        es = t.experts() if t.exists(0) else None
                        for v in steps:
                            if t.exists(v - 2):
                                u = (v - 2) % V
                                t.done("lin", v - 2)
                                t.done("gs", v - 2)
                                nc.vector.scalar_tensor_tensor(glu[u], lin[u], 1.0, sg[u][:, :], ALU.add, ALU.mult).then_inc(s["a"], 1)
                            if t.exists(v):
                                t.done("a_ps", v - V)
                                t.done("h_ps", v)
                                nc.vector.tensor_tensor(hid[v][:, :], ps[:, v % 2, :], b1[:, bass.ds(es[v] * I2, I2)], ALU.add).then_inc(s["h"], 1)
                                t.done("h", v)
                                nc.vector.tensor_scalar(glu[v], glu[v], 7.0, None, ALU.min).then_inc(s["glu"], 1)
                                nc.vector.tensor_scalar(lin[v], lin[v], 7.0, -7.0, ALU.min, ALU.max).then_inc(s["lin"], 1)
                            if t.exists(v) and v % GT == GT - 1:
                                weights_and_places(t, v + 1 - GT)
                    passes(dve, body, back=2)

                @block.tensor
                def _(pe):

                    def turn(t, v):
                        if t.exists(v):
                            t.done("x_t", v - 2)
                            t.landed(s_in, v)
                            nc.tensor.transpose(ps[:, 2 + v % 2, 0:P], xt[:, v % V, 0:D], ident).then_inc(s["x_ps"], 1)

                    def body(t, steps):
                        es = t.experts() if t.exists(0) else None
                        before = t.experts(-1) if t.exists(-1) else None
                        for v in steps:
                            if v == 0 and isinstance(t.i, int) and t.i == 0:
                                turn(t, 0)
                            turn(t, v + 1)
                            if t.exists(v):
                                t.done("x_t", v)
                                t.done("h", v - 2)
                                nc.tensor.matmul(ps[:, v % 2, :], x_t[v][:, :], w1[:, bass.ds(es[v] * I2, I2)], start=True, stop=True).then_inc(s["h_ps"], 1)
                            if t.exists(v - 3):
                                t.done("a_t", v - 5)
                                t.done("a", v - 3)
                                for j in range(2):
                                    last = nc.tensor.transpose(ps[:, 4 + (v - 3) % 2, j * P:(j + 1) * P], glu[(v - 3) % V][:, j * P:(j + 1) * P], ident)
                                last.then_inc(s["a_ps"], 1)
                            if t.exists(v - 5):
                                u = (v - 5) % V
                                e = es[v - 5] if v >= 5 else before[v + 3]
                                if isinstance(t.i, int) and t.i == 0 and v == 5:
                                    pe.wait_ge(s["weights"], 2 * 16)
                                t.done("yw", v - 7)
                                t.done("a_t", v - 5)
                                nc.tensor.matmul(ps[:, 6 + u % 2, 0:D], ident, b2[:, bass.ds(e * D, D)], start=True, stop=False)
                                for j in range(2):
                                    last = nc.tensor.matmul(ps[:, 6 + u % 2, 0:D], act_t[u][:, j * P:(j + 1) * P], w2[:, bass.ds(e * (2 * D) + j * D, D)],
                                                            start=False, stop=(j == 1))
                                last.then_inc(s["y_ps"], 1)
                    passes(pe, body, back=5)

        with ExitStack() as sc:
            part = [[sb(f"part{u}{j}", [P, C, D], scope=sc) for j in range(2)] for u in range(U)]
            gates = [sb(f"gates{u}", [P, D], scope=sc) for u in range(U)]
            s_part = [sem(f"p5_part{u}") for u in range(U)]
            s_sum = sem("p5_sum")
            s_scaled = sem("p5_scaled")
            s_total = sem("p5_total")
            s_out = [sem(f"p5_out{u}") for u in range(U)]
            parts_v = parts.rearrange("(t p) d -> p t d", p=P)
            with nc.Block() as block:
                @block.sync
                def _(sp):
                    with sp.Fori(0, NI) as i:
                        for u in range(U):
                            sp.wait_ge(s_total, sp.snap(i * U + u + 1))
                            for j in range(2):
                                sp.dma_start(part[u][j][:, :, :], parts_v[:, bass.ds((i * U + u) * C + j * TILES, C), :]).then_inc(s_part[u], 16)
                            src = rows_dram[bass.ds(i * U + u, 1), 4 * D:5 * D].squeeze(0)
                            sp.dma_start(gates[u][:, :], src.partition_broadcast(P)).then_inc(s_part[u], 16)
                    for u in range(U):
                        sp.wait_ge(s_part[u], 3 * 16 * NI)

                @block.scalar
                def _(act):
                    with act.Fori(0, NI) as i:
                        for u in range(U):
                            act.wait_ge(s_total, act.snap(i * U + U + u + 1))
                            act.dma_start(out[bass.ds(i * U + u, 1)].rearrange("o (c p) d -> p (o c) d", p=P), x_tok[:, bass.ds((i * U + u) * C, C), :]).then_inc(s_out[u], 16)
                    for u in range(U):
                        act.wait_ge(s_out[u], 16 * NI)

                @block.vector
                def _(dve):
                    nc.vector.memset(part[0][0][:, 0, 0:1], 0.0).then_inc(s_total, U)
                    with dve.Fori(0, NI) as i:
                        n = [dve.snap(i * U + u + 1) for u in range(U)]
                        landed = dve.snap((i + 1) * 48)
                        for u in range(U):
                            dve.wait_ge(s_part[u], landed)
                            nc.vector.tensor_tensor(part[u][0][:, :, :], part[u][0][:, :, :], part[u][1][:, :, :], ALU.add).then_inc(s_sum, 1)
                        for u in range(U):
                            dve.wait_ge(s_sum, n[u])
                            nc.vector.tensor_tensor(part[u][1][:, :, :], part[u][0][:, :, :], gates[u][:, :].unsqueeze(1).to_broadcast([P, C, D]),
                                                    ALU.mult).then_inc(s_scaled, 1)
                        for u in range(U):
                            dve.wait_ge(s_scaled, n[u])
                            xs = x_tok[:, bass.ds((i * U + u) * C, C), :]
                            nc.vector.tensor_tensor(xs, xs, part[u][1][:, :, :], ALU.add).then_inc(s_total, 1)


def constants():
    import numpy as np
    q = np.arange(P)
    parts = dict(
        ident=np.eye(P),
        upto=q[:, None] <= q[None],
        before=q[:, None] < q[None],
        ones=np.ones((P, P)),
        group_of=q[:, None] // N == np.arange(R)[None],
        head_of=q[:, None] // HD == np.arange(H)[None],
        iota=np.broadcast_to(np.arange(E), (P, E)),
        powers=np.broadcast_to(float(E) ** np.arange(E), (P, E)),
        token=q[:, None] + P * np.arange(16)[None],
        restart=np.broadcast_to(np.arange(128) % 16 > 0, (P, 128)),
        minus_half=np.full((P, 16), -0.5))
    return np.concatenate([parts[name] for name in CON], 1).astype(np.float32)


def layouts(i):
    import numpy as np

    def by_state(v):
        return v.reshape(G, R, N).transpose(1, 2, 0).reshape(P, G)

    mats = i["L0_attn_A"].reshape(G, R, N, N)
    w1, b1 = i["L1_ffn_mlp1_w"], i["L1_ffn_mlp1_b"]
    tiles = i["L0_attn_x"].shape[0] * C
    return dict(
        con=constants(),
        numbers=np.arange(-(-(2 * tiles + E - 1) // 8) * 8).astype(np.float32),
        x=i["L0_attn_x"],
        A=mats.transpose(1, 2, 0, 3), A_t=mats.transpose(1, 3, 0, 2),
        B_col=by_state(i["L0_attn_Bp"]), C_col=by_state(i["L0_attn_Cp"]), D_col=i["L0_attn_Dp"].reshape(G, R).T,
        Wg_t=i["L0_attn_Wg"].T, bg=i["L0_attn_bg"][:, None],
        gamma=i["L0_attn_gamma"], beta=i["L0_attn_beta"], bo=i["L1_attn_bo"][:, None],
        c_t=np.stack([i["L0_c"].T, i["L1_c"].T], 1), wmod=np.stack([i["L0_wmod"], i["L1_wmod"]], 1),
        gw0=i["L0_ffn_gate_w"], gb0=i["L0_ffn_gate_b"], ew0=i["L0_ffn_expert_w"].transpose(1, 0, 2), eb0=i["L0_ffn_expert_b"],
        Wqkv_t=np.concatenate([i["L1_attn_Wq"].T, i["L1_attn_Wk"].T, i["L1_attn_Wv"].T], 1),
        bqkv=np.concatenate([i["L1_attn_bq"], i["L1_attn_bk"], i["L1_attn_bv"]]), Wo_t=i["L1_attn_Wo"].T,
        ns=i["L1_ffn_norm_scale"], gw1=i["L1_ffn_gate_w"], gb1=i["L1_ffn_gate_b"],
        w1=np.concatenate([w1[:, :, 0::2], w1[:, :, 1::2]], 2).transpose(1, 0, 2),
        b1=np.concatenate([b1[:, 0::2], b1[:, 1::2]], 1),
        w2=i["L1_ffn_mlp2_w"].reshape(E, 2, P, D).transpose(2, 0, 1, 3), b2=i["L1_ffn_mlp2_b"])


def kernel(**inputs):
    import numpy as np
    import concourse.bacc as bacc
    from concourse.bass_utils import run_bass_kernel_spmd

    nc = bacc.Bacc("TRN2", target_bir_lowering=False, num_devices=1)
    arrays, args = {}, {}
    for name, v in layouts({n: np.asarray(v) for n, v in inputs.items()}).items():
        arrays[f"in_{name}_dram"] = np.ascontiguousarray(v)
        args[name] = nc.dram_tensor(f"in_{name}_dram", v.shape, mybir.dt.from_np(v.dtype), kind="ExternalInput").ap()
    shape = inputs["L0_attn_x"].shape
    out = nc.dram_tensor("out_0_dram", shape, F32, kind="ExternalOutput").ap()
    build(nc, args, out)
    r = run_bass_kernel_spmd(nc, [arrays], core_ids=[0])
    return r.results[0]["out_0_dram"]
```
